# Optimizing a Trainium2 kernel written in Bass

```python
import numpy as np
import jax
import jax.numpy as jnp

def _softmax(x, axis=-1):
    return jax.nn.softmax(x, axis=axis)

def _gelu(x):
    return jax.nn.gelu(x, approximate=True)

def _silu(x):
    return jax.nn.silu(x)

def _sigmoid(x):
    return jax.nn.sigmoid(x)

def _layernorm(x, axis=-1, eps=1e-05):
    m = jnp.mean(x, axis=axis, keepdims=True)
    v = jnp.var(x, axis=axis, keepdims=True)
    return (x - m) / jnp.sqrt(v + eps)

def _scatter_add(tgt, idx, src, axis=0):
    return tgt.at[idx].add(src)

def _segment_sum(src, seg, n):
    return jax.ops.segment_sum(src, seg, n)
kernel_name = 'mk_gnn_preln_d4_gnn_r8_dbc2ed'

def setup_inputs(seed: int=0):
    np.random.seed(seed)
    _w = jnp.asarray

    def _rec_inputs():
        import jax
        import jax.numpy as jnp
        _gk = jax.random.key(seed)
        x = -8.776e-05 + 1 * jax.random.normal(jax.random.fold_in(_gk, 1), (2500, 256), jnp.float32)
        _s = jax.random.randint(jax.random.fold_in(_gk, 2), (20000,), 0, 2500, jnp.int32)
        _d = jax.random.randint(jax.random.fold_in(_gk, 3), (20000,), 0, 2500, jnp.int32)
        _loop = jnp.arange(2500, dtype=jnp.int32)
        src = jnp.concatenate([_s, _d, _loop])
        dst = jnp.concatenate([_d, _s, _loop])
        _o = jnp.argsort(dst, stable=True)
        src = src[_o]
        dst = dst[_o]
        edge_attr_256 = -6.47781e-05 + 0.999943 * jax.random.normal(jax.random.fold_in(_gk, 11), (42500, 256), jnp.float32)
        edge_attr_64 = jax.random.uniform(jax.random.fold_in(_gk, 12), (42500, 64), jnp.float32, 0.0, 1)
        edge_type_8 = jax.random.randint(jax.random.fold_in(_gk, 14), (42500,), 0, 8, jnp.int32)
        return (x, src, dst, edge_attr_256, edge_attr_64, edge_type_8)
    x, src, dst, edge_attr_256, edge_attr_64, edge_type_8 = _rec_inputs()

    def _L0_gnn_setup():
        import jax, jax.numpy as jnp
        import numpy as np
        N_NODES = 2500
        N_EDGES = 40000
        D = 256
        R = 8

        def _xavier(key, shape):
            fan_in, fan_out = (shape[-2], shape[-1])
            bound = float(np.sqrt(6.0 / (fan_in + fan_out)))
            return jax.random.uniform(key, shape, jnp.float32, -bound, bound)

        def _rgcn_layer(x, W, self_w, b, src, dst, edge_type, num_nodes):
            xW = jnp.einsum('ni,rio->rno', x, W)
            msg = xW[edge_type, src]
            agg = jax.ops.segment_sum(msg, dst, num_segments=num_nodes)
            return agg + x @ self_w + b
        key = jax.random.key(seed)
        ks = jax.random.split(key, 10)
        x = jax.random.normal(ks[0], (N_NODES, D), jnp.float32)
        edge_index = jax.random.randint(ks[1], (2, N_EDGES), 0, N_NODES)
        edge_type = jax.random.randint(ks[2], (N_EDGES,), 0, R)
        W1 = _xavier(ks[3], (R, D, D))
        self_w1 = _xavier(ks[4], (D, D))
        b1 = jnp.zeros((D,), jnp.float32)
        W2 = _xavier(ks[5], (R, D, D))
        self_w2 = _xavier(ks[6], (D, D))
        b2 = jnp.zeros((D,), jnp.float32)
        return {'x': x, 'W1': W1, 'self_w1': self_w1, 'b1': b1, 'W2': W2, 'self_w2': self_w2, 'b2': b2, 'edge_index': edge_index, 'edge_type': edge_type}
    _L0_gnn_all = _L0_gnn_setup()
    _L0_gnn_in = {k: v for k, v in _L0_gnn_all.items() if k in ('W1', 'self_w1', 'b1', 'W2', 'self_w2', 'b2')}
    del _L0_gnn_all

    def _L1_gnn_setup():
        import jax, jax.numpy as jnp
        import numpy as np
        N = 12500
        E = 200000
        D_NODE = 256
        D_MSG = 128
        D_RAD = 64
        HEADS = 4
        OUTC = D_MSG // HEADS

        def _w(key, shape):
            fan_in = shape[-1]
            return jax.random.normal(key, shape, dtype=jnp.float32) / jnp.sqrt(jnp.float32(fan_in))
        key = jax.random.key(seed)
        ks = jax.random.split(key, 16)
        x = jax.random.normal(ks[0], (N, D_NODE), dtype=jnp.float32)
        edge_attr = jax.random.uniform(ks[1], (E, D_RAD), dtype=jnp.float32)
        edge_index = jax.random.randint(ks[2], (2, E), 0, N, dtype=jnp.int64)
        return {'x': x, 'edge_attr': edge_attr, 'edge_index': edge_index, 'W_edge': _w(ks[3], (D_RAD, D_RAD)), 'W_n2m': _w(ks[4], (D_MSG, D_NODE)), 'Wq': _w(ks[5], (D_MSG, D_MSG)), 'bq': jnp.zeros((D_MSG,), jnp.float32), 'Wk': _w(ks[6], (D_MSG, D_MSG)), 'bk': jnp.zeros((D_MSG,), jnp.float32), 'Wv': _w(ks[7], (D_MSG, D_MSG)), 'bv': jnp.zeros((D_MSG,), jnp.float32), 'We': _w(ks[8], (D_MSG, D_RAD)), 'Wskip': _w(ks[9], (D_MSG, D_MSG)), 'bskip': jnp.zeros((D_MSG,), jnp.float32), 'Wbeta': _w(ks[10], (1, 3 * D_MSG)), 'W_m2n': _w(ks[11], (D_NODE, D_MSG))}
    _L1_gnn_all = _L1_gnn_setup()
    _L1_gnn_in = {k: v for k, v in _L1_gnn_all.items() if k in ('W_edge', 'W_n2m', 'Wq', 'bq', 'Wk', 'bk', 'Wv', 'bv', 'We', 'Wskip', 'bskip', 'Wbeta', 'W_m2n')}
    del _L1_gnn_all

    def _L2_gnn_setup():
        import jax, jax.numpy as jnp
        import numpy as np
        N_NODES = 12500
        N_EDGES = 400000
        D_IN = 256
        D_HID = 256
        D_OUT = 256

        def _sage_conv(x, src, tgt, W_l, b_l, W_r):
            n = x.shape[0]
            msgs = x[src]
            agg = jax.ops.segment_sum(msgs, tgt, num_segments=n)
            deg = jax.ops.segment_sum(jnp.ones((src.shape[0],), x.dtype), tgt, num_segments=n)
            agg = agg / jnp.maximum(deg, 1.0)[:, None]
            return agg @ W_l + b_l + x @ W_r
        key = jax.random.key(seed)
        ks = jax.random.split(key, 8)
        x = jax.random.normal(ks[0], (N_NODES, D_IN), dtype=jnp.float32)
        edge_index = jax.random.randint(ks[1], (2, N_EDGES), 0, N_NODES, dtype=jnp.int64)
        s1 = 1.0 / np.sqrt(D_IN)
        s2 = 1.0 / np.sqrt(D_HID)
        return {'x': x, 'edge_index': edge_index, 'W_l1': jax.random.uniform(ks[2], (D_IN, D_HID), jnp.float32, -s1, s1), 'b1': jnp.zeros((D_HID,), jnp.float32), 'W_r1': jax.random.uniform(ks[3], (D_IN, D_HID), jnp.float32, -s1, s1), 'W_l2': jax.random.uniform(ks[4], (D_HID, D_OUT), jnp.float32, -s2, s2), 'b2': jnp.zeros((D_OUT,), jnp.float32), 'W_r2': jax.random.uniform(ks[5], (D_HID, D_OUT), jnp.float32, -s2, s2)}
    _L2_gnn_all = _L2_gnn_setup()
    _L2_gnn_in = {k: v for k, v in _L2_gnn_all.items() if k in ('W_l1', 'b1', 'W_r1', 'W_l2', 'b2', 'W_r2')}
    del _L2_gnn_all

    def _L3_gnn_setup():
        import jax, jax.numpy as jnp
        import numpy as np
        N_NODES = 6250
        N_EDGES = 100000
        DIM = 256
        LEAKY_SLOPE = 0.015

        def leaky_relu(x):
            return jnp.where(x > 0, x, LEAKY_SLOPE * x)
        key = jax.random.key(seed)
        k_v, k_e, k_idx, k_w1, k_w2 = jax.random.split(key, 5)
        v = jax.random.normal(k_v, (N_NODES, DIM), dtype=jnp.float32)
        e = jax.random.normal(k_e, (N_EDGES, DIM), dtype=jnp.float32)
        edge_index = jax.random.randint(k_idx, (2, N_EDGES), 0, N_NODES, dtype=jnp.int64)
        limit = float(np.sqrt(6.0 / (DIM + DIM)))
        W1 = jax.random.uniform(k_w1, (DIM, DIM), minval=-limit, maxval=limit, dtype=jnp.float32)
        b1 = jnp.zeros((DIM,), dtype=jnp.float32)
        W2 = jax.random.uniform(k_w2, (DIM, DIM), minval=-limit, maxval=limit, dtype=jnp.float32)
        b2 = jnp.zeros((DIM,), dtype=jnp.float32)
        return {'v': v, 'e': e, 'edge_index': edge_index, 'W1': W1, 'b1': b1, 'W2': W2, 'b2': b2}
    _L3_gnn_all = _L3_gnn_setup()
    _L3_gnn_in = {k: v for k, v in _L3_gnn_all.items() if k in ('W1', 'b1', 'W2', 'b2')}
    del _L3_gnn_all
    return {'x': x, 'src': src, 'dst': dst, 'edge_attr_256': edge_attr_256, 'edge_attr_64': edge_attr_64, 'edge_type_8': edge_type_8, 'L0_gnn_W1': _L0_gnn_in['W1'], 'L0_gnn_self_w1': _L0_gnn_in['self_w1'], 'L0_gnn_b1': _L0_gnn_in['b1'], 'L0_gnn_W2': _L0_gnn_in['W2'], 'L0_gnn_self_w2': _L0_gnn_in['self_w2'], 'L0_gnn_b2': _L0_gnn_in['b2'], 'L1_gnn_W_edge': _L1_gnn_in['W_edge'], 'L1_gnn_W_n2m': _L1_gnn_in['W_n2m'], 'L1_gnn_Wq': _L1_gnn_in['Wq'], 'L1_gnn_bq': _L1_gnn_in['bq'], 'L1_gnn_Wk': _L1_gnn_in['Wk'], 'L1_gnn_bk': _L1_gnn_in['bk'], 'L1_gnn_Wv': _L1_gnn_in['Wv'], 'L1_gnn_bv': _L1_gnn_in['bv'], 'L1_gnn_We': _L1_gnn_in['We'], 'L1_gnn_Wskip': _L1_gnn_in['Wskip'], 'L1_gnn_bskip': _L1_gnn_in['bskip'], 'L1_gnn_Wbeta': _L1_gnn_in['Wbeta'], 'L1_gnn_W_m2n': _L1_gnn_in['W_m2n'], 'L2_gnn_W_l1': _L2_gnn_in['W_l1'], 'L2_gnn_b1': _L2_gnn_in['b1'], 'L2_gnn_W_r1': _L2_gnn_in['W_r1'], 'L2_gnn_W_l2': _L2_gnn_in['W_l2'], 'L2_gnn_b2': _L2_gnn_in['b2'], 'L2_gnn_W_r2': _L2_gnn_in['W_r2'], 'L3_gnn_W1': _L3_gnn_in['W1'], 'L3_gnn_b1': _L3_gnn_in['b1'], 'L3_gnn_W2': _L3_gnn_in['W2'], 'L3_gnn_b2': _L3_gnn_in['b2']}

def reference(x, src, dst, edge_attr_256, edge_attr_64, edge_type_8, L0_gnn_W1, L0_gnn_self_w1, L0_gnn_b1, L0_gnn_W2, L0_gnn_self_w2, L0_gnn_b2, L1_gnn_W_edge, L1_gnn_W_n2m, L1_gnn_Wq, L1_gnn_bq, L1_gnn_Wk, L1_gnn_bk, L1_gnn_Wv, L1_gnn_bv, L1_gnn_We, L1_gnn_Wskip, L1_gnn_bskip, L1_gnn_Wbeta, L1_gnn_W_m2n, L2_gnn_W_l1, L2_gnn_b1, L2_gnn_W_r1, L2_gnn_W_l2, L2_gnn_b2, L2_gnn_W_r2, L3_gnn_W1, L3_gnn_b1, L3_gnn_W2, L3_gnn_b2):
    import jax
    import jax.numpy as jnp

    def _L0_gnn_ref(x, W1, self_w1, b1, W2, self_w2, b2, edge_index, edge_type):
        import jax, jax.numpy as jnp
        import numpy as np
        N_NODES = 2500
        N_EDGES = 40000
        D = 256
        R = 8

        def _xavier(key, shape):
            fan_in, fan_out = (shape[-2], shape[-1])
            bound = float(np.sqrt(6.0 / (fan_in + fan_out)))
            return jax.random.uniform(key, shape, jnp.float32, -bound, bound)

        def _rgcn_layer(x, W, self_w, b, src, dst, edge_type, num_nodes):
            xW = jnp.einsum('ni,rio->rno', x, W)
            msg = xW[edge_type, src]
            agg = jax.ops.segment_sum(msg, dst, num_segments=num_nodes)
            return agg + x @ self_w + b
        src, dst = (edge_index[0], edge_index[1])
        h = _rgcn_layer(x, W1, self_w1, b1, src, dst, edge_type, N_NODES)
        h = jax.nn.relu(h)
        out = _rgcn_layer(h, W2, self_w2, b2, src, dst, edge_type, N_NODES)
        return out

    def _L1_gnn_ref(x, edge_attr, edge_index, W_edge, W_n2m, Wq, bq, Wk, bk, Wv, bv, We, Wskip, bskip, Wbeta, W_m2n):
        import jax, jax.numpy as jnp
        import numpy as np
        N = 12500
        E = 200000
        D_NODE = 256
        D_MSG = 128
        D_RAD = 64
        HEADS = 4
        OUTC = D_MSG // HEADS

        def _w(key, shape):
            fan_in = shape[-1]
            return jax.random.normal(key, shape, dtype=jnp.float32) / jnp.sqrt(jnp.float32(fan_in))
        src = edge_index[0]
        dst = edge_index[1]
        n = x.shape[0]
        scale = 1.0 / jnp.sqrt(jnp.float32(OUTC))
        ee = edge_attr @ W_edge.T
        m = x @ W_n2m.T
        q = (m @ Wq.T + bq).reshape(n, HEADS, OUTC)
        k = (m @ Wk.T + bk).reshape(n, HEADS, OUTC)
        v = (m @ Wv.T + bv).reshape(n, HEADS, OUTC)
        e = (ee @ We.T).reshape(-1, HEADS, OUTC)
        kj = k[src] + e
        alpha = jnp.einsum('ehc,ehc->eh', q[dst], kj) * scale
        amax = jax.ops.segment_max(alpha, dst, num_segments=n)
        expa = jnp.exp(alpha - amax[dst])
        asum = jax.ops.segment_sum(expa, dst, num_segments=n)
        alpha = expa / (asum[dst] + 1e-16)
        msg = (v[src] + e) * alpha[..., None]
        out = jax.ops.segment_sum(msg, dst, num_segments=n)
        out = out.reshape(n, D_MSG)
        x_r = m @ Wskip.T + bskip
        beta = jax.nn.sigmoid(jnp.concatenate([out, x_r, out - x_r], axis=-1) @ Wbeta.T)
        out = beta * x_r + (1.0 - beta) * out
        return out @ W_m2n.T

    def _L2_gnn_ref(x, edge_index, W_l1, b1, W_r1, W_l2, b2, W_r2):
        import jax, jax.numpy as jnp
        import numpy as np
        N_NODES = 12500
        N_EDGES = 400000
        D_IN = 256
        D_HID = 256
        D_OUT = 256

        def _sage_conv(x, src, tgt, W_l, b_l, W_r):
            n = x.shape[0]
            msgs = x[src]
            agg = jax.ops.segment_sum(msgs, tgt, num_segments=n)
            deg = jax.ops.segment_sum(jnp.ones((src.shape[0],), x.dtype), tgt, num_segments=n)
            agg = agg / jnp.maximum(deg, 1.0)[:, None]
            return agg @ W_l + b_l + x @ W_r
        src, tgt = (edge_index[0], edge_index[1])
        h = jax.nn.relu(_sage_conv(x, src, tgt, W_l1, b1, W_r1))
        logits = _sage_conv(h, src, tgt, W_l2, b2, W_r2)
        return logits

    def _L3_gnn_ref(v, e, edge_index, W1, b1, W2, b2):
        import jax, jax.numpy as jnp
        import numpy as np
        N_NODES = 6250
        N_EDGES = 100000
        DIM = 256
        LEAKY_SLOPE = 0.015

        def leaky_relu(x):
            return jnp.where(x > 0, x, LEAKY_SLOPE * x)
        dst = edge_index[1]
        agg = jax.ops.segment_sum(e, dst, num_segments=v.shape[0])
        h = leaky_relu(agg @ W1.T + b1)
        h = h @ W2.T + b2
        return v + h
    edge_index = jnp.stack([src, dst])
    h = jnp.maximum(_layernorm(x, axis=-1), 0.0)
    x = x + _L0_gnn_ref(h, L0_gnn_W1, L0_gnn_self_w1, L0_gnn_b1, L0_gnn_W2, L0_gnn_self_w2, L0_gnn_b2, edge_index, edge_type_8)
    h = jnp.maximum(_layernorm(x, axis=-1), 0.0)
    x = x + _L1_gnn_ref(h, edge_attr_64, edge_index, L1_gnn_W_edge, L1_gnn_W_n2m, L1_gnn_Wq, L1_gnn_bq, L1_gnn_Wk, L1_gnn_bk, L1_gnn_Wv, L1_gnn_bv, L1_gnn_We, L1_gnn_Wskip, L1_gnn_bskip, L1_gnn_Wbeta, L1_gnn_W_m2n)
    h = jnp.maximum(_layernorm(x, axis=-1), 0.0)
    x = x + _L2_gnn_ref(h, edge_index, L2_gnn_W_l1, L2_gnn_b1, L2_gnn_W_r1, L2_gnn_W_l2, L2_gnn_b2, L2_gnn_W_r2)
    h = jnp.maximum(_layernorm(x, axis=-1), 0.0)
    x = x + _L3_gnn_ref(h, edge_attr_256, edge_index, L3_gnn_W1, L3_gnn_b1, L3_gnn_W2, L3_gnn_b2)
    return x

_drawn_inputs = setup_inputs


def setup_inputs(seed=0):
    import zlib

    import numpy as np

    out = dict(_drawn_inputs(seed))
    spreads = {'L0_gnn_b1': (0.0, 0.292),
     'L0_gnn_b2': (0.0, 0.8),
     'L1_gnn_bq': (0.0, 0.8),
     'L1_gnn_bk': (0.0, 2.0),
     'L1_gnn_bv': (0.0, 2.0),
     'L1_gnn_bskip': (0.0, 0.8),
     'L2_gnn_b1': (0.0, 0.8),
     'L2_gnn_b2': (0.0, 2.0),
     'L3_gnn_b1': (0.0, 2.0),
     'L3_gnn_b2': (0.0, 2.0)}
    factors = {'edge_attr_64': 8.0,
     'L1_gnn_W_edge': 5.487,
     'L1_gnn_Wq': 8.0,
     'L1_gnn_Wk': 8.0,
     'L1_gnn_Wv': 4.307,
     'L1_gnn_We': 5.37,
     'L1_gnn_Wbeta': 8.0,
     'L2_gnn_W_l1': 5.513,
     'L2_gnn_W_r1': 5.956,
     'L2_gnn_W_l2': 5.637,
     'L2_gnn_W_r2': 5.118}
    for name, (base, spread) in spreads.items():
        noise = np.random.default_rng([zlib.crc32(name.encode()), seed]).standard_normal(out[name].shape)
        drawn = base * np.exp(spread * noise) if base else spread * noise
        out[name] = jnp.asarray(drawn.astype(out[name].dtype))
    for name, factor in factors.items():
        out[name] = (out[name] * factor).astype(out[name].dtype)
    return out
```

```python
import concourse.bass as bass
from concourse import mybir
from contextlib import ExitStack

F32 = mybir.dt.float32
BF16 = mybir.dt.bfloat16
I32 = mybir.dt.int32
ALU = mybir.AluOpType
ACT = mybir.ActivationFunctionType
AX = mybir.AxisListType

P = 128
N = 2500
E = 42500
D = 256
REL = 8
DM = 128
DR = 64
HEADS = 4
HC = DM // HEADS
NB = -(-N // P)
LAST = N - (NB - 1) * P
NPAD = NB * P
COLS = -(-E // P)
TAIL = E - (P - 1) * COLS
RING = 16
GRP = 4
SLOTS = -(-(-(-(E + NB * (P - 1)) // P)) // RING) * RING
TURNS = SLOTS // RING
GROUPS = RING // GRP
SCOLS = -(-COLS // RING) * RING
NOWHERE = 255.0
OUTSIDE = 1 << 17
NEG = -1e30
HU = HC + 1
WA = D + 1
SM_SCALE = float(HC) ** -0.5
BIASES = ["l0_b1", "l0_b2", "l1_qs", "l1_kv", "l2_b1", "l2_b2", "l3_b1", "l3_b2"]
EPS = 1e-5
SLOPE = 0.015


class At:

    def __init__(self, i, step, k):
        self.i, self.step, self.k = i, step, k

    @property
    def n(self):
        return self.k if self.i is None else self.i * self.step + self.k

    def of(self, ring):
        return self.k % ring

    @property
    def turn(self):
        return self.k // self.step if self.i is None else self.i + self.k // self.step

    def plus(self, d):
        return At(self.i, self.step, self.k + d)


def dyn(at):
    return bass.ds(at.n, 1)


def pipeline(eng, count, step, stages):
    first, last = max(lead for lead, _ in stages), min(lead for lead, _ in stages)
    turns = (count - (first - last)) // step
    for tick in range(-first, -last):
        for lead, body in stages:
            if 0 <= tick + lead < count:
                body(At(None, step, tick + lead))
    with eng.Fori(0, turns) as i:
        for j in range(step):
            for lead, body in stages:
                body(At(i, step, j - last + lead))
    for tick in range(turns * step - last, count - last):
        for lead, body in stages:
            if 0 <= tick + lead < count:
                body(At(None, step, tick + lead))


class Chain:

    def __init__(self, eng, sem):
        self.eng, self.sem, self.count, self.loop = eng, sem, 0, None

    def after(self):
        if self.loop is None:
            self.eng.wait_ge(self.sem, self.count)
        else:
            i, per = self.loop
            self.eng.wait_ge(self.sem, i * per + self.count)

    def step(self, ins):
        ins.then_inc(self.sem, 1)
        self.count += 1

    def link(self, ins):
        self.step(ins)
        self.after()

    def run(self, times, per, body):
        start = self.count
        with self.eng.Fori(0, times) as i:
            self.loop = (i, per)
            body(i)
        assert self.count == start + per, (self.count - start, per)
        self.loop, self.count = None, start + per * times


def build(nc, a, out):
    top = ExitStack()

    def sb(name, shape, dt=F32, ctx=top):
        return ctx.enter_context(nc.sbuf_tensor(name, shape, dt))

    def sem(name):
        return top.enter_context(nc.semaphore(name))

    def dram(name, shape):
        return nc.dram_tensor(name, shape, F32, kind="Internal").ap()

    x = sb("x", [P, NB, D])
    h = sb("h", [P, NB, D])
    s = sb("s", [P, NB, D])
    acc = sb("acc", [P, NB, WA])
    esum = sb("esum", [P, NB, WA])
    ring = sb("ring", [P, RING, DR + D + 1])
    index = sb("index", [P, 3, SLOTS + RING])
    local = sb("local", [P, SLOTS])
    blocks = sb("blocks", [1, SLOTS], I32)
    keep = sb("keep", [P, SLOTS])
    forget = sb("forget", [P, SLOTS])
    now = sb("now", [P, 4, WA])
    cur = sb("cur", [P, RING], I32)
    onehot = sb("onehot", [P, RING, P])
    ident = sb("ident", [P, P])
    identb = sb("identb", [P, P], BF16)
    iota = sb("iota", [P, P])
    biases = sb("biases", [P, len(BIASES), D])
    small = sb("small", [P, 4, NB])
    ps = top.enter_context(nc.psum_tensor("ps", [P, 8, 512], F32))

    records = dram("records", (P * SLOTS, 4))
    table0 = dram("table0", (NPAD * REL, D))
    table1 = dram("table1", (NPAD * REL, D))
    kv_table = dram("kv_table", (NPAD, 2 * DM))
    h_table = dram("h_table", (NPAD, D))
    h1_table = dram("h1_table", (NPAD, D))
    e_store = dram("e_store", (SLOTS // GRP * P, GRP * DM))

    got = [sem(f"got{j}") for j in range(RING)]
    hot, summed, added, collected = sem("onehot_ready"), sem("slot_summed"), sem("sum_added"), sem("sum_collected")
    staged, gather_tick = sem("indices_staged"), sem("gather_tick")
    BANKS = 4
    slots_done = [0]

    def rows(table):
        return table.rearrange("(b p) f -> p b f", p=P)

    def bucket():
        with ExitStack() as ctx:
            dst = sb("dst", [P, SCOLS], I32, ctx)
            src = sb("src", [P, SCOLS], I32, ctx)
            typ = sb("typ", [P, SCOLS], I32, ctx)
            blk = sb("blk", [P, SCOLS], F32, ctx)
            loc = sb("loc", [P, SCOLS], F32, ctx)
            hit = sb("hit", [P, SCOLS], F32, ctx)
            run = sb("run", [P, SCOLS], F32, ctx)
            tmp = sb("tmp", [P, SCOLS], F32, ctx)
            pos = sb("pos", [P, SCOLS], F32, ctx)
            rec = sb("rec", [P, SCOLS, 4], F32, ctx)
            posi = sb("posi", [P, SCOLS], I32, ctx)
            sloti = sb("sloti", [P, SCOLS], I32, ctx)
            recring = sb("recring", [P, RING, 4], F32, ctx)
            empty = sb("empty", [P, SLOTS, 4], F32, ctx)
            iota_s = sb("iota_s", [P, SLOTS + RING], F32, ctx)
            bslot = sb("bslot", [P, SLOTS + RING], F32, ctx)
            every = sb("every", [P, SCOLS], F32, ctx)
            tri = sb("tri", [P, P], F32, ctx)
            ones = sb("ones", [P, P], F32, ctx)
            tot = sb("tot", [P, NB], F32, ctx)
            cnt = sb("cnt", [P, NB], I32, ctx)
            slots = sb("slots", [P, NB], F32, ctx)
            ends = sb("ends", [P, NB], F32, ctx)
            base = sb("base", [P, NB], F32, ctx)
            loaded, cleared, consts, iotas = sem("edges_loaded"), sem("edges_cleared"), sem("consts"), sem("iotas")
            chain_sem, totals_ready, prefix_ready = sem("bucket_chain"), sem("totals_ready"), sem("prefix_ready")
            empty_ready, empty_written = sem("empty_ready"), sem("empty_written")
            rec_ready, staged, scattered = sem("rec_ready"), sem("rec_staged"), [sem(f"scattered{j}") for j in range(RING)]
            tick, back, xcl, xl = sem("scatter_tick"), sem("records_back"), sem("x_cleared"), sem("x_loaded")
            with nc.Block() as block:

                @block.sync
                def _(sp):
                    sp.wait_ge(cleared, 3)
                    for t, source in ((dst, a["dst"]), (src, a["src"]), (typ, a["edge_type_8"])):
                        sp.dma_start(t[0:P - 1, 0:COLS], source[0:(P - 1) * COLS].rearrange("(p t) -> p t", t=COLS)).then_inc(loaded, 16)
                        sp.dma_start(t[P - 1:P, 0:TAIL], source[(P - 1) * COLS:E].rearrange("(p t) -> p t", p=1)).then_inc(loaded, 16)
                    sp.wait_ge(empty_ready, 3)
                    sp.dma_start(records.rearrange("(p s) c -> p (s c)", p=P), empty[:, :, :].rearrange("p s c -> p (s c)")).then_inc(empty_written, 16)
                    sp.wait_ge(xcl, 1)
                    sp.dma_start(x[:, 0:NB - 1, :], a["x"][0:(NB - 1) * P, :].rearrange("(b p) f -> p b f", p=P)).then_inc(xl, 16)
                    sp.dma_start(x[0:LAST, NB - 1, :], a["x"][(NB - 1) * P:N, :]).then_inc(xl, 16)
                    sp.dma_start(biases[:, :, :].rearrange("p k c -> p (k c)"), a["biases"].to_broadcast([P, len(BIASES) * D])).then_inc(xl, 16)
                    sp.wait_ge(xl, 48)
                    for j in range(RING):
                        sp.wait_ge(scattered[j], 16 * (SCOLS // RING))
                    sp.dma_start(empty[:, :, :].rearrange("p s c -> p (s c)"), records.rearrange("(p s) c -> p (s c)", p=P)).then_inc(back, 16)

                @block.gpsimd
                def _(pool):
                    pool.memset(dst[:, :], NPAD).then_inc(cleared, 1)
                    pool.memset(src[:, :], 0).then_inc(cleared, 1)
                    pool.memset(typ[:, :], 0).then_inc(cleared, 1)
                    pool.memset(x[:, NB - 1, :], 0.0).then_inc(xcl, 1)
                    pool.iota(iota[:, :], [[1, P]], 0, 0, allow_small_or_imprecise_dtypes=True).then_inc(iotas, 1)
                    pool.iota(iota_s[:, :], [[1, SLOTS + RING]], 0, 0, allow_small_or_imprecise_dtypes=True).then_inc(iotas, 1)
                    pool.iota(rec[:, :, 2], [[1, SCOLS]], 0, COLS, allow_small_or_imprecise_dtypes=True).then_inc(iotas, 1)
                    pool.memset(ones[:, :], 1.0).then_inc(consts, 1)
                    pool.memset(ident[:, :], 1.0).then_inc(consts, 1)
                    pool.memset(tri[:, :], 1.0).then_inc(consts, 1)
                    pool.memset(ring[:, :, DR + D:DR + D + 1], 1.0).then_inc(consts, 1)
                    pool.wait_ge(consts, 4)
                    pool.affine_select(out=ident[:, :], in_=ident[:, :], pattern=[[1, P]], compare_op=ALU.is_equal,
                                       fill=0.0, base=0, channel_multiplier=-1).then_inc(consts, 1)
                    pool.affine_select(out=tri[:, :], in_=tri[:, :], pattern=[[1, P]], compare_op=ALU.is_gt,
                                       fill=0.0, base=0, channel_multiplier=-1).then_inc(consts, 1)
                    pool.wait_ge(empty_written, 16)
                    with pool.Fori(0, SCOLS // RING) as i:
                        for g in range(GROUPS):
                            pool.wait_ge(staged, (i * (GROUPS) + g + 1) * 2)
                            pool.sem_inc(tick, 1)
                            for j in range(g * GRP, (g + 1) * GRP):
                                pool.indirect_dma_start(records, bass.IndirectOffsetOnAxis(ap=cur[:, j:j + 1], axis=0),
                                                        recring[:, j, :], None, bounds_check=P * SLOTS - 1,
                                                        oob_is_err=False).then_inc(scattered[j], 16)

                @block.scalar
                def _(act):
                    act.wait_ge(rec_ready, 1)

                    def stage(i, g):
                        at = At(i, RING, g * GRP)
                        js = slice(g * GRP, (g + 1) * GRP)
                        act.copy(cur[:, js], posi[:, bass.ds(at.n, GRP)]).then_inc(staged, 1)
                        act.copy(recring[:, js, :], rec[:, bass.ds(at.n, GRP), :]).then_inc(staged, 1)

                    for g in range(GROUPS):
                        stage(None, g)
                    with act.Fori(1, SCOLS // RING) as i:
                        for g in range(GROUPS):
                            for j in range(g * GRP, (g + 1) * GRP):
                                act.wait_ge(scattered[j], i * 16)
                            stage(i, g)

                @block.tensor
                def _(pe):
                    pe.wait_ge(consts, 6)
                    pe.wait_ge(totals_ready, 1)
                    pe.matmul(ps[:, 0, 0:NB], tri[:, :], tot[:, :], start=True, stop=True).then_inc(prefix_ready, 1)
                    pe.matmul(ps[:, 1, 0:NB], ones[:, :], tot[:, :], start=True, stop=True).then_inc(prefix_ready, 1)

                @block.vector
                def _(v):
                    c = Chain(v, chain_sem)
                    v.memset(empty[:, :, 0:3], 0.0).then_inc(empty_ready, 1)
                    v.memset(empty[:, :, 3:4], NOWHERE).then_inc(empty_ready, 1)
                    v.memset(index[:, :, SLOTS:], 0.0).then_inc(empty_ready, 1)
                    v.wait_ge(consts, 6)
                    c.step(v.tensor_copy(identb[:, :], ident[:, :]))
                    v.wait_ge(loaded, 96)
                    c.step(v.tensor_scalar(sloti[:, :], dst[:, :], 7, None, ALU.logical_shift_right))
                    c.step(v.tensor_scalar(posi[:, :], dst[:, :], P - 1, None, ALU.bitwise_and))
                    c.step(v.tensor_copy(rec[:, :, 1], src[:, :]))
                    c.step(v.tensor_copy(tmp[:, :], typ[:, :]))
                    c.step(v.memset(pos[:, :], 0.0))
                    c.link(v.memset(every[:, :], 1.0))
                    c.step(v.tensor_copy(blk[:, :], sloti[:, :]))
                    c.step(v.tensor_copy(rec[:, :, 3], posi[:, :]))
                    c.link(v.scalar_tensor_tensor(rec[:, :, 0], rec[:, :, 1], float(REL), tmp[:, :], ALU.mult, ALU.add))
                    v.wait_ge(iotas, 3)

                    def ranks(i):
                        col = bass.ds(i, 1)
                        c.link(v.tensor_scalar(hit[:, :], blk[:, :], iota[:, col], None, ALU.is_equal))
                        c.link(v.tensor_tensor_scan(run[:, :], every[:, :], hit[:, :], 0.0, ALU.mult, ALU.add))
                        c.step(v.tensor_copy(tot[:, col], run[:, SCOLS - 1:SCOLS]))
                        c.link(v.tensor_tensor(tmp[:, :], run[:, :], hit[:, :], ALU.mult))
                        c.link(v.tensor_tensor(pos[:, :], pos[:, :], tmp[:, :], ALU.add))

                    c.run(NB, 5, ranks)
                    v.tensor_copy(tmp[:, 0:1], tot[:, 0:1]).then_inc(totals_ready, 1)
                    v.wait_ge(prefix_ready, 2)
                    c.link(v.tensor_scalar(slots[:, :], ps[:, 1, 0:NB], float(P - 1), None, ALU.add))
                    c.link(v.tensor_copy(cnt[:, :], slots[:, :]))
                    c.link(v.tensor_scalar(cnt[:, :], cnt[:, :], 7, None, ALU.logical_shift_right))
                    c.link(v.tensor_copy(slots[:, :], cnt[:, :]))
                    c.link(v.tensor_tensor_scan(ends[:, :], every[:, 0:NB], slots[:, :], 0.0, ALU.mult, ALU.add))
                    c.link(v.tensor_tensor(base[:, :], ends[:, :], slots[:, :], ALU.subtract))
                    c.link(v.scalar_tensor_tensor(base[:, :], base[:, :], float(P), ps[:, 0, 0:NB], ALU.mult, ALU.add))
                    c.link(v.tensor_scalar(base[:, :], base[:, :], -1.0, None, ALU.add))
                    c.step(v.memset(bslot[:, :], 0.0))

                    def places(i):
                        col = bass.ds(i, 1)
                        c.step(v.tensor_scalar(hit[:, :], blk[:, :], iota[:, col], base[:, col], ALU.is_equal, ALU.mult))
                        c.link(v.tensor_scalar(empty[:, :, 0], iota_s[:, 0:SLOTS], ends[:, col], None, ALU.is_ge))
                        c.step(v.tensor_tensor(bslot[:, 0:SLOTS], bslot[:, 0:SLOTS], empty[:, :, 0], ALU.add))
                        c.link(v.tensor_tensor(pos[:, :], pos[:, :], hit[:, :], ALU.add))

                    v.wait_ge(empty_written, 16)
                    c.after()
                    c.run(NB, 4, places)
                    c.step(v.tensor_copy(posi[:, :], pos[:, :]))
                    c.link(v.tensor_scalar(bslot[:, :], bslot[:, :], float(NB - 1), None, ALU.min))
                    c.step(v.tensor_copy(blocks[:, :], bslot[0:1, 0:SLOTS]))
                    c.step(v.memset(keep[:, 0:1], 0.0))
                    c.link(v.tensor_tensor(keep[:, 1:SLOTS], bslot[:, 1:SLOTS], bslot[:, 0:SLOTS - 1], ALU.is_equal))
                    c.step(v.tensor_scalar(forget[:, :], keep[:, :], 1.0, -NEG, ALU.subtract, ALU.mult))
                    c.step(v.tensor_scalar(sloti[:, :], posi[:, :], 7, None, ALU.logical_shift_right))
                    c.link(v.tensor_scalar(posi[:, :], posi[:, :], P - 1, None, ALU.bitwise_and))
                    c.step(v.tensor_copy(tmp[:, :], sloti[:, :]))
                    c.step(v.tensor_copy(run[:, :], posi[:, :]))
                    c.link(v.tensor_scalar(hit[:, :], blk[:, :], float(NB), float(OUTSIDE), ALU.is_ge, ALU.mult))
                    c.link(v.scalar_tensor_tensor(run[:, :], run[:, :], float(SLOTS), tmp[:, :], ALU.mult, ALU.add))
                    c.link(v.tensor_tensor(run[:, :], run[:, :], hit[:, :], ALU.add))
                    c.link(v.tensor_copy(posi[:, :], run[:, :]))
                    v.tensor_copy(tmp[:, 0:1], pos[:, 0:1]).then_inc(rec_ready, 1)
                    v.wait_ge(back, 16)
                    c.step(v.tensor_copy(index[:, :, 0:SLOTS], empty[:, :, 0:3].rearrange("p s c -> p c s")))
                    c.link(v.tensor_copy(local[:, 0:SLOTS], empty[:, :, 3]))

    def layernorm(name):
        with ExitStack() as ctx:
            stats = sb(f"{name}_stats", [P, NB, 6], F32, ctx)
            mv = sb(f"{name}_mv", [P, NB, 2], F32, ctx)
            chain_sem, var_ready, std_ready, scale_ready = (sem(f"{name}_{n}") for n in ("chain", "var", "std", "scale"))
            with nc.Block() as block:

                @block.vector
                def _(v):
                    c = Chain(v, chain_sem)

                    def moments(i):
                        b = bass.ds(i, 1)
                        c.step(v.bn_stats(stats[:, b, :].rearrange("p o c -> p (o c)"), x[:, b, :].rearrange("p o c -> p (o c)")))

                    c.run(NB, 1, moments)
                    c.after()
                    for b in range(NB):
                        c.step(v.bn_aggr(mv[:, b, :], stats[:, b, :]))
                    c.after()
                    v.tensor_scalar(small[:, 0, :], mv[:, :, 1], EPS, None, ALU.add).then_inc(var_ready, 1)
                    v.wait_ge(std_ready, 1)
                    c.link(v.reciprocal(small[:, 2, :], small[:, 1, :]))
                    v.scalar_tensor_tensor(small[:, 3, :], mv[:, :, 0], -1.0, small[:, 2, :], ALU.mult, ALU.mult).then_inc(scale_ready, 1)

                @block.scalar
                def _(act):
                    act.wait_ge(var_ready, 1)
                    act.activation(small[:, 1, :], small[:, 0, :], ACT.Sqrt).then_inc(std_ready, 1)
                    act.wait_ge(scale_ready, 1)
                    with act.Fori(0, NB) as i:
                        b = bass.ds(i, 1)
                        act.activation(h[:, b, :].rearrange("p o c -> p (o c)"), x[:, b, :].rearrange("p o c -> p (o c)"), ACT.Relu,
                                       bias=small[:, 3, b], scale=small[:, 2, b])

    def gather_rows(pool, table, first_turn):
        with pool.Fori(0, SLOTS // RING) as i:
            for g in range(GROUPS):
                pool.wait_ge(staged, i * GROUPS + (first_turn // TURNS * (TURNS + 1) * GROUPS + g + 1))
                pool.sem_inc(gather_tick, 1)
                for j in range(g * GRP, (g + 1) * GRP):
                    pool.indirect_dma_start(ring[:, j, 0:table.shape[1]], None, table,
                                            bass.IndirectOffsetOnAxis(ap=cur[:, j:j + 1], axis=0)).then_inc(got[j], 16)

    def index_stager(act, column, used, base):
        for g in range(GROUPS):
            act.copy(cur[:, g * GRP:(g + 1) * GRP], index[:, column, g * GRP:(g + 1) * GRP]).then_inc(staged, 1)

        def stage(t):
            if t.k % GRP == GRP - 1:
                act.wait_ge(used, base + t.plus(1).n)
                g = t.of(RING) // GRP
                act.copy(cur[:, g * GRP:(g + 1) * GRP],
                         index[:, column, bass.ds(t.plus(RING - GRP + 1).n, GRP)]).then_inc(staged, 1)
        return stage

    def slot_block(eng, t):
        return bass.ds(eng.value_load(blocks[0:1, dyn(t)], min_val=0, max_val=NB - 1), 1)

    def onehot_maker(v, base):
        def make_onehot(t):
            v.tensor_scalar(onehot[:, t.of(RING), :], iota[:, :], local[:, dyn(t)], None, ALU.is_equal).then_inc(hot, 1)
        return make_onehot

    def slot_summer(pe, base, turn, first, width):
        def sum_slot(t):
            pe.wait_ge(got[t.of(RING)], (t.turn + turn) * 16 + 16)
            pe.wait_ge(hot, base + t.plus(1).n)
            pe.wait_ge(added, base + t.plus(1).n)
            pe.matmul(ps[:, t.of(BANKS), 0:width], onehot[:, t.of(RING), :],
                      ring[:, t.of(RING), first:first + width], start=True, stop=True).then_inc(summed, 1)
        return sum_slot

    def slot_adder(v, base, width):
        def add_slot(t):
            v.wait_ge(summed, base + t.plus(1).n)
            v.wait_ge(added, base + t.plus(BANKS).n)
            v.wait_ge(collected, base + t.plus(1).n)
            v.scalar_tensor_tensor(now[:, t.of(4), 0:width], now[:, (t.k - 1) % 4, 0:width], keep[:, dyn(t)],
                                   ps[:, t.of(BANKS), 0:width], ALU.mult, ALU.add).then_inc(added, 1)
        return add_slot

    def slot_collector(act, base, into, width):
        def collect(t):
            block = slot_block(act, t)
            act.wait_ge(added, base + t.plus(BANKS + 1).n)
            act.wait_ge(collected, base + t.plus(4).n)
            act.copy(into[:, block, 0:width], now[:, t.of(4):t.of(4) + 1, 0:width]).then_inc(collected, 1)
        return collect

    def clear_sums(v, base, into, width, cleared):
        if base == 0:
            v.sem_inc(added, BANKS)
            v.sem_inc(collected, 4)
        v.memset(now[:, 3, 0:width], 0.0).then_inc(cleared, 1)
        v.memset(into[:, :, 0:width], 0.0).then_inc(cleared, 1)
        v.wait_ge(cleared, 2)

    def gather_sum(name, table, column, load=None):
        turn, base = slots_done[0] // RING, slots_done[0]
        slots_done[0] += SLOTS
        cleared = sem(f"{name}_cleared")
        with nc.Block() as block:

            @block.gpsimd
            def _(pool):
                gather_rows(pool, table, turn)

            @block.scalar
            def _(act):
                stager = index_stager(act, column, summed, base)
                act.wait_ge(cleared, 2)
                pipeline(act, SLOTS, RING, [(0, stager), (-1, slot_collector(act, base, acc, D))])

            @block.tensor
            def _(pe):
                pipeline(pe, SLOTS, RING, [(0, slot_summer(pe, base, turn, 0, D))])

            @block.vector
            def _(v):
                clear_sums(v, base, acc, D, cleared)
                pipeline(v, SLOTS, RING, [(2, onehot_maker(v, base)), (0, slot_adder(v, base, D))])

            if load:

                @block.sync
                def _(sp):
                    load(sp)

    def edge_pass():
        turn, base = slots_done[0] // RING, slots_done[0]
        slots_done[0] += SLOTS
        cleared, loaded, turned, copied, projected, kept = (
            sem(f"edge_{n}") for n in ("cleared", "w_loaded", "turned", "turned_copied", "projected", "kept"))
        w_product, w_ready = sem("edge_w_product"), sem("edge_w_ready")
        stored = [sem(f"edge_stored{g}") for g in range(2)]
        with ExitStack() as ctx:
            w_edge = sb("w_edge", [DR, DR], F32, ctx)
            we_t = sb("we_t", [DR, DM], F32, ctx)
            w_e = sb("w_e", [DR, DM], F32, ctx)
            attr_t = sb("attr_t", [DR, 4, P], F32, ctx)
            e_out = sb("e_out", [P, 2, GRP * DM], F32, ctx)
            with nc.Block() as block:

                @block.sync
                def _(sp):
                    sp.dma_start(w_edge[:, :], a["w_edge"]).then_inc(loaded, 16)
                    sp.dma_start(we_t[:, :], a["we_t"]).then_inc(loaded, 16)
                    for g in range(2):
                        sp.sem_inc(stored[g], 16)
                    with sp.Fori(0, SLOTS // GRP // 2) as i:
                        for g in range(2):
                            t = At(i, 2, g)
                            sp.wait_ge(kept, i * (2 * GRP) + (g + 1) * GRP + 2)
                            sp.dma_start(e_store[bass.ds(i * (2 * P) + g * P, P), :], e_out[:, g, :]).then_inc(stored[g], 16)
                    for g in range(2):
                        sp.wait_ge(stored[g], 16 * (SLOTS // GRP // 2 + 1))

                @block.gpsimd
                def _(pool):
                    gather_rows(pool, a["edge_attrs"], turn)

                @block.tensor
                def _(pe):
                    pe.wait_ge(loaded, 32)
                    pe.matmul(ps[0:DR, 7, 0:DM], w_edge[:, :], we_t[:, :], start=True, stop=True).then_inc(w_product, 1)
                    pe.wait_ge(w_ready, 1)
                    pe.sem_inc(turned, 2)

                    def turn_attr(t):
                        pe.wait_ge(got[t.of(RING)], (t.turn + turn) * 16 + 16)
                        pe.wait_ge(copied, t.plus(1).n)
                        pe.transpose(ps[:, 4 + t.of(2), 0:P], ring[:, t.of(RING), 0:P], ident[:, :]).then_inc(turned, 1)

                    def project_attr(t):
                        pe.wait_ge(copied, t.plus(3).n)
                        pe.wait_ge(kept, t.plus(1).n)
                        pe.matmul(ps[:, 6 + t.of(2), 0:DM], attr_t[:, t.of(4), :], w_e[:, :],
                                  start=True, stop=True).then_inc(projected, 1)

                    pipeline(pe, SLOTS, RING, [(2, turn_attr), (0, project_attr),
                                               (0, slot_summer(pe, base, turn, DR, WA))])

                @block.scalar
                def _(act):
                    act.wait_ge(w_product, 1)
                    act.copy(w_e[:, :], ps[0:DR, 7, 0:DM]).then_inc(w_ready, 1)
                    act.sem_inc(copied, 2)
                    act.sem_inc(kept, 2)

                    def copy_turned(t):
                        act.wait_ge(turned, t.plus(3).n)
                        act.copy(attr_t[:, t.of(4), :], ps[0:DR, 4 + t.of(2), 0:P]).then_inc(copied, 1)

                    def keep_projected(t):
                        act.wait_ge(projected, t.plus(1).n)
                        g = t.k // GRP % 2
                        if t.k % GRP == 0:
                            act.wait_ge(stored[g], 16 * (t.k // (2 * GRP) + 1) if t.i is None
                                        else t.i * (16 * RING // (2 * GRP)) + 16 * (t.k // (2 * GRP) + 1))
                        act.copy(e_out[:, g, t.of(GRP) * DM:(t.of(GRP) + 1) * DM],
                                 ps[:, 6 + t.of(2), 0:DM]).then_inc(kept, 1)

                    stager = index_stager(act, 2, summed, base)
                    act.wait_ge(cleared, 2)
                    pipeline(act, SLOTS, RING, [(2, copy_turned), (0, stager), (0, keep_projected),
                                                (-1, slot_collector(act, base, esum, WA))])

                @block.vector
                def _(v):
                    clear_sums(v, base, esum, WA, cleared)
                    pipeline(v, SLOTS, RING, [(2, onehot_maker(v, base)), (0, slot_adder(v, base, WA))])

    def attention():
        turn, base = slots_done[0] // RING, slots_done[0]
        slots_done[0] += SLOTS
        (cleared, turned, ot_ready, pen_ready, qx_ready, kve_ready, prod_ready, alpha_ready, scored, mx_ready,
         mnew_ready, md_ready, r_ready, me_ready, ad_ready, p_ready, msg_ready, scaled) = (
            sem(f"att_{n}") for n in ("cleared", "turned", "ot", "pen", "qx", "kve", "prod", "alpha", "scored", "mx",
                                      "mnew", "md", "r", "me", "ad", "p", "msg", "scaled"))
        e_got = [sem(f"att_e{g}") for g in range(GROUPS)]
        with ExitStack() as ctx:
            e_in = sb("e_in", [P, GROUPS, GRP, DM], F32, ctx)
            onehot_t = sb("onehot_t", [P, 8, P], F32, ctx)
            penalty = sb("penalty", [P, 8, P], BF16, ctx)
            kve = sb("kve", [P, 8, 2, DM], F32, ctx)
            prod = sb("prod", [P, 2, DM], F32, ctx)
            alpha = sb("alpha", [P, 8, HEADS], F32, ctx)
            mx = sb("mx", [P, 4, HEADS], F32, ctx)
            mnew = sb("mnew", [P, 4, HEADS], F32, ctx)
            md = sb("md", [P, 4, HEADS], F32, ctx)
            r = sb("r", [P, 8, HEADS], F32, ctx)
            ad = sb("ad", [P, 4, HEADS], F32, ctx)
            msg = sb("msg", [P, 4, HEADS, HU], F32, ctx)
            WM = HEADS * HU

            def sums_at(t):
                return ps[:, 6 + t.of(2), 0:WM]

            with nc.Block() as block:

                @block.sync
                def _(sp):
                    for g in range(GROUPS):
                        sp.dma_start(e_in[:, g, :, :].rearrange("p s c -> p (s c)"), e_store[g * P:(g + 1) * P, :]).then_inc(e_got[g], 16)
                    with sp.Fori(1, SLOTS // RING) as i:
                        for g in range(GROUPS):
                            sp.wait_ge(kve_ready, (i - 1) * RING + (g + 1) * GRP)
                            sp.dma_start(e_in[:, g, :, :].rearrange("p s c -> p (s c)"),
                                         e_store[bass.ds(i * (P * GROUPS) + g * P, P), :]).then_inc(e_got[g], 16)

                @block.gpsimd
                def _(pool):
                    gather_rows(pool, kv_table, turn)

                @block.tensor
                def _(pe):
                    pe.wait_ge(cleared, 2)

                    def sum_messages(t):
                        pe.wait_ge(msg_ready, t.plus(1).n)
                        pe.wait_ge(added, base + t.plus(BANKS - 1).n)
                        pe.matmul(sums_at(t), onehot[:, t.of(RING), :], msg[:, t.of(4), :, :].rearrange("p h c -> p (h c)"),
                                  start=True, stop=True).then_inc(summed, 1)

                    def spread_maxima(t):
                        pe.wait_ge(mnew_ready, t.plus(2).n)
                        pe.wait_ge(ad_ready, t.plus(1).n)
                        pe.matmul(ps[:, 1, 0:HEADS], onehot_t[:, t.of(8), :], mnew[:, t.of(4), :], start=True, stop=True).then_inc(me_ready, 1)

                    def spread_scores(t):
                        pe.wait_ge(pen_ready, t.plus(2).n)
                        pe.wait_ge(mx_ready, t.plus(1).n)
                        bank = ps[:, 4 + t.of(2), :]
                        pe.matmul(bank, identb[:, :], penalty[:, t.of(8):t.of(8) + 1, :].to_broadcast([P, HEADS, P]),
                                  start=True, stop=False)
                        pe.wait_ge(alpha_ready, t.plus(1).n)
                        for head in range(HEADS):
                            ins = pe.matmul(bank[:, head * P:(head + 1) * P],
                                            alpha[:, t.of(8), head:head + 1].to_broadcast([P, P]), ident[:, :],
                                            start=False, stop=head == HEADS - 1)
                        ins.then_inc(scored, 1)

                    def spread_queries(t):
                        block_of = slot_block(pe, t)
                        pe.wait_ge(ot_ready, t.plus(1).n)
                        pe.wait_ge(prod_ready, t.plus(1).n)
                        pe.matmul(ps[:, 2 + t.of(2), 0:DM], onehot_t[:, t.of(8), :],
                                  s[:, block_of, 0:DM].rearrange("p o c -> p (o c)"), start=True, stop=True).then_inc(qx_ready, 1)

                    def turn_onehot(t):
                        pe.wait_ge(hot, base + t.plus(1).n)
                        pe.wait_ge(pen_ready, t.plus(1).n)
                        pe.transpose(ps[:, 0, 0:P], onehot[:, t.of(RING), :], ident[:, :]).then_inc(turned, 1)

                    pipeline(pe, SLOTS, RING, [(-6, sum_messages), (1, spread_scores),
                                               (3, spread_queries), (5, turn_onehot), (-2, spread_maxima)])

                @block.scalar
                def _(act):
                    act.sem_inc(pen_ready, 1)

                    def old_factor(t):
                        act.wait_ge(md_ready, t.plus(1).n)
                        act.activation(r[:, t.of(8), :], md[:, t.of(4), :], ACT.Exp, scale=SM_SCALE).then_inc(r_ready, 1)

                    def weights(t):
                        act.wait_ge(ad_ready, t.plus(2).n)
                        act.activation(msg[:, t.of(4), :, HC], ad[:, t.of(4), :], ACT.Exp, scale=SM_SCALE).then_inc(p_ready, 1)

                    def copy_turned(t):
                        act.wait_ge(turned, t.plus(1).n)
                        act.copy(onehot_t[:, t.of(8), :], ps[:, 0, 0:P]).then_inc(ot_ready, 1)
                        act.activation(penalty[:, t.of(8), :], ps[:, 0, 0:P], ACT.Copy, scale=-NEG, bias=NEG).then_inc(pen_ready, 1)

                    stager = index_stager(act, 1, kve_ready, 0)
                    act.wait_ge(cleared, 2)
                    pipeline(act, SLOTS, RING, [(4, copy_turned), (1, stager), (-8, slot_collector(act, base, acc, WM)),
                                                (-4, weights), (-1, old_factor)])

                @block.vector
                def _(v):
                    clear_sums(v, base, acc, WM, cleared)
                    v.memset(mnew[:, 3, :], NEG).then_inc(mnew_ready, 1)
                    v.sem_inc(prod_ready, 2)
                    v.sem_inc(mx_ready, 2)
                    v.sem_inc(ad_ready, 1)

                    def add_edge_part(t):
                        v.wait_ge(got[t.of(RING)], (t.turn + turn) * 16 + 16)
                        v.wait_ge(e_got[t.of(RING) // GRP], t.turn * 16 + 16)
                        e = e_in[:, t.of(RING) // GRP, t.of(GRP):t.of(GRP) + 1, :].to_broadcast([P, 2, DM])
                        v.tensor_tensor(kve[:, t.of(8), :, :], ring[:, t.of(RING), 0:2 * DM].rearrange("p (a c) -> p a c", a=2),
                                        e, ALU.add).then_inc(kve_ready, 1)

                    def rescale(t):
                        v.wait_ge(r_ready, t.plus(1).n)
                        v.wait_ge(added, base + t.plus(BANKS).n)
                        v.wait_ge(collected, base + t.plus(1).n)
                        v.tensor_tensor(now[:, t.of(4), 0:WM].rearrange("p (h c) -> p h c", h=HEADS),
                                        now[:, (t.k - 1) % 4, 0:WM].rearrange("p (h c) -> p h c", h=HEADS),
                                        r[:, t.of(8), :].unsqueeze(2).to_broadcast([P, HEADS, HU]), ALU.mult).then_inc(scaled, 1)

                    def multiply(t):
                        v.wait_ge(qx_ready, t.plus(1).n)
                        v.wait_ge(kve_ready, t.plus(1).n)
                        v.tensor_tensor(prod[:, t.of(2), :], kve[:, t.of(8), 0, :], ps[:, 2 + t.of(2), 0:DM], ALU.mult).then_inc(prod_ready, 1)

                    def weigh(t):
                        v.wait_ge(p_ready, t.plus(1).n)
                        m = msg[:, t.of(4), :, :]
                        v.tensor_tensor(m[:, :, 0:HC], kve[:, t.of(8), 1, :].rearrange("p (h c) -> p h c", h=HEADS),
                                        m[:, :, HC:HU].to_broadcast([P, HEADS, HC]), ALU.mult).then_inc(msg_ready, 1)

                    def score(t):
                        v.wait_ge(prod_ready, t.plus(3).n)
                        v.tensor_reduce(alpha[:, t.of(8), :], prod[:, t.of(2), :].rearrange("p (h c) -> p h c", h=HEADS),
                                        AX.X, ALU.add).then_inc(alpha_ready, 1)

                    def add(t):
                        new = now[:, t.of(4), 0:WM]
                        v.wait_ge(summed, base + t.plus(1).n)
                        v.wait_ge(scaled, t.plus(1).n)
                        v.tensor_tensor(new, new, sums_at(t), ALU.add).then_inc(added, 1)

                    def slot_max(t):
                        v.wait_ge(scored, t.plus(1).n)
                        v.tensor_reduce(mx[:, t.of(4), :], ps[:, 4 + t.of(2), :].rearrange("p (h e) -> p h e", h=HEADS),
                                        AX.X, ALU.max).then_inc(mx_ready, 1)

                    def subtract(t):
                        v.wait_ge(me_ready, t.plus(1).n)
                        v.tensor_tensor(ad[:, t.of(4), :], alpha[:, t.of(8), :], ps[:, 1, 0:HEADS], ALU.subtract).then_inc(ad_ready, 1)

                    def new_max(t):
                        v.wait_ge(mx_ready, t.plus(3).n)
                        v.wait_ge(mnew_ready, t.plus(1).n)
                        v.scalar_tensor_tensor(mnew[:, t.of(4), :], mnew[:, (t.k - 1) % 4, :], forget[:, dyn(t)],
                                               mx[:, t.of(4), :], ALU.add, ALU.max).then_inc(mnew_ready, 1)

                    def max_step(t):
                        v.wait_ge(mnew_ready, t.plus(2).n)
                        v.scalar_tensor_tensor(md[:, t.of(4), :], mnew[:, (t.k - 1) % 4, :], forget[:, dyn(t)],
                                               mnew[:, t.of(4), :], ALU.add, ALU.subtract).then_inc(md_ready, 1)

                    pipeline(v, SLOTS, RING, [(-3, subtract), (6, onehot_maker(v, base)), (2, add_edge_part), (-7, rescale), (2, multiply),
                                              (-5, weigh), (2, score), (-7, add), (0, slot_max), (0, new_max), (0, max_step)])

    tin_ready, turned_in, tin_turned = sem("tin_ready"), sem("tin_turned"), sem("turned_copied")
    multiplied = [sem(f"multiplied{k}") for k in range(6)]
    taken = [sem(f"taken{k}") for k in range(6)]
    stage_free = [sem(f"stage_free{j}") for j in range(2)]
    calls = {"tile": 0, "store": 0, **{k: 0 for k in range(6)}}

    def project(name, inputs, source, width, outs, weights=None, store=None):
        kt = sum(w for _, w in inputs) // P
        tiles, stores = calls["tile"], calls["store"]
        chunk_base = [calls[k] for k in range(len(outs))]
        calls["tile"] += NB
        for k in range(len(outs)):
            calls[k] += NB
        if store:
            calls["store"] += NB // 2
        loaded = sem(f"{name}_w_loaded")
        assert outs[-1][1] == "dve"

        def chunk_done(k, t):
            return chunk_base[k] + t.plus(1).n

        with ExitStack() as ctx:
            w = weights if weights is not None else sb(f"{name}_w", [P, kt, width], F32, ctx)
            tin = sb(f"{name}_tin", [P, 2, kt * P], F32, ctx)
            tt = sb(f"{name}_tt", [P, 2, kt * P], F32, ctx)
            with nc.Block() as block:

                @block.sync
                def _(sp):
                    if source is not None:
                        sp.dma_start(w[:, :, :], source.rearrange("(k p) n -> p k n", p=P)).then_inc(loaded, 16)
                    if store is not None:
                        if stores == 0:
                            for j in range(2):
                                sp.sem_inc(stage_free[j], 16)
                        with sp.Fori(0, NB // 2) as i:
                            for j in range(2):
                                t = At(i, 2, j)
                                for k, (_, _, _, staged_out) in enumerate(outs):
                                    if staged_out:
                                        sp.wait_ge(taken[k], chunk_base[k] + t.plus(2).n)
                                sp.dma_start(store[bass.ds(i * (2 * P) + j * P, P), :], stage[:, j, 0:store.shape[1]]).then_inc(stage_free[j], 16)
                        for j in range(2):
                            sp.wait_ge(stage_free[j], 16 * (stores + NB // 2 + 1))

                def evacuate(eng, mine):
                    def body(t):
                        for k, (cols, engine, write, staged_out) in enumerate(outs):
                            if engine == mine:
                                eng.wait_ge(multiplied[k], chunk_done(k, t))
                                if staged_out:
                                    eng.wait_ge(stage_free[t.of(2)], (t.turn + stores) * 16 + 16)
                                write(eng, t, ps[:, 2 + k, 0:cols]).then_inc(taken[k], 1)
                    return body

                @block.scalar
                def _(act):
                    if tiles == 0:
                        act.sem_inc(turned_in, 2)

                    def take_in(t):
                        act.wait_ge(turned_in, tiles + t.plus(1).n)
                        c = 0
                        for array, wide in inputs:
                            ins = act.copy(tin[:, t.of(2):t.of(2) + 1, c:c + wide], array[:, dyn(t), 0:wide])
                            c += wide
                        ins.then_inc(tin_ready, 1)

                    pipeline(act, NB, 2, [(1, take_in), (0, evacuate(act, "act"))])

                @block.tensor
                def _(pe):
                    if source is not None:
                        pe.wait_ge(loaded, 16)

                    def turn_in(t):
                        pe.wait_ge(tin_ready, tiles + t.plus(1).n)
                        pe.wait_ge(tin_turned, tiles + t.plus(1).n)
                        for k in range(kt):
                            ins = pe.transpose(ps[:, t.of(2), k * P:(k + 1) * P], tin[:, t.of(2), k * P:(k + 1) * P], ident[:, :])
                        ins.then_inc(turned_in, 1)

                    def multiply(t):
                        pe.wait_ge(tin_turned, tiles + t.plus(3).n)
                        c = 0
                        for n, (cols, _, _, _) in enumerate(outs):
                            pe.wait_ge(taken[n], chunk_base[n] + t.plus(1).n)
                            for k in range(kt):
                                ins = pe.matmul(ps[:, 2 + n, 0:cols], tt[:, t.of(2), k * P:(k + 1) * P], w[:, k, c:c + cols],
                                                start=k == 0, stop=k == kt - 1)
                            ins.then_inc(multiplied[n], 1)
                            c += cols

                    pipeline(pe, NB, 2, [(1, turn_in), (0, multiply)])

                @block.vector
                def _(v):
                    if tiles == 0:
                        v.sem_inc(tin_turned, 2)
                    for k in range(len(outs)):
                        if chunk_base[k] == 0:
                            v.sem_inc(taken[k], 1)

                    def copy_turned(t):
                        v.wait_ge(turned_in, tiles + t.plus(3).n)
                        v.tensor_copy(tt[:, t.of(2), :], ps[:, t.of(2), 0:kt * P]).then_inc(tin_turned, 1)

                    pipeline(v, NB, 2, [(1, copy_turned), (0, evacuate(v, "dve"))])

    def copy_to_stage(c0):
        def write(eng, t, psum):
            dest = stage[:, t.of(2), c0:c0 + psum.shape[1]]
            return eng.copy(dest, psum) if eng is nc.scalar else eng.tensor_copy(dest, psum)
        return write

    def add_to(dest, other, c0=0):
        def write(eng, t, psum):
            n = psum.shape[1]
            d = dest[:, dyn(t), c0:c0 + n].rearrange("p o c -> p (o c)")
            return eng.tensor_tensor(d, psum, d if other is None else other[:, 0:n], ALU.add)
        return write

    def add_to_stage(other):
        def write(eng, t, psum):
            return eng.tensor_tensor(stage[:, t.of(2), 0:psum.shape[1]], psum, other[:, 0:psum.shape[1]], ALU.add)
        return write

    def on_all(name, fn, store=None):
        chain_sem, done, written = sem(f"{name}_chain"), sem(f"{name}_done"), sem(f"{name}_written")
        with nc.Block() as block:

            @block.vector
            def _(v):
                fn(Chain(v, chain_sem), v)
                if store:
                    v.drain().then_inc(done, 1)

            if store:

                @block.sync
                def _(sp):
                    sp.wait_ge(done, 1)
                    sp.dma_start(rows(store[0]), store[1][:, :, 0:D]).then_inc(written, 16)
                    sp.wait_ge(written, 16)

    stage = ring[:, :, :].rearrange("p r c -> p (r c)")[:, 0:2 * REL * D].rearrange("p (j n) -> p j n", j=2)

    def store_rows(name, table, array):
        written = sem(f"{name}_written")
        with nc.Block() as block:

            @block.sync
            def _(sp):
                sp.dma_start(rows(table), array[:, :, 0:D]).then_inc(written, 16)
                sp.wait_ge(written, 16)

    def relational(layer, source, table, own_bias):
        outs = [(2 * D, "act" if k % 2 else "dve", copy_to_stage(2 * k * D), True) for k in range(REL // 2)]
        outs.append((D, "dve", add_to(s, own_bias), False))
        project(f"rel{layer}", [(h, D)], source, (REL + 1) * D, outs, store=table.rearrange("(n r) f -> n (r f)", r=REL))

    bias = {n: biases[:, k, :] for k, n in enumerate(BIASES)}

    bucket()
    edge_pass()
    layernorm("norm0")
    relational(0, a["l0_w1"], table0, bias["l0_b1"])
    gather_sum("rel0_sum", table0, 0)

    def hidden0(c, v):
        c.link(v.tensor_tensor(h[:, :, :], acc[:, :, 0:D], s[:, :, :], ALU.add))
        c.link(v.tensor_scalar(h[:, :, :], h[:, :, :], 0.0, None, ALU.max))
    on_all("hidden0", hidden0)
    relational(1, a["l0_w2"], table1, bias["l0_b2"])
    gather_sum("rel1_sum", table1, 0)

    def residual0(c, v):
        c.link(v.tensor_tensor(s[:, :, :], acc[:, :, 0:D], s[:, :, :], ALU.add))
        c.link(v.tensor_tensor(x[:, :, :], x[:, :, :], s[:, :, :], ALU.add))
    on_all("residual0", residual0)

    layernorm("norm1")
    with ExitStack() as att:
        w_att = sb("w_att", [P, 2, 4 * DM], F32, att)
        w_n2m = sb("w_n2m", [P, D], F32, att)
        w_cat = sb("w_cat", [P, 4 * DM], F32, att)
        loaded, product = sem("att_w_loaded"), sem("att_w_product")
        with nc.Block() as block:

            @block.sync
            def _(sp):
                sp.dma_start(w_n2m[:, :], a["w_n2m"]).then_inc(loaded, 16)
                sp.dma_start(w_cat[:, :], a["w_qskv_t"]).then_inc(loaded, 16)

            @block.tensor
            def _(pe):
                pe.wait_ge(loaded, 32)
                for k in range(2):
                    pe.matmul(ps[:, k, :], w_n2m[:, k * P:(k + 1) * P], w_cat[:, :], start=True, stop=True).then_inc(product, 1)

            @block.scalar
            def _(act):
                for k in range(2):
                    act.wait_ge(product, k + 1)
                    act.copy(w_att[:, k, :], ps[:, k, :])
        project("att_in", [(h, D)], None, 4 * DM,
                [(D, "dve", add_to(s, bias["l1_qs"]), False), (D, "dve", add_to_stage(bias["l1_kv"]), True)],
                weights=w_att, store=kv_table)
    attention()

    with ExitStack() as fin:
        wbeta = sb("wbeta", [P, 3 * DM], F32, fin)
        col = sb("col", [P, 4, NB], F32, fin)
        inv = sb("inv", [P, NB, HEADS], F32, fin)
        loaded, logit, sig = sem("beta_loaded"), sem("beta_logit"), sem("beta_sigmoid")
        chain_sem = sem("beta_chain")
        with nc.Block() as block:

            @block.sync
            def _(sp):
                sp.dma_start(wbeta[:, :], a["wbeta"].to_broadcast([P, 3 * DM])).then_inc(loaded, 16)

            @block.scalar
            def _(act):
                act.wait_ge(logit, 1)
                act.activation(col[:, 3, :], col[:, 2, :], ACT.Sigmoid).then_inc(sig, 1)

            @block.vector
            def _(v):
                c = Chain(v, chain_sem)
                o, diff, xr = h[:, :, 0:DM], h[:, :, DM:D], s[:, :, DM:D]

                def over_nodes(row):
                    return row.unsqueeze(1).to_broadcast([P, NB, DM])
                heads = acc[:, :, 0:HEADS * HU].rearrange("p b (h c) -> p b h c", h=HEADS)
                c.link(v.tensor_scalar(inv[:, :, :], heads[:, :, :, HC], 1e-16, None, ALU.add))
                c.link(v.reciprocal(inv[:, :, :], inv[:, :, :]))
                for head in range(HEADS):
                    c.step(v.tensor_tensor(h[:, :, head * HC:(head + 1) * HC], heads[:, :, head, 0:HC],
                                           inv[:, :, head:head + 1].to_broadcast([P, NB, HC]), ALU.mult))
                c.after()
                c.link(v.tensor_tensor(diff, o, xr, ALU.subtract))
                v.wait_ge(loaded, 16)
                c.step(v.tensor_tensor(acc[:, :, 0:DM], o, over_nodes(wbeta[:, 0:DM]), ALU.mult))
                c.link(v.tensor_tensor(acc[:, :, DM:D], xr, over_nodes(wbeta[:, DM:2 * DM]), ALU.mult))
                c.link(v.tensor_reduce(col[:, 0, :], acc[:, :, 0:D], AX.X, ALU.add))
                c.link(v.tensor_tensor(acc[:, :, 0:DM], diff, over_nodes(wbeta[:, 2 * DM:3 * DM]), ALU.mult))
                c.link(v.tensor_reduce(col[:, 1, :], acc[:, :, 0:DM], AX.X, ALU.add))
                v.tensor_tensor(col[:, 2, :], col[:, 0, :], col[:, 1, :], ALU.add).then_inc(logit, 1)
                v.wait_ge(sig, 1)
                c.link(v.tensor_tensor(diff, diff, col[:, 3, :].unsqueeze(2).to_broadcast([P, NB, DM]), ALU.mult))
                c.link(v.tensor_tensor(o, o, diff, ALU.subtract))
    project("att_out", [(h, DM)], a["w_m2n_t"], D, [(D, "dve", add_to(x, None), False)])

    layernorm("norm2")
    store_rows("h", h_table, h)
    gather_sum("mean0", h_table, 1)

    def mean(c, v):
        c.link(v.tensor_scalar(small[:, 0, :], esum[:, :, D], 1.0, None, ALU.max))
        c.link(v.reciprocal(small[:, 1, :], small[:, 0, :]))
        c.link(v.tensor_tensor(acc[:, :, 0:D], acc[:, :, 0:D], small[:, 1, :].unsqueeze(2).to_broadcast([P, NB, D]), ALU.mult))
    on_all("mean0", mean)
    project("sage0", [(acc, D), (h, D)], a["l2_w1"], D, [(D, "dve", add_to(s, bias["l2_b1"]), False)])

    def relu_s(c, v):
        c.link(v.tensor_scalar(s[:, :, :], s[:, :, :], 0.0, None, ALU.max))
    on_all("sage_relu", relu_s, store=(h1_table, s))
    gather_sum("mean1", h1_table, 1)

    def mean1(c, v):
        mean(c, v)
        c.link(v.tensor_tensor(x[:, :, :], x[:, :, :], bias["l2_b2"].unsqueeze(1).to_broadcast([P, NB, D]), ALU.add))
    on_all("mean1", mean1)
    project("sage1", [(acc, D), (s, D)], a["l2_w2"], D, [(D, "dve", add_to(x, None), False)])

    layernorm("norm3")
    project("edge0", [(esum, D)], a["l3_w1_t"], D, [(D, "dve", add_to(s, bias["l3_b1"]), False)])

    def leaky(c, v):
        c.link(v.scalar_tensor_tensor(s[:, :, :], s[:, :, :], SLOPE, s[:, :, :], ALU.mult, ALU.max))
        c.link(v.tensor_tensor(x[:, :, :], x[:, :, :], h[:, :, :], ALU.add))
        c.link(v.tensor_tensor(x[:, :, :], x[:, :, :], bias["l3_b2"].unsqueeze(1).to_broadcast([P, NB, D]), ALU.add))
    on_all("leaky", leaky)
    project("edge1", [(s, D)], a["l3_w2_t"], D, [(D, "dve", add_to(x, None), False)])

    written = sem("written")
    with nc.Block() as block:

        @block.sync
        def _(sp):
            sp.dma_start(out[0:(NB - 1) * P, :].rearrange("(b p) f -> p b f", p=P), x[:, 0:NB - 1, :]).then_inc(written, 16)
            sp.dma_start(out[(NB - 1) * P:N, :], x[0:LAST, NB - 1, :]).then_inc(written, 16)
            sp.wait_ge(written, 32)
    top.close()


INPUTS = ["x", "src", "dst", "edge_type_8"]


def kernel(**inputs):
    import numpy as np
    from concourse import bacc
    from concourse.bass_utils import run_bass_kernel_spmd

    nc = bacc.Bacc("TRN2", target_bir_lowering=False, num_devices=1)
    arrays, args = {}, {}
    of = {k: np.asarray(v) for k, v in inputs.items()}

    def give(name, value):
        value = np.ascontiguousarray(value)
        arrays[f"in_{name}"] = value
        args[name] = nc.dram_tensor(f"in_{name}", value.shape, mybir.dt.from_np(value.dtype), kind="ExternalInput").ap()

    for name in INPUTS:
        give(name, of[name])
    give("edge_attrs", np.concatenate([of["edge_attr_64"], of["edge_attr_256"]], axis=1))
    for layer in "12":
        w = of[f"L0_gnn_W{layer}"].transpose(1, 0, 2).reshape(D, REL * D)
        give(f"l0_w{layer}", np.concatenate([w, of[f"L0_gnn_self_w{layer}"]], axis=1))
        give(f"l2_w{layer}", np.concatenate([of[f"L2_gnn_W_l{layer}"], of[f"L2_gnn_W_r{layer}"]], axis=0))
        give(f"l3_w{layer}_t", of[f"L3_gnn_W{layer}"].T)
    give("w_edge", of["L1_gnn_W_edge"])
    give("we_t", of["L1_gnn_We"].T)
    give("w_n2m", of["L1_gnn_W_n2m"])
    give("w_qskv_t", np.concatenate([of[f"L1_gnn_W{n}"].T for n in ("q", "skip", "k", "v")], axis=1))
    give("wbeta", of["L1_gnn_Wbeta"])
    give("w_m2n_t", of["L1_gnn_W_m2n"].T)
    rows = [of["L0_gnn_b1"], of["L0_gnn_b2"], np.concatenate([of["L1_gnn_bq"], of["L1_gnn_bskip"]]),
            np.concatenate([of["L1_gnn_bk"], of["L1_gnn_bv"]]), of["L2_gnn_b1"], of["L2_gnn_b2"], of["L3_gnn_b1"], of["L3_gnn_b2"]]
    give("biases", np.stack(rows).reshape(1, len(BIASES) * D))
    out = nc.dram_tensor("out", (N, D), F32, kind="ExternalOutput").ap()
    build(nc, args, out)
    r = run_bass_kernel_spmd(nc, [arrays], core_ids=[0])
    return r.results[0]["out"]
```

```python
import concourse.bass as bass
from concourse import mybir
from contextlib import ExitStack

F32 = mybir.dt.float32
BF16 = mybir.dt.bfloat16
I32 = mybir.dt.int32
ALU = mybir.AluOpType
ACT = mybir.ActivationFunctionType
AX = mybir.AxisListType

P = 128
N = 2500
E = 42500
D = 256
REL = 8
DM = 128
DR = 64
HEADS = 4
HC = DM // HEADS
NB = -(-N // P)
LAST = N - (NB - 1) * P
NPAD = NB * P
TILES = -(-E // P)
EP = TILES * P
COLS = TILES
CH = 3
TQ = TILES // CH
SLOTS = TILES + NB - 1
RING = 16
ERING = 8
GRP = 4
TURNS = SLOTS // RING
GROUPS = RING // GRP
LOG_P = P.bit_length() - 1
assert CH * TQ == TILES and TQ <= P and TURNS * RING == SLOTS
NEG = -1e30
FORGET = 4 * NEG
HU = HC + 1
WA = D + 1
SM_SCALE = float(HC) ** -0.5
BIASES = ["l0_b1", "l0_b2", "l1_qs", "l1_kv", "l2_b1", "l2_b2", "l3_b1", "l3_b2"]
EPS = 1e-5
SLOPE = 0.015


class At:

    def __init__(self, i, step, k):
        self.i, self.step, self.k = i, step, k

    @property
    def n(self):
        return self.k if self.i is None else self.i * self.step + self.k

    def of(self, ring):
        return self.k % ring

    @property
    def turn(self):
        return self.k // self.step if self.i is None else self.i + self.k // self.step

    def in_ring(self, ring):
        return self.k // ring if self.i is None else self.i * (self.step // ring) + self.k // ring

    def plus(self, d):
        return At(self.i, self.step, self.k + d)


def dyn(at):
    return bass.ds(at.n, 1)


def pipeline(eng, count, step, stages, beside=()):
    first, last = max(lead for lead, _ in stages), min(lead for lead, _ in stages)
    turns = (count - (first - last)) // step
    if beside:
        assert turns >= NB
        turns = NB
    for tick in range(-first, -last):
        for lead, body in stages:
            if 0 <= tick + lead < count:
                body(At(None, step, tick + lead))
    with eng.Fori(0, turns) as i:
        for j in range(step):
            for lead, body in stages:
                body(At(i, step, j - last + lead))
            for tick, body in beside:
                if tick == j:
                    body(i)
    for tick in range(turns * step - last, count - last):
        for lead, body in stages:
            if 0 <= tick + lead < count:
                body(At(None, step, tick + lead))


class Chain:

    def __init__(self, eng, sem):
        self.eng, self.sem, self.count, self.loop = eng, sem, 0, None

    def after(self):
        if self.loop is None:
            self.eng.wait_ge(self.sem, self.count)
        else:
            i, per = self.loop
            self.eng.wait_ge(self.sem, i * per + self.count)

    def step(self, ins):
        ins.then_inc(self.sem, 1)
        self.count += 1

    def link(self, ins):
        self.step(ins)
        self.after()

    def run(self, times, per, body):
        start = self.count
        with self.eng.Fori(0, times) as i:
            self.loop = (i, per)
            body(i)
        assert self.count == start + per, (self.count - start, per)
        self.loop, self.count = None, start + per * times


def build(nc, a, out):
    top = ExitStack()

    def sb(name, shape, dt=F32, ctx=top):
        return ctx.enter_context(nc.sbuf_tensor(name, shape, dt))

    def sem(name):
        return top.enter_context(nc.semaphore(name))

    def dram(name, shape):
        return nc.dram_tensor(name, shape, F32, kind="Internal").ap()

    x = sb("x", [P, NB, D])
    h = sb("h", [P, NB, D])
    s = sb("s", [P, NB, D])
    acc = sb("acc", [P, NB, WA])
    esum = sb("esum", [P, NB, WA])
    ring = sb("ring", [P, RING, D])
    index = sb("index", [P, 2, SLOTS + RING])
    local = sb("local", [P, SLOTS])
    tile_rows = sb("tile_rows", [1, SLOTS], I32)
    unsorted = sb("unsorted", [1, 1], I32)
    ones = sb("ones", [P, P])
    iota_s = sb("iota_s", [P, SLOTS])
    iota_t = sb("iota_t", [P, CH])
    blocks = sb("blocks", [1, SLOTS], I32)
    keep = sb("keep", [P, SLOTS])
    forget = sb("forget", [P, SLOTS])
    now = sb("now", [P, 4, D])
    cur = sb("cur", [P, RING], I32)
    onehot = sb("onehot", [P, RING, P])
    ident = sb("ident", [P, P])
    identb = sb("identb", [P, P], BF16)
    iota = sb("iota", [P, P])
    biases = sb("biases", [P, len(BIASES), D])
    small = sb("small", [P, 4, NB])
    ps = top.enter_context(nc.psum_tensor("ps", [P, 8, 512], F32))

    records = nc.dram_tensor("records", (EP, 4), I32, kind="Internal").ap()
    edge_sorted = dram("edge_sorted", (EP, DR + D))
    table0 = dram("table0", (NPAD * REL, D))
    table1 = dram("table1", (NPAD * REL, D))
    kv_table = dram("kv_table", (NPAD, 2 * DM))
    h_table = dram("h_table", (NPAD, D))
    h1_table = dram("h1_table", (NPAD, D))
    e_store = dram("e_store", (SLOTS // GRP * P, GRP * DM))

    chain = Chain(nc.vector, sem("vector_chain"))
    got = [sem(f"got{j}") for j in range(RING)]
    hot, summed, added, collected = sem("onehot_ready"), sem("slot_summed"), sem("sum_added"), sem("sum_collected")
    staged, gather_tick = sem("indices_staged"), sem("gather_tick")
    BANKS = 4
    slots_done = [0]

    def rows(table):
        return table.rearrange("(b p) f -> p b f", p=P)

    def inspect():
        with ExitStack() as ctx:
            first_next = sb("first_next", [P, 4], I32, ctx)
            block_of = sb("block_of", [P, COLS + 1], I32, ctx)
            block_f = sb("block_f", [P, COLS + 1], F32, ctx)
            breaks = sb("breaks", [P, COLS], F32, ctx)
            count = sb("count", [P, 1], F32, ctx)
            loaded, filled, iotas, x_cleared, x_loaded = (
                sem(f"in_{n}") for n in ("loaded", "filled", "iotas", "x_cleared", "x_loaded"))
            counted, total = sem("breaks_counted"), sem("breaks_total")
            with nc.Block() as block:

                @block.sync
                def _(sp):
                    sp.dma_start(rec_p[:, :, :].rearrange("p t c -> p (t c)"),
                                 a["records"][0:EP, :].rearrange("(p t) c -> p (t c)", p=P)).then_inc(loaded, 16)
                    sp.dma_start(first_next[:, :], a["records"][COLS:EP + 1:COLS, :]).then_inc(loaded, 16)
                    sp.wait_ge(x_cleared, 1)
                    sp.dma_start(x[:, 0:NB - 1, :], a["x"][0:(NB - 1) * P, :].rearrange("(b p) f -> p b f", p=P)).then_inc(x_loaded, 16)
                    sp.dma_start(x[0:LAST, NB - 1, :], a["x"][(NB - 1) * P:N, :]).then_inc(x_loaded, 16)
                    sp.dma_start(biases[:, :, :].rearrange("p k c -> p (k c)"), a["biases"].to_broadcast([P, len(BIASES) * D])).then_inc(x_loaded, 16)
                    sp.wait_ge(x_loaded, 48)

                @block.gpsimd
                def _(pool):
                    pool.memset(x[:, NB - 1, :], 0.0).then_inc(x_cleared, 1)
                    pool.memset(ones[:, :], 1.0).then_inc(filled, 1)
                    pool.memset(ident[:, :], 1.0).then_inc(filled, 1)
                    pool.wait_ge(filled, 2)
                    pool.affine_select(out=ident[:, :], in_=ident[:, :], pattern=[[1, P]], compare_op=ALU.is_equal,
                                       fill=0.0, base=0, channel_multiplier=-1).then_inc(filled, 1)
                    pool.iota(iota[:, :], [[1, P]], 0, 0, allow_small_or_imprecise_dtypes=True).then_inc(iotas, 1)
                    pool.iota(iota_s[:, :], [[1, SLOTS]], 0, 0, allow_small_or_imprecise_dtypes=True).then_inc(iotas, 1)
                    pool.iota(iota_t[:, :], [[TQ, CH]], 0, 1, allow_small_or_imprecise_dtypes=True).then_inc(iotas, 1)

                @block.tensor
                def _(pe):
                    pe.wait_ge(filled, 3)
                    pe.wait_ge(counted, 1)
                    pe.matmul(ps[:, 0, 0:1], ones[:, :], count[:, :], start=True, stop=True).then_inc(total, 1)

                @block.vector
                def _(v):
                    c = chain
                    v.wait_ge(filled, 3)
                    c.step(v.tensor_copy(identb[:, :], ident[:, :]))
                    c.step(v.memset(index[:, :, SLOTS:], 0.0))
                    v.wait_ge(loaded, 32)
                    c.step(v.tensor_scalar(block_of[:, 0:COLS], rec_p[:, :, 0], LOG_P, None, ALU.logical_shift_right))
                    c.link(v.tensor_scalar(block_of[:, COLS:], first_next[:, 0:1], LOG_P, None, ALU.logical_shift_right))
                    c.link(v.tensor_copy(block_f[:, :], block_of[:, :]))
                    c.link(v.tensor_tensor(breaks[:, :], block_f[:, 0:COLS], block_f[:, 1:], ALU.is_gt))
                    v.tensor_reduce(count[:, :], breaks[:, :], AX.X, ALU.add).then_inc(counted, 1)
                    v.wait_ge(total, 1)
                    c.step(v.tensor_scalar(unsorted[:, :], ps[0:1, 0, 0:1], 1.0, None, ALU.min))

    def sort_edges():
        RB = next(k for k in (3, 2, 1) if COLS % k == 0)
        BUCKETS = NB + 1
        with ExitStack() as ctx:
            block_of = sb("block_of2", [P, COLS], I32, ctx)
            block_f = sb("block_f2", [P, COLS], F32, ctx)
            hit, run, tmp, place, every = (sb(n, [P, COLS], F32, ctx) for n in ("hit", "run", "tmp", "place", "every"))
            tri = sb("tri", [P, P], F32, ctx)
            tot = sb("tot", [P, BUCKETS], F32, ctx)
            ends = sb("ends", [P, BUCKETS], F32, ctx)
            base = sb("base", [P, BUCKETS], F32, ctx)
            attr = sb("attr", [P, RB, DR + D], F32, ctx)
            rec = sb("rec", [P, RB, 4], I32, ctx)
            copied, tri_ready, totals_ready, prefix_ready, places_ready, rec_staged, tick = (
                sem(f"sort_{n}") for n in ("copied", "tri", "totals", "prefix", "places", "staged", "tick"))
            attr_loaded = [sem(f"sort_attr{j}") for j in range(RB)]
            rec_out = [sem(f"sort_rec_out{j}") for j in range(RB)]
            attr_out = [sem(f"sort_attr_out{j}") for j in range(RB)]
            chain_sem = sem("sort_chain")

            def is_unsorted(eng):
                return eng.value_load(unsorted[0:1, 0:1], min_val=0, max_val=1)

            with nc.Block() as block:

                @block.sync
                def _(sp):
                    flag = is_unsorted(sp)
                    with sp.If(flag < 1):
                        sp.dma_start(records.rearrange("(p t) c -> p (t c)", p=P),
                                     a["records"][0:EP, :].rearrange("(p t) c -> p (t c)", p=P)).then_inc(copied, 16)
                        sp.wait_ge(copied, 16)
                    with sp.If(flag > 0):
                        columns = a["edge_attrs"].rearrange("(p t) f -> p t f", p=P)
                        for j in range(RB):
                            sp.dma_start(attr[:, j, :], columns[:, j, :]).then_inc(attr_loaded[j], 16)
                        with sp.Fori(1, COLS // RB) as i:
                            for j in range(RB):
                                sp.wait_ge(attr_out[j], i * 16)
                                sp.dma_start(attr[:, j:j + 1, :], columns[:, bass.ds(i * RB + j, 1), :]).then_inc(attr_loaded[j], 16)
                        for j in range(RB):
                            sp.wait_ge(attr_out[j], 16 * (COLS // RB))
                            sp.wait_ge(rec_out[j], 16 * (COLS // RB))

                @block.gpsimd
                def _(pool):
                    flag = is_unsorted(pool)
                    with pool.If(flag > 0):
                        pool.affine_select(out=tri[:, :], in_=ones[:, :], pattern=[[1, P]], compare_op=ALU.is_gt,
                                           fill=0.0, base=0, channel_multiplier=-1).then_inc(tri_ready, 1)
                        with pool.Fori(0, COLS // RB) as i:
                            for j in range(RB):
                                pool.wait_ge(rec_staged, (i * RB + j + 1) * 2)
                                pool.sem_inc(tick, 1)
                                pool.wait_ge(attr_loaded[j], i * 16 + 16)
                                pool.sem_inc(tick, 1)
                                where = bass.IndirectOffsetOnAxis(ap=cur[:, j:j + 1], axis=0)
                                pool.indirect_dma_start(records, where, rec[:, j, :], None).then_inc(rec_out[j], 16)
                                pool.indirect_dma_start(edge_sorted, where, attr[:, j, :], None).then_inc(attr_out[j], 16)

                @block.scalar
                def _(act):
                    flag = is_unsorted(act)
                    with act.If(flag > 0):
                        act.wait_ge(places_ready, 1)

                        def stage(at, j):
                            act.copy(cur[:, j:j + 1], place[:, at]).then_inc(rec_staged, 1)
                            act.copy(rec[:, j:j + 1, :], rec_p[:, at, :]).then_inc(rec_staged, 1)

                        for j in range(RB):
                            stage(slice(j, j + 1), j)
                        with act.Fori(1, COLS // RB) as i:
                            for j in range(RB):
                                act.wait_ge(rec_out[j], i * 16)
                                act.wait_ge(attr_out[j], i * 16)
                                stage(bass.ds(i * RB + j, 1), j)

                @block.tensor
                def _(pe):
                    flag = is_unsorted(pe)
                    with pe.If(flag > 0):
                        pe.wait_ge(tri_ready, 1)
                        pe.wait_ge(totals_ready, 1)
                        pe.matmul(ps[:, 0, 0:BUCKETS], tri[:, :], tot[:, :], start=True, stop=True).then_inc(prefix_ready, 1)
                        pe.matmul(ps[:, 1, 0:BUCKETS], ones[:, :], tot[:, :], start=True, stop=True).then_inc(prefix_ready, 1)

                @block.vector
                def _(v):
                    flag = is_unsorted(v)
                    with v.If(flag > 0):
                        c = Chain(v, chain_sem)
                        c.step(v.memset(place[:, :], 0.0))
                        c.step(v.memset(every[:, :], 1.0))
                        c.link(v.tensor_scalar(block_of[:, :], rec_p[:, :, 0], LOG_P, None, ALU.logical_shift_right))
                        c.link(v.tensor_copy(block_f[:, :], block_of[:, :]))

                        def ranks(i):
                            col = bass.ds(i, 1)
                            c.link(v.tensor_scalar(hit[:, :], block_f[:, :], iota[:, col], None, ALU.is_equal))
                            c.link(v.tensor_tensor_scan(run[:, :], every[:, :], hit[:, :], 0.0, ALU.mult, ALU.add))
                            c.step(v.tensor_copy(tot[:, col], run[:, COLS - 1:COLS]))
                            c.link(v.tensor_tensor(tmp[:, :], run[:, :], hit[:, :], ALU.mult))
                            c.link(v.tensor_tensor(place[:, :], place[:, :], tmp[:, :], ALU.add))

                        c.run(BUCKETS, 5, ranks)
                        v.tensor_copy(tmp[:, 0:1], tot[:, 0:1]).then_inc(totals_ready, 1)
                        v.wait_ge(prefix_ready, 2)
                        c.link(v.tensor_copy(base[:, :], ps[:, 1, 0:BUCKETS]))
                        c.link(v.tensor_tensor_scan(ends[:, :], every[:, 0:BUCKETS], base[:, :], -1.0, ALU.mult, ALU.add))
                        c.link(v.tensor_tensor(base[:, :], ends[:, :], base[:, :], ALU.subtract))
                        c.link(v.tensor_tensor(base[:, :], base[:, :], ps[:, 0, 0:BUCKETS], ALU.add))

                        def places(i):
                            col = bass.ds(i, 1)
                            c.link(v.tensor_scalar(hit[:, :], block_f[:, :], iota[:, col], base[:, col], ALU.is_equal, ALU.mult))
                            c.link(v.tensor_tensor(place[:, :], place[:, :], hit[:, :], ALU.add))

                        c.run(BUCKETS, 2, places)
                        v.tensor_copy(tmp[:, 0:1], place[:, 0:1]).then_inc(places_ready, 1)

    def make_slots():
        with ExitStack() as ctx:
            rt = sb("rt", [TQ, CH, P, 4], I32, ctx)
            first = sb("first", [TQ, CH], I32, ctx)
            start = sb("start", [TQ, CH], F32, ctx)
            fields = sb("fields", [TQ, 3, CH, P], F32, ctx)
            typ = sb("typ", [TQ, CH, P], F32, ctx)
            begun = sb("begun", [TQ, CH, SLOTS], F32, ctx)
            pick = sb("pick", [TQ, CH, SLOTS], F32, ctx)
            tile = sb("tile", [P, SLOTS], F32, ctx)
            block_f = sb("block_s", [P, SLOTS], F32, ctx)
            loaded, begun_ready, tiles_ready, pick_ready, picked = (
                sem(f"slots_{n}") for n in ("loaded", "begun", "tiles", "pick", "picked"))
            with nc.Block() as block:

                @block.sync
                def _(sp):
                    sp.dma_start(rt[:, :, :, :].rearrange("q c p f -> q c (p f)"),
                                 records.rearrange("(c q p) f -> q c (p f)", c=CH, q=TQ)).then_inc(loaded, 16)

                @block.tensor
                def _(pe):
                    pe.wait_ge(begun_ready, 1)
                    for c in range(CH):
                        ins = pe.matmul(ps[:, 0, 0:SLOTS], ones[0:TQ, :], begun[:, c, :], start=c == 0, stop=c == CH - 1)
                    ins.then_inc(tiles_ready, 1)
                    pe.wait_ge(pick_ready, 1)
                    for k in range(3):
                        for c in range(CH):
                            ins = pe.matmul(ps[:, 1 + k, 0:SLOTS], fields[:, k, c, :], pick[:, c, :], start=c == 0, stop=c == CH - 1)
                        ins.then_inc(picked, 1)

                @block.vector
                def _(v):
                    c = chain
                    v.wait_ge(loaded, 16)
                    c.link(v.tensor_scalar(first[:, :], rt[:, :, 0, 0], LOG_P, None, ALU.logical_shift_right))
                    c.link(v.tensor_copy(start[:, :], first[:, :]))
                    c.link(v.tensor_scalar(start[:, :], start[:, :], float(NB - 1), None, ALU.min))
                    c.link(v.tensor_tensor(start[:, :], start[:, :], iota_t[0:TQ, :], ALU.add))
                    c.link(v.memset(start[0:1, 0:1], 1e9))
                    for k in range(CH):
                        ins = v.tensor_scalar(begun[:, k, :], iota_s[0:TQ, :], start[:, k:k + 1], None, ALU.is_ge)
                        c.step(ins) if k < CH - 1 else ins.then_inc(begun_ready, 1)
                    c.step(v.tensor_copy(fields[:, 1, :, :], rt[:, :, :, 1]))
                    c.step(v.tensor_copy(fields[:, 2, :, :], rt[:, :, :, 0]))
                    c.link(v.tensor_copy(typ[:, :, :], rt[:, :, :, 2]))
                    c.step(v.scalar_tensor_tensor(fields[:, 0, :, :].rearrange("q c p -> q (c p)"),
                                                  fields[:, 1, :, :].rearrange("q c p -> q (c p)"), float(REL),
                                                  typ[:, :, :].rearrange("q c p -> q (c p)"), ALU.mult, ALU.add))
                    v.wait_ge(tiles_ready, 1)
                    c.link(v.tensor_copy(tile[:, :], ps[:, 0, 0:SLOTS]))
                    for k in range(CH):
                        ins = v.tensor_scalar(pick[:, k, :], tile[0:TQ, :], iota_t[0:TQ, k:k + 1], None, ALU.is_equal)
                        c.step(ins) if k < CH - 1 else ins.then_inc(pick_ready, 1)
                    c.link(v.tensor_tensor(block_f[:, :], iota_s[:, :], tile[:, :], ALU.subtract))
                    c.step(v.tensor_copy(blocks[:, :], block_f[0:1, :]))
                    c.step(v.tensor_scalar(tile_rows[:, :], tile[0:1, :], float(P), None, ALU.mult))
                    c.step(v.memset(keep[:, 0:1], 0.0))
                    c.link(v.tensor_tensor(keep[:, 1:], block_f[:, 1:], block_f[:, 0:SLOTS - 1], ALU.is_equal))
                    c.step(v.tensor_scalar(forget[:, :], keep[:, :], 1.0, -FORGET, ALU.subtract, ALU.mult))
                    v.wait_ge(picked, 3)
                    c.step(v.tensor_copy(index[:, 0, 0:SLOTS], ps[:, 1, 0:SLOTS]))
                    c.step(v.tensor_copy(index[:, 1, 0:SLOTS], ps[:, 2, 0:SLOTS]))
                    c.step(v.scalar_tensor_tensor(local[:, :], block_f[:, :], -float(P), ps[:, 3, 0:SLOTS], ALU.mult, ALU.add))

    var_ready, std_ready, scale_ready = sem("var_ready"), sem("std_ready"), sem("scale_ready")
    norms = [0]

    def normalised(act, dest, b):
        return act.activation(dest, x[:, b, :].rearrange("p o c -> p (o c)"), ACT.Relu, bias=small[:, 3, b], scale=small[:, 2, b])

    def layernorm(name, write=True):
        with ExitStack() as ctx:
            stats = sb(f"{name}_stats", [P, NB, 6], F32, ctx)
            mv = sb(f"{name}_mv", [P, NB, 2], F32, ctx)
            norms[0] += 1
            nth = norms[0]
            with nc.Block() as block:

                @block.vector
                def _(v):
                    c = chain

                    for b in range(NB):
                        c.step(v.bn_stats(stats[:, b, :], x[:, b, :]))
                    c.after()
                    for b in range(NB):
                        c.step(v.bn_aggr(mv[:, b, :], stats[:, b, :]))
                    c.after()
                    v.tensor_scalar(small[:, 0, :], mv[:, :, 1], EPS, None, ALU.add).then_inc(var_ready, 1)
                    v.wait_ge(std_ready, nth)
                    c.link(v.reciprocal(small[:, 2, :], small[:, 1, :]))
                    v.scalar_tensor_tensor(small[:, 3, :], mv[:, :, 0], -1.0, small[:, 2, :], ALU.mult, ALU.mult).then_inc(scale_ready, 1)

                @block.scalar
                def _(act):
                    act.wait_ge(var_ready, nth)
                    act.activation(small[:, 1, :], small[:, 0, :], ACT.Sqrt).then_inc(std_ready, 1)
                    if write:
                        act.wait_ge(scale_ready, nth)
                        for b in range(NB):
                            act.activation(h[:, b, :], x[:, b, :], ACT.Relu, bias=small[:, 3, b:b + 1], scale=small[:, 2, b:b + 1])

    def gather_rows(pool, table, first_turn):
        with pool.Fori(0, SLOTS // RING) as i:
            for g in range(GROUPS):
                pool.wait_ge(staged, i * GROUPS + (first_turn // TURNS * (TURNS + 1) * GROUPS + g + 1))
                pool.sem_inc(gather_tick, 1)
                for j in range(g * GRP, (g + 1) * GRP):
                    pool.indirect_dma_start(ring[:, j, 0:table.shape[1]], None, table,
                                            bass.IndirectOffsetOnAxis(ap=cur[:, j:j + 1], axis=0)).then_inc(got[j], 16)

    def index_stager(act, column, used, base):
        for g in range(GROUPS):
            act.copy(cur[:, g * GRP:(g + 1) * GRP], index[:, column, g * GRP:(g + 1) * GRP]).then_inc(staged, 1)

        def stage(t):
            if t.k % GRP == GRP - 1:
                act.wait_ge(used, base + t.plus(1).n)
                g = t.of(RING) // GRP
                act.copy(cur[:, g * GRP:(g + 1) * GRP],
                         index[:, column, bass.ds(t.plus(RING - GRP + 1).n, GRP)]).then_inc(staged, 1)
        return stage

    def slot_block(eng, t):
        return bass.ds(eng.value_load(blocks[0:1, dyn(t)], min_val=0, max_val=NB - 1), 1)

    def onehot_maker(v, base):
        def make_onehot(t):
            v.tensor_scalar(onehot[:, t.of(RING), :], iota[:, :], local[:, dyn(t)], None, ALU.is_equal).then_inc(hot, 1)
        return make_onehot

    def slot_summer(pe, base, turn, width, banks=BANKS):
        def sum_slot(t):
            pe.wait_ge(got[t.of(RING)], (t.turn + turn) * 16 + 16)
            pe.wait_ge(hot, base + t.plus(1).n)
            pe.wait_ge(added, base + t.plus(1 + BANKS - banks).n)
            pe.matmul(ps[:, t.of(banks), 0:width], onehot[:, t.of(RING), :], ring[:, t.of(RING), 0:width],
                      start=True, stop=True).then_inc(summed, 1)
        return sum_slot

    def slot_adder(v, base, width, banks=BANKS):
        def add_slot(t):
            v.wait_ge(summed, base + t.plus(1).n)
            v.wait_ge(added, base + t.plus(BANKS).n)
            v.wait_ge(collected, base + t.plus(1).n)
            v.scalar_tensor_tensor(now[:, t.of(4), 0:width], now[:, (t.k - 1) % 4, 0:width], keep[:, dyn(t)],
                                   ps[:, t.of(banks), 0:width], ALU.mult, ALU.add).then_inc(added, 1)
        return add_slot

    def slot_collector(act, base, into, width):
        def collect(t):
            block = slot_block(act, t)
            act.wait_ge(added, base + t.plus(BANKS + 1).n)
            act.wait_ge(collected, base + t.plus(4).n)
            act.copy(into[:, block, 0:width], now[:, t.of(4):t.of(4) + 1, 0:width]).then_inc(collected, 1)
        return collect

    def clear_sums(v, base, into, width, cleared, count=2):
        if base == 0:
            v.sem_inc(added, BANKS)
            v.sem_inc(collected, 4)
        v.memset(now[:, 3, 0:width], 0.0).then_inc(cleared, 1)
        v.memset(into[:, :, 0:width], 0.0).then_inc(cleared, 1)
        v.wait_ge(cleared, count)

    tin_ready, turned_in, tin_turned = sem("tin_ready"), sem("tin_turned"), sem("turned_copied")
    multiplied = [sem(f"multiplied{k}") for k in range(5)]
    taken = [sem(f"taken{k}") for k in range(5)]
    stage_free = [sem(f"stage_free{j}") for j in range(2)]
    weights_loaded = sem("weights_loaded")
    calls = {"weights": 0, "tile": 0, "store": 0, **{k: 0 for k in range(6)}}

    def node_products(ctx, products):
        if not products:
            return (lambda sp: None), (), (), ()
        each, tiles, base = len(products), calls["tile"], calls[0]
        calls["tile"] += NB * each
        calls[0] += NB * each
        calls["weights"] += 16 * each
        weights = [sb(f"beside{tiles}_w{q}", [P, 2, D], F32, ctx) for q in range(each)]
        tin = sb(f"beside{tiles}_tin", [P, D], F32, ctx)
        tt = sb(f"beside{tiles}_tt", [P, D], F32, ctx)
        turned_bank, product_bank = 4, 5
        work = {"act": [], "pe": [], "dve": []}

        def load(sp):
            for q, (_, source, _, _) in enumerate(products):
                sp.dma_start(weights[q][:, :, :], source.rearrange("(k p) n -> p k n", p=P)).then_inc(weights_loaded, 16)

        def add_product(q, first, take, write):
            def before(i):
                return i * each + q
            engine, body = take
            eng = {"act": nc.scalar, "dve": nc.vector}[engine]

            def take_in(i):
                eng.wait_ge(turned_in, before(i) + (tiles + 2))
                eng.wait_ge(taken[0], before(i) + (base + 1))
                body(eng, bass.ds(i, 1), tin).then_inc(tin_ready, 1)

            def turn_in(i):
                nc.tensor.wait_ge(tin_ready, before(i) + (tiles + 1))
                nc.tensor.wait_ge(tin_turned, before(i) + (tiles + 2))
                for k in range(2):
                    ins = nc.tensor.transpose(ps[:, turned_bank, k * P:(k + 1) * P], tin[:, k * P:(k + 1) * P], ident[:, :])
                ins.then_inc(turned_in, 1)

            def copy_turned(i):
                nc.vector.wait_ge(turned_in, before(i) + (tiles + 3))
                nc.vector.tensor_copy(tt[:, :], ps[:, turned_bank, 0:D]).then_inc(tin_turned, 1)

            def multiply(i):
                nc.tensor.wait_ge(weights_loaded, calls["weights"])
                nc.tensor.wait_ge(tin_turned, before(i) + (tiles + 3))
                nc.tensor.wait_ge(taken[0], before(i) + (base + 1))
                for k in range(2):
                    ins = nc.tensor.matmul(ps[:, product_bank, 0:D], tt[:, k * P:(k + 1) * P], weights[q][:, k, :],
                                           start=k == 0, stop=k == 1)
                ins.then_inc(multiplied[0], 1)

            def use_product(i):
                nc.vector.wait_ge(multiplied[0], before(i) + (base + 1))
                write(nc.vector, bass.ds(i, 1), ps[:, product_bank, 0:D]).then_inc(taken[0], 1)

            work[engine].append((first, take_in))
            work["pe"] += [(first + 1, turn_in), (first + 3, multiply)]
            work["dve"] += [(first + 2, copy_turned), (first + 5, use_product)]

        for q, (first, _, take, write) in enumerate(products):
            add_product(q, first, take, write)
        return load, work["act"], work["pe"], work["dve"]

    gather_cleared, clearings = sem("gather_cleared"), [0]

    def gather_sum(table, column, products=()):
        turn, base = slots_done[0] // RING, slots_done[0]
        slots_done[0] += SLOTS
        clearings[0] += 2
        with ExitStack() as ctx:
            load, act_work, pe_work, v_work = node_products(ctx, products)
            with nc.Block() as block:

                @block.sync
                def _(sp):
                    load(sp)

                @block.gpsimd
                def _(pool):
                    gather_rows(pool, table, turn)

                @block.scalar
                def _(act):
                    stager = index_stager(act, column, summed, base)
                    act.wait_ge(gather_cleared, clearings[0])
                    pipeline(act, SLOTS, RING, [(0, stager), (-1, slot_collector(act, base, acc, D))], act_work)

                @block.tensor
                def _(pe):
                    pipeline(pe, SLOTS, RING, [(0, slot_summer(pe, base, turn, D))], pe_work)

                @block.vector
                def _(v):
                    clear_sums(v, base, acc, D, gather_cleared, clearings[0])
                    pipeline(v, SLOTS, RING, [(2, onehot_maker(v, base)), (0, slot_adder(v, base, D))], v_work)

    def gather_sum_with_edges(table, column):
        turn, base = slots_done[0] // RING, slots_done[0]
        slots_done[0] += SLOTS
        cleared, loaded, turned, copied, projected, kept, e_summed, e_added, e_collected, w_product, w_ready, ones_in = (
            sem(f"edge_{n}") for n in ("cleared", "w_loaded", "turned", "turned_copied", "projected", "kept", "summed",
                                       "added", "collected", "w_product", "w_ready", "ones_in"))
        stored = [sem(f"edge_stored{g}") for g in range(2)]
        edge_in = [sem(f"edge_in{j}") for j in range(ERING)]
        with ExitStack() as ctx:
            w_edge = sb("w_edge", [DR, DR], F32, ctx)
            we_t = sb("we_t", [DR, DM], F32, ctx)
            w_e = sb("w_e", [DR, DM], F32, ctx)
            edge_ring = sb("edge_ring", [P, ERING, DR + WA], F32, ctx)
            now_e = sb("now_e", [P, 4, WA], F32, ctx)
            attr_t = sb("attr_t", [DR, 4, P], F32, ctx)
            e_out = sb("e_out", [P, 2, GRP * DM], F32, ctx)

            def group_rows(t):
                g = t.i * (GROUPS * P) + t.k // GRP * P if t.i is not None else t.k // GRP * P
                return bass.ds(g, P)

            with nc.Block() as block:

                @block.sync
                def _(sp):
                    sp.dma_start(w_edge[:, :], a["w_edge"]).then_inc(loaded, 16)
                    sp.dma_start(we_t[:, :], a["we_t"]).then_inc(loaded, 16)
                    flag = sp.value_load(unsorted[0:1, 0:1], min_val=0, max_val=1)

                    def load_tiles(source):
                        def load(t, wait):
                            row = sp.value_load(tile_rows[0:1, dyn(t)], min_val=0, max_val=EP - P)
                            if wait:
                                sp.wait_ge(e_summed, t.plus(1 - ERING).n)
                            sp.dma_start(edge_ring[:, t.of(ERING), 0:DR + D], source[bass.ds(row, P), :]).then_inc(edge_in[t.of(ERING)], 16)

                        for j in range(ERING):
                            load(At(None, ERING, j), False)
                        with sp.Fori(1, SLOTS // ERING) as i:
                            for j in range(ERING):
                                load(At(i, ERING, j), True)

                    with sp.If(flag < 1):
                        load_tiles(a["edge_attrs"])
                    with sp.If(flag > 0):
                        load_tiles(edge_sorted)

                @block.gpsimd
                def _(pool):
                    gather_rows(pool, table, turn)

                @block.tensor
                def _(pe):
                    pe.wait_ge(loaded, 32)
                    pe.matmul(ps[0:DR, 7, 0:DM], w_edge[:, :], we_t[:, :], start=True, stop=True).then_inc(w_product, 1)
                    pe.wait_ge(w_ready, 1)
                    pe.wait_ge(ones_in, 1)

                    def turn_attr(t):
                        pe.wait_ge(edge_in[t.of(ERING)], t.in_ring(ERING) * 16 + 16)
                        pe.wait_ge(copied, t.plus(1).n)
                        pe.transpose(ps[:, 4 + t.of(2), 0:P], edge_ring[:, t.of(ERING), 0:P], ident[:, :]).then_inc(turned, 1)

                    def project_attr(t):
                        pe.wait_ge(copied, t.plus(3).n)
                        pe.wait_ge(kept, t.plus(1).n)
                        pe.matmul(ps[:, 6 + t.of(2), 0:DM], attr_t[:, t.of(4), :], w_e[:, :],
                                  start=True, stop=True).then_inc(projected, 1)

                    def sum_edges(t):
                        pe.wait_ge(hot, base + t.plus(1).n)
                        pe.wait_ge(e_added, t.plus(1).n)
                        pe.matmul(ps[:, 2 + t.of(2), 0:WA], onehot[:, t.of(RING), :], edge_ring[:, t.of(ERING), DR:DR + WA],
                                  start=True, stop=True).then_inc(e_summed, 1)

                    pipeline(pe, SLOTS, RING, [(2, turn_attr), (0, project_attr), (0, sum_edges),
                                               (0, slot_summer(pe, base, turn, D, banks=2))])

                @block.scalar
                def _(act):
                    act.wait_ge(w_product, 1)
                    act.copy(w_e[:, :], ps[0:DR, 7, 0:DM]).then_inc(w_ready, 1)
                    stager = index_stager(act, column, summed, base)
                    act.wait_ge(cleared, 4)
                    for g in range(2):
                        act.sem_inc(stored[g], 16)

                    def store(t):
                        if t.k % GRP == GRP - 1:
                            g = t.k // GRP % 2
                            act.wait_ge(kept, t.plus(3).n)
                            act.dma_start(e_store[group_rows(t), :], e_out[:, g, :]).then_inc(stored[g], 16)

                    def collect(t):
                        block_of = slot_block(act, t)
                        act.wait_ge(added, base + t.plus(BANKS + 1).n)
                        act.wait_ge(collected, base + t.plus(4).n)
                        act.copy(acc[:, block_of, 0:D], now[:, t.of(4):t.of(4) + 1, 0:D]).then_inc(collected, 1)
                        act.wait_ge(e_added, t.plus(3).n)
                        act.wait_ge(e_collected, t.plus(4).n)
                        act.copy(esum[:, block_of, :], now_e[:, t.of(4):t.of(4) + 1, :]).then_inc(e_collected, 1)

                    pipeline(act, SLOTS, RING, [(0, stager), (0, store), (-1, collect)])
                    for g in range(2):
                        act.wait_ge(stored[g], 16 * (SLOTS // GRP // 2 + 1))

                @block.vector
                def _(v):
                    clear_sums(v, base, acc, D, cleared)
                    v.memset(now_e[:, 3, :], 0.0).then_inc(cleared, 1)
                    v.memset(esum[:, :, :], 0.0).then_inc(cleared, 1)
                    v.wait_ge(cleared, 4)
                    v.memset(edge_ring[:, :, DR + D:], 1.0).then_inc(ones_in, 1)
                    v.sem_inc(copied, 2)
                    v.sem_inc(kept, 2)
                    v.sem_inc(e_added, 2)
                    v.sem_inc(e_collected, 4)

                    def copy_turned(t):
                        v.wait_ge(turned, t.plus(1).n)
                        v.tensor_copy(attr_t[:, t.of(4), :], ps[0:DR, 4 + t.of(2), 0:P]).then_inc(copied, 1)

                    def keep_projected(t):
                        v.wait_ge(projected, t.plus(1).n)
                        if t.k % GRP == 0:
                            v.wait_ge(stored[t.k // GRP % 2], t.in_ring(2 * GRP) * 16 + 16)
                        v.tensor_copy(e_out[:, t.k // GRP % 2, t.of(GRP) * DM:(t.of(GRP) + 1) * DM],
                                      ps[:, 6 + t.of(2), 0:DM]).then_inc(kept, 1)

                    def add_edges(t):
                        v.wait_ge(e_summed, t.plus(1).n)
                        v.wait_ge(e_added, t.plus(2).n)
                        v.wait_ge(e_collected, t.plus(1).n)
                        v.scalar_tensor_tensor(now_e[:, t.of(4), :], now_e[:, (t.k - 1) % 4, :], keep[:, dyn(t)],
                                               ps[:, 2 + t.of(2), 0:WA], ALU.mult, ALU.add).then_inc(e_added, 1)

                    pipeline(v, SLOTS, RING, [(2, onehot_maker(v, base)), (2, copy_turned), (0, keep_projected),
                                              (0, add_edges), (0, slot_adder(v, base, D, banks=2))])

    def attention():
        turn, base = slots_done[0] // RING, slots_done[0]
        slots_done[0] += SLOTS
        (cleared, turned, ot_ready, pen_ready, qx_ready, kve_ready, prod_ready, alpha_ready, scored, mx_ready,
         mnew_ready, md_ready, r_ready, me_ready, ad_ready, p_ready, msg_ready, scaled) = (
            sem(f"att_{n}") for n in ("cleared", "turned", "ot", "pen", "qx", "kve", "prod", "alpha", "scored", "mx",
                                      "mnew", "md", "r", "me", "ad", "p", "msg", "scaled"))
        e_got = [sem(f"att_e{g}") for g in range(GROUPS)]
        with ExitStack() as ctx:
            e_in = sb("e_in", [P, GROUPS, GRP, DM], F32, ctx)
            onehot_t = sb("onehot_t", [P, 8, P], F32, ctx)
            penalty = sb("penalty", [P, 8, P], BF16, ctx)
            kve = sb("kve", [P, 8, 2, DM], F32, ctx)
            prod = sb("prod", [P, 2, DM], F32, ctx)
            alpha = sb("alpha", [P, 8, HEADS], F32, ctx)
            mx = sb("mx", [P, 4, HEADS], F32, ctx)
            mnew = sb("mnew", [P, 4, HEADS], F32, ctx)
            md = sb("md", [P, 4, HEADS], F32, ctx)
            r = sb("r", [P, 8, HEADS], F32, ctx)
            ad = sb("ad", [P, 4, HEADS], F32, ctx)
            msg = sb("msg", [P, 4, HEADS, HU], F32, ctx)
            WM = HEADS * HU

            def sums_at(t):
                return ps[:, 6 + t.of(2), 0:WM]

            with nc.Block() as block:

                @block.sync
                def _(sp):
                    for g in range(GROUPS):
                        sp.dma_start(e_in[:, g, :, :].rearrange("p s c -> p (s c)"), e_store[g * P:(g + 1) * P, :]).then_inc(e_got[g], 16)
                    with sp.Fori(1, SLOTS // RING) as i:
                        for g in range(GROUPS):
                            sp.wait_ge(kve_ready, (i - 1) * RING + (g + 1) * GRP)
                            sp.dma_start(e_in[:, g, :, :].rearrange("p s c -> p (s c)"),
                                         e_store[bass.ds(i * (P * GROUPS) + g * P, P), :]).then_inc(e_got[g], 16)

                @block.gpsimd
                def _(pool):
                    groups = turn // TURNS * (TURNS + 1) * GROUPS

                    def gather(t):
                        if t.k % GRP == 0:
                            at = t.i * GROUPS if t.i is not None else 0
                            pool.wait_ge(staged, at + (groups + t.k // GRP + 1))
                            pool.sem_inc(gather_tick, 1)
                        j = t.of(RING)
                        pool.indirect_dma_start(ring[:, j, 0:2 * DM], None, kv_table,
                                                bass.IndirectOffsetOnAxis(ap=cur[:, j:j + 1], axis=0)).then_inc(got[j], 16)

                    def add_edge_part(t):
                        pool.wait_ge(got[t.of(RING)], (t.turn + turn) * 16 + 16)
                        pool.wait_ge(e_got[t.of(RING) // GRP], t.turn * 16 + 16)
                        pool.wait_ge(msg_ready, t.plus(1).n)
                        e = e_in[:, t.of(RING) // GRP, t.of(GRP):t.of(GRP) + 1, :].to_broadcast([P, 2, DM])
                        pool.tensor_tensor(kve[:, t.of(8), :, :], ring[:, t.of(RING), 0:2 * DM].rearrange("p (a c) -> p a c", a=2),
                                           e, ALU.add).then_inc(kve_ready, 1)

                    pipeline(pool, SLOTS, RING, [(3, add_edge_part), (11, gather)])

                @block.tensor
                def _(pe):
                    pe.wait_ge(cleared, 2)

                    def sum_messages(t):
                        pe.wait_ge(msg_ready, t.plus(1 + 8).n)
                        pe.wait_ge(added, base + t.plus(BANKS - 1).n)
                        pe.matmul(sums_at(t), onehot[:, t.of(RING), :], msg[:, t.of(4), :, :].rearrange("p h c -> p (h c)"),
                                  start=True, stop=True).then_inc(summed, 1)

                    def spread_maxima(t):
                        pe.wait_ge(mnew_ready, t.plus(2).n)
                        pe.wait_ge(ad_ready, t.plus(1).n)
                        pe.matmul(ps[:, 1, 0:HEADS], onehot_t[:, t.of(8), :], mnew[:, t.of(4), :], start=True, stop=True).then_inc(me_ready, 1)

                    def spread_scores(t):
                        pe.wait_ge(pen_ready, t.plus(2).n)
                        pe.wait_ge(mx_ready, t.plus(1).n)
                        bank = ps[:, 4 + t.of(2), :]
                        pe.matmul(bank, identb[:, :], penalty[:, t.of(8):t.of(8) + 1, :].to_broadcast([P, HEADS, P]),
                                  start=True, stop=False)
                        pe.wait_ge(alpha_ready, t.plus(1).n)
                        for head in range(HEADS):
                            ins = pe.matmul(bank[:, head * P:(head + 1) * P],
                                            alpha[:, t.of(8), head:head + 1].to_broadcast([P, P]), ident[:, :],
                                            start=False, stop=head == HEADS - 1)
                        ins.then_inc(scored, 1)

                    def spread_queries(t):
                        block_of = slot_block(pe, t)
                        pe.wait_ge(ot_ready, t.plus(1).n)
                        pe.wait_ge(prod_ready, t.plus(1).n)
                        pe.matmul(ps[:, 2 + t.of(2), 0:DM], onehot_t[:, t.of(8), :],
                                  s[:, block_of, 0:DM].rearrange("p o c -> p (o c)"), start=True, stop=True).then_inc(qx_ready, 1)

                    def turn_onehot(t):
                        pe.wait_ge(hot, base + t.plus(1).n)
                        pe.wait_ge(pen_ready, t.plus(1).n)
                        pe.transpose(ps[:, 0, 0:P], onehot[:, t.of(RING), :], ident[:, :]).then_inc(turned, 1)

                    pipeline(pe, SLOTS, RING, [(-6, sum_messages), (1, spread_scores),
                                               (3, spread_queries), (5, turn_onehot), (-2, spread_maxima)])

                @block.scalar
                def _(act):
                    act.sem_inc(pen_ready, 1)

                    def old_factor(t):
                        act.wait_ge(md_ready, t.plus(1).n)
                        act.activation(r[:, t.of(8), :], md[:, t.of(4), :], ACT.Exp, scale=SM_SCALE).then_inc(r_ready, 1)

                    def weights(t):
                        act.wait_ge(ad_ready, t.plus(2).n)
                        act.activation(msg[:, t.of(4), :, HC], ad[:, t.of(4), :], ACT.Exp, scale=SM_SCALE).then_inc(p_ready, 1)

                    def copy_turned(t):
                        act.wait_ge(turned, t.plus(1).n)
                        act.copy(onehot_t[:, t.of(8), :], ps[:, 0, 0:P]).then_inc(ot_ready, 1)
                        act.activation(penalty[:, t.of(8), :], ps[:, 0, 0:P], ACT.Copy, scale=-NEG, bias=NEG).then_inc(pen_ready, 1)

                    stager = index_stager(act, 1, kve_ready, 0)
                    act.wait_ge(cleared, 2)
                    pipeline(act, SLOTS, RING, [(4, copy_turned), (1, stager), (-8, slot_collector(act, base, acc, WM)),
                                                (-4, weights), (-1, old_factor)])

                @block.vector
                def _(v):
                    clear_sums(v, base, acc, WM, cleared)
                    v.memset(mnew[:, 3, :], NEG).then_inc(mnew_ready, 1)
                    v.sem_inc(prod_ready, 2)
                    v.sem_inc(mx_ready, 2)
                    v.sem_inc(ad_ready, 1)
                    v.sem_inc(msg_ready, 8)

                    def rescale(t):
                        v.wait_ge(r_ready, t.plus(1).n)
                        v.wait_ge(added, base + t.plus(BANKS).n)
                        v.wait_ge(collected, base + t.plus(1).n)
                        v.tensor_tensor(now[:, t.of(4), 0:WM].rearrange("p (h c) -> p h c", h=HEADS),
                                        now[:, (t.k - 1) % 4, 0:WM].rearrange("p (h c) -> p h c", h=HEADS),
                                        r[:, t.of(8), :].unsqueeze(2).to_broadcast([P, HEADS, HU]), ALU.mult).then_inc(scaled, 1)

                    def multiply(t):
                        v.wait_ge(qx_ready, t.plus(1).n)
                        v.wait_ge(kve_ready, t.plus(1).n)
                        v.tensor_tensor(prod[:, t.of(2), :], kve[:, t.of(8), 0, :], ps[:, 2 + t.of(2), 0:DM], ALU.mult).then_inc(prod_ready, 1)

                    def weigh(t):
                        v.wait_ge(p_ready, t.plus(1).n)
                        m = msg[:, t.of(4), :, :]
                        v.tensor_tensor(m[:, :, 0:HC], kve[:, t.of(8), 1, :].rearrange("p (h c) -> p h c", h=HEADS),
                                        m[:, :, HC:HU].to_broadcast([P, HEADS, HC]), ALU.mult).then_inc(msg_ready, 1)

                    def score(t):
                        v.wait_ge(prod_ready, t.plus(3).n)
                        v.tensor_reduce(alpha[:, t.of(8), :], prod[:, t.of(2), :].rearrange("p (h c) -> p h c", h=HEADS),
                                        AX.X, ALU.add).then_inc(alpha_ready, 1)

                    def add(t):
                        new = now[:, t.of(4), 0:WM]
                        v.wait_ge(summed, base + t.plus(1).n)
                        v.wait_ge(scaled, t.plus(1).n)
                        v.tensor_tensor(new, new, sums_at(t), ALU.add).then_inc(added, 1)

                    def slot_max(t):
                        v.wait_ge(scored, t.plus(1).n)
                        v.tensor_reduce(mx[:, t.of(4), :], ps[:, 4 + t.of(2), :].rearrange("p (h e) -> p h e", h=HEADS),
                                        AX.X, ALU.max).then_inc(mx_ready, 1)

                    def subtract(t):
                        v.wait_ge(me_ready, t.plus(1).n)
                        v.tensor_tensor(ad[:, t.of(4), :], alpha[:, t.of(8), :], ps[:, 1, 0:HEADS], ALU.subtract).then_inc(ad_ready, 1)

                    def new_max(t):
                        v.wait_ge(mx_ready, t.plus(3).n)
                        v.wait_ge(mnew_ready, t.plus(1).n)
                        v.scalar_tensor_tensor(mnew[:, t.of(4), :], mnew[:, (t.k - 1) % 4, :], forget[:, dyn(t)],
                                               mx[:, t.of(4), :], ALU.add, ALU.max).then_inc(mnew_ready, 1)

                    def max_step(t):
                        v.wait_ge(mnew_ready, t.plus(2).n)
                        v.scalar_tensor_tensor(md[:, t.of(4), :], mnew[:, (t.k - 1) % 4, :], forget[:, dyn(t)],
                                               mnew[:, t.of(4), :], ALU.add, ALU.subtract).then_inc(md_ready, 1)

                    pipeline(v, SLOTS, RING, [(-3, subtract),  (-7, rescale), (2, multiply),
                                              (-5, weigh), (2, score), (-7, add), (0, slot_max), (6, onehot_maker(v, base)), (0, new_max), (0, max_step)])

    def project(name, inputs, source, width, outs, weights=None, store=None):
        kt = sum(w for _, w in inputs) // P
        tiles, stores = calls["tile"], calls["store"]
        chunk_base = [calls[k] for k in range(len(outs))]
        calls["tile"] += NB
        for k in range(len(outs)):
            calls[k] += NB
        if store:
            calls["store"] += NB // 2
        if source is not None:
            calls["weights"] += 16
        assert outs[-1][1] == "dve"

        def chunk_done(k, t):
            return chunk_base[k] + t.plus(1).n

        with ExitStack() as ctx:
            w = weights if weights is not None else sb(f"{name}_w", [P, kt, width], F32, ctx)
            tin = sb(f"{name}_tin", [P, 2, kt * P], F32, ctx)
            tt = sb(f"{name}_tt", [P, 2, kt * P], F32, ctx)
            with nc.Block() as block:

                @block.sync
                def _(sp):
                    if source is not None:
                        sp.dma_start(w[:, :, :], source.rearrange("(k p) n -> p k n", p=P)).then_inc(weights_loaded, 16)
                    if store is not None:
                        if stores == 0:
                            for j in range(2):
                                sp.sem_inc(stage_free[j], 16)
                        with sp.Fori(0, NB // 2) as i:
                            for j in range(2):
                                t = At(i, 2, j)
                                for k, (_, _, _, staged_out) in enumerate(outs):
                                    if staged_out:
                                        sp.wait_ge(taken[k], chunk_base[k] + t.plus(2).n)
                                sp.dma_start(store[bass.ds(i * (2 * P) + j * P, P), :], stage[:, j, 0:store.shape[1]]).then_inc(stage_free[j], 16)
                        for j in range(2):
                            sp.wait_ge(stage_free[j], 16 * (stores + NB // 2 + 1))

                def evacuate(eng, mine):
                    def body(t):
                        for k, (cols, engine, write, staged_out) in enumerate(outs):
                            if engine == mine:
                                eng.wait_ge(multiplied[k], chunk_done(k, t))
                                if staged_out:
                                    eng.wait_ge(stage_free[t.of(2)], (t.turn + stores) * 16 + 16)
                                write(eng, t, ps[:, 2 + k, 0:cols]).then_inc(taken[k], 1)
                    return body

                @block.scalar
                def _(act):
                    if tiles == 0:
                        act.sem_inc(turned_in, 2)

                    def take_in(t):
                        act.wait_ge(turned_in, tiles + t.plus(1).n)
                        c = 0
                        for take, wide in inputs:
                            ins = take(act, dyn(t), tin[:, t.of(2), c:c + wide])
                            c += wide
                        ins.then_inc(tin_ready, 1)

                    pipeline(act, NB, 2, [(1, take_in), (0, evacuate(act, "act"))])

                @block.tensor
                def _(pe):
                    if source is not None:
                        pe.wait_ge(weights_loaded, calls["weights"])

                    def turn_in(t):
                        pe.wait_ge(tin_ready, tiles + t.plus(1).n)
                        pe.wait_ge(tin_turned, tiles + t.plus(1).n)
                        for k in range(kt):
                            ins = pe.transpose(ps[:, t.of(2), k * P:(k + 1) * P], tin[:, t.of(2), k * P:(k + 1) * P], ident[:, :])
                        ins.then_inc(turned_in, 1)

                    def multiply(t):
                        pe.wait_ge(tin_turned, tiles + t.plus(3).n)
                        c = 0
                        for n, (cols, _, _, _) in enumerate(outs):
                            pe.wait_ge(taken[n], chunk_base[n] + t.plus(1).n)
                            for k in range(kt):
                                ins = pe.matmul(ps[:, 2 + n, 0:cols], tt[:, t.of(2), k * P:(k + 1) * P], w[:, k, c:c + cols],
                                                start=k == 0, stop=k == kt - 1)
                            ins.then_inc(multiplied[n], 1)
                            c += cols

                    pipeline(pe, NB, 2, [(1, turn_in), (0, multiply)])

                @block.vector
                def _(v):
                    if tiles == 0:
                        v.sem_inc(tin_turned, 2)
                    for k in range(len(outs)):
                        if chunk_base[k] == 0:
                            v.sem_inc(taken[k], 1)

                    def copy_turned(t):
                        v.wait_ge(turned_in, tiles + t.plus(3).n)
                        v.tensor_copy(tt[:, t.of(2), :], ps[:, t.of(2), 0:kt * P]).then_inc(tin_turned, 1)

                    pipeline(v, NB, 2, [(1, copy_turned), (0, evacuate(v, "dve"))])

    def flat(array, b, n=D):
        return array[:, b, 0:n].rearrange("p o c -> p (o c)")

    def plain(array):
        return lambda act, b, dest: act.copy(dest, flat(array, b, dest.shape[-1]))

    def rectified(array):
        return lambda act, b, dest: act.activation(dest, flat(array, b), ACT.Relu)

    def averaged(act, b, dest):
        return act.activation(dest, flat(acc, b), ACT.Copy, scale=small[:, 1, b])

    def copy_to_stage(c0):
        def write(eng, t, psum):
            dest = stage[:, t.of(2), c0:c0 + psum.shape[1]]
            return eng.copy(dest, psum) if eng is nc.scalar else eng.tensor_copy(dest, psum)
        return write

    def add_to(dest, other, c0=0):
        def write(eng, t, psum):
            n = psum.shape[1]
            d = dest[:, dyn(t), c0:c0 + n].rearrange("p o c -> p (o c)")
            return eng.tensor_tensor(d, psum, d if other is None else other[:, 0:n], ALU.add)
        return write

    def add_to_stage(other):
        def write(eng, t, psum):
            return eng.tensor_tensor(stage[:, t.of(2), 0:psum.shape[1]], psum, other[:, 0:psum.shape[1]], ALU.add)
        return write

    def on_all(fn):
        with nc.Block() as block:

            @block.vector
            def _(v):
                fn(chain, v)

    stage = ring[:, :, :].rearrange("p r c -> p (r c)").rearrange("p (j n) -> p j n", j=2)

    rows_written, row_stores = sem("rows_written"), [0]

    def store_rows(table, array):
        row_stores[0] += 1
        with nc.Block() as block:

            @block.sync
            def _(sp):
                sp.dma_start(rows(table), array[:, :, 0:D]).then_inc(rows_written, 16)
                sp.wait_ge(rows_written, 16 * row_stores[0])

    def relational(layer, take, source, table, own_bias):
        outs = [(2 * D, "act" if k % 2 else "dve", copy_to_stage(2 * k * D), True) for k in range(REL // 2)]
        outs.append((D, "dve", add_to(s, own_bias), False))
        project(f"rel{layer}", [(take, D)], source, (REL + 1) * D, outs, store=table.rearrange("(n r) f -> n (r f)", r=REL))

    bias = {n: biases[:, k, :] for k, n in enumerate(BIASES)}

    with ExitStack() as edges_in:
        rec_p = sb("rec_p", [P, COLS, 4], I32, edges_in)
        inspect()
        sort_edges()
    make_slots()
    layernorm("norm0", write=False)
    relational(0, lambda act, b, dest: normalised(act, dest, b), a["l0_w1"], table0, bias["l0_b1"])
    gather_sum_with_edges(table0, 0)

    def hidden0(c, v):
        c.link(v.tensor_tensor(h[:, :, :], acc[:, :, 0:D], s[:, :, :], ALU.add))
    on_all(hidden0)
    relational(1, rectified(h), a["l0_w2"], table1, bias["l0_b2"])

    with ExitStack() as network:
        hidden3 = sb("hidden3", [P, D], F32, network)

        def to_hidden(v, b, psum):
            return v.tensor_tensor(hidden3[:, :], psum, bias["l3_b1"], ALU.add)

        def take_leaky(v, b, tin):
            return v.scalar_tensor_tensor(tin[:, :], hidden3[:, :], SLOPE, hidden3[:, :], ALU.mult, ALU.max)

        def to_esum(v, b, psum):
            return v.tensor_tensor(flat(esum, b), psum, bias["l3_b2"], ALU.add)
        gather_sum(table1, 0, [(0, a["l3_w1_t"], ("act", lambda act, b, tin: act.copy(tin[:, :], flat(esum, b))), to_hidden),
                               (7, a["l3_w2_t"], ("dve", take_leaky), to_esum)])

    def residual0(c, v):
        c.link(v.tensor_tensor(s[:, :, :], acc[:, :, 0:D], s[:, :, :], ALU.add))
        c.link(v.tensor_tensor(x[:, :, :], x[:, :, :], s[:, :, :], ALU.add))
    on_all(residual0)

    layernorm("norm1", write=False)
    with ExitStack() as att:
        w_att = sb("w_att", [P, 2, 4 * DM], F32, att)
        w_n2m = sb("w_n2m", [P, D], F32, att)
        w_cat = sb("w_cat", [P, 4 * DM], F32, att)
        loaded, product = sem("att_w_loaded"), sem("att_w_product")
        with nc.Block() as block:

            @block.sync
            def _(sp):
                sp.dma_start(w_n2m[:, :], a["w_n2m"]).then_inc(loaded, 16)
                sp.dma_start(w_cat[:, :], a["w_qskv_t"]).then_inc(loaded, 16)

            @block.tensor
            def _(pe):
                pe.wait_ge(loaded, 32)
                for k in range(2):
                    pe.matmul(ps[:, k, :], w_n2m[:, k * P:(k + 1) * P], w_cat[:, :], start=True, stop=True).then_inc(product, 1)

            @block.scalar
            def _(act):
                for k in range(2):
                    act.wait_ge(product, k + 1)
                    act.copy(w_att[:, k, :], ps[:, k, :])
        project("att_in", [(lambda act, b, dest: normalised(act, dest, b), D)], None, 4 * DM,
                [(D, "dve", add_to(s, bias["l1_qs"]), False), (D, "dve", add_to_stage(bias["l1_kv"]), True)],
                weights=w_att, store=kv_table)
    attention()

    with ExitStack() as fin:
        wbeta = sb("wbeta", [P, 3 * DM], F32, fin)
        col = sb("col", [P, 4, NB], F32, fin)
        inv = sb("inv", [P, NB, HEADS], F32, fin)
        loaded, logit, sig = sem("beta_loaded"), sem("beta_logit"), sem("beta_sigmoid")
        with nc.Block() as block:

            @block.sync
            def _(sp):
                sp.dma_start(wbeta[:, :], a["wbeta"].to_broadcast([P, 3 * DM])).then_inc(loaded, 16)

            @block.scalar
            def _(act):
                act.wait_ge(logit, 1)
                act.activation(col[:, 3, :], col[:, 2, :], ACT.Sigmoid).then_inc(sig, 1)

            @block.vector
            def _(v):
                c = chain
                o, diff, xr = h[:, :, 0:DM], h[:, :, DM:D], s[:, :, DM:D]

                def over_nodes(row):
                    return row.unsqueeze(1).to_broadcast([P, NB, DM])
                heads = acc[:, :, 0:HEADS * HU].rearrange("p b (h c) -> p b h c", h=HEADS)
                c.link(v.tensor_scalar(inv[:, :, :], heads[:, :, :, HC], 1e-16, None, ALU.add))
                c.link(v.reciprocal(inv[:, :, :], inv[:, :, :]))
                for head in range(HEADS):
                    c.step(v.tensor_tensor(h[:, :, head * HC:(head + 1) * HC], heads[:, :, head, 0:HC],
                                           inv[:, :, head:head + 1].to_broadcast([P, NB, HC]), ALU.mult))
                c.after()
                c.link(v.tensor_tensor(diff, o, xr, ALU.subtract))
                v.wait_ge(loaded, 16)
                c.step(v.tensor_tensor(acc[:, :, 0:DM], o, over_nodes(wbeta[:, 0:DM]), ALU.mult))
                c.link(v.tensor_tensor(acc[:, :, DM:D], xr, over_nodes(wbeta[:, DM:2 * DM]), ALU.mult))
                c.link(v.tensor_reduce(col[:, 0, :], acc[:, :, 0:D], AX.X, ALU.add))
                c.link(v.tensor_tensor(acc[:, :, 0:DM], diff, over_nodes(wbeta[:, 2 * DM:3 * DM]), ALU.mult))
                c.link(v.tensor_reduce(col[:, 1, :], acc[:, :, 0:DM], AX.X, ALU.add))
                v.tensor_tensor(col[:, 2, :], col[:, 0, :], col[:, 1, :], ALU.add).then_inc(logit, 1)
                v.wait_ge(sig, 1)
                c.link(v.tensor_tensor(diff, diff, col[:, 3, :].unsqueeze(2).to_broadcast([P, NB, DM]), ALU.mult))
                c.link(v.tensor_tensor(o, o, diff, ALU.subtract))
    project("att_out", [(plain(h), DM)], a["w_m2n_t"], D, [(D, "dve", add_to(x, None), False)])

    layernorm("norm2")
    store_rows(h_table, h)

    def from_nodes(array):
        return "act", lambda act, b, tin: act.copy(tin[:, :], flat(array, b))

    gather_sum(h_table, 1, [(0, a["l2_w1"][D:2 * D, :], from_nodes(h),
                             lambda v, b, psum: v.tensor_tensor(flat(s, b), psum, bias["l2_b1"], ALU.add))])

    def inverse_counts(c, v):
        c.link(v.tensor_scalar(small[:, 0, :], esum[:, :, D], 1.0, None, ALU.max))
        c.link(v.reciprocal(small[:, 1, :], small[:, 0, :]))
    on_all(inverse_counts)
    project("sage0", [(averaged, D)], a["l2_w1"][0:D, :], D, [(D, "dve", add_to(s, None), False)])

    def relu_s(c, v):
        c.link(v.tensor_scalar(s[:, :, :], s[:, :, :], 0.0, None, ALU.max))
    on_all(relu_s)
    store_rows(h1_table, s)
    gather_sum(h1_table, 1, [(0, a["l2_w2"][D:2 * D, :], from_nodes(s),
                              lambda v, b, psum: v.tensor_tensor(flat(x, b), psum, flat(x, b), ALU.add))])

    def add_bias(c, v):
        c.link(v.tensor_tensor(x[:, :, :], x[:, :, :], bias["l2_b2"].unsqueeze(1).to_broadcast([P, NB, D]), ALU.add))
    on_all(add_bias)
    project("sage1", [(averaged, D)], a["l2_w2"][0:D, :], D, [(D, "dve", add_to(x, None), False)])

    layernorm("norm3")

    def finish(c, v):
        c.link(v.tensor_tensor(x[:, :, :], x[:, :, :], h[:, :, :], ALU.add))
        c.link(v.tensor_tensor(x[:, :, :], x[:, :, :], esum[:, :, 0:D], ALU.add))
    on_all(finish)

    written = sem("written")
    with nc.Block() as block:

        @block.sync
        def _(sp):
            sp.dma_start(out[0:(NB - 1) * P, :].rearrange("(b p) f -> p b f", p=P), x[:, 0:NB - 1, :]).then_inc(written, 16)
            sp.dma_start(out[(NB - 1) * P:N, :], x[0:LAST, NB - 1, :]).then_inc(written, 16)
            sp.wait_ge(written, 32)
    top.close()



def kernel(**inputs):
    import numpy as np
    from concourse import bacc
    from concourse.bass_utils import run_bass_kernel_spmd

    nc = bacc.Bacc("TRN2", target_bir_lowering=False, num_devices=1)
    arrays, args = {}, {}
    of = {k: np.asarray(v) for k, v in inputs.items()}

    def give(name, value):
        value = np.ascontiguousarray(value)
        arrays[f"in_{name}"] = value
        args[name] = nc.dram_tensor(f"in_{name}", value.shape, mybir.dt.from_np(value.dtype), kind="ExternalInput").ap()

    give("x", of["x"])
    records = np.stack([of["dst"], of["src"], of["edge_type_8"], np.zeros_like(of["dst"])], axis=1)
    padding = np.zeros((EP + 1 - E, 4), records.dtype)
    padding[:, 0] = NPAD
    give("records", np.concatenate([records, padding]))
    features = np.concatenate([of["edge_attr_64"], of["edge_attr_256"]], axis=1)
    give("edge_attrs", np.concatenate([features, np.zeros((EP - E, DR + D), features.dtype)]))
    for layer in "12":
        w = of[f"L0_gnn_W{layer}"].transpose(1, 0, 2).reshape(D, REL * D)
        give(f"l0_w{layer}", np.concatenate([w, of[f"L0_gnn_self_w{layer}"]], axis=1))
        give(f"l2_w{layer}", np.concatenate([of[f"L2_gnn_W_l{layer}"], of[f"L2_gnn_W_r{layer}"]], axis=0))
        give(f"l3_w{layer}_t", of[f"L3_gnn_W{layer}"].T)
    give("w_edge", of["L1_gnn_W_edge"])
    give("we_t", of["L1_gnn_We"].T)
    give("w_n2m", of["L1_gnn_W_n2m"])
    give("w_qskv_t", np.concatenate([of[f"L1_gnn_W{n}"].T for n in ("q", "skip", "k", "v")], axis=1))
    give("wbeta", of["L1_gnn_Wbeta"])
    give("w_m2n_t", of["L1_gnn_W_m2n"].T)
    rows = [of["L0_gnn_b1"], of["L0_gnn_b2"], np.concatenate([of["L1_gnn_bq"], of["L1_gnn_bskip"]]),
            np.concatenate([of["L1_gnn_bk"], of["L1_gnn_bv"]]), of["L2_gnn_b1"], of["L2_gnn_b2"], of["L3_gnn_b1"], of["L3_gnn_b2"]]
    give("biases", np.stack(rows).reshape(1, len(BIASES) * D))
    out = nc.dram_tensor("out", (N, D), F32, kind="ExternalOutput").ap()
    build(nc, args, out)
    r = run_bass_kernel_spmd(nc, [arrays], core_ids=[0])
    return r.results[0]["out"]
```

```python
import concourse.bass as bass
from concourse import mybir
from contextlib import ExitStack

F32 = mybir.dt.float32
BF16 = mybir.dt.bfloat16
I32 = mybir.dt.int32
ALU = mybir.AluOpType
ACT = mybir.ActivationFunctionType
AX = mybir.AxisListType

P = 128
N = 2500
E = 42500
D = 256
REL = 8
DM = 128
DR = 64
HEADS = 4
HC = DM // HEADS
NB = -(-N // P)
LAST = N - (NB - 1) * P
NPAD = NB * P
TILES = -(-E // P)
EP = TILES * P
COLS = TILES
CH = 3
TQ = TILES // CH
SLOTS = TILES + NB - 1
RING = 16
ERING = 8
GRP = 4
TURNS = SLOTS // RING
GROUPS = RING // GRP
LOG_P = P.bit_length() - 1
assert CH * TQ == TILES and TQ <= P and TURNS * RING == SLOTS
NEG = -1e30
FORGET = 4 * NEG
HU = HC + 1
WC = D + 1
SM_SCALE = float(HC) ** -0.5
BIASES = ["l0_b1", "l0_b2", "l1_qs", "l1_kv", "l2_b1", "l2_b2", "l3_b1", "l3_b2"]
EPS = 1e-5
SLOPE = 0.015


class At:

    def __init__(self, i, step, k):
        self.i, self.step, self.k = i, step, k

    @property
    def n(self):
        return self.k if self.i is None else self.i * self.step + self.k

    def of(self, ring):
        return self.k % ring

    @property
    def turn(self):
        return self.k // self.step if self.i is None else self.i + self.k // self.step

    def in_ring(self, ring):
        return self.k // ring if self.i is None else self.i * (self.step // ring) + self.k // ring

    def plus(self, d):
        return At(self.i, self.step, self.k + d)


def dyn(at):
    return bass.ds(at.n, 1)


def pipeline(eng, count, step, stages, beside=()):
    first, last = max(lead for lead, _ in stages), min(lead for lead, _ in stages)
    turns = (count - (first - last)) // step
    if beside:
        assert turns >= NB
        turns = NB
    for tick in range(-first, -last):
        for lead, body in stages:
            if 0 <= tick + lead < count:
                body(At(None, step, tick + lead))
    with eng.Fori(0, turns) as i:
        for j in range(step):
            for lead, body in stages:
                body(At(i, step, j - last + lead))
            for tick, body in beside:
                if tick == j:
                    body(i)
    for tick in range(turns * step - last, count - last):
        for lead, body in stages:
            if 0 <= tick + lead < count:
                body(At(None, step, tick + lead))


class Chain:

    def __init__(self, eng, sem):
        self.eng, self.sem, self.count, self.loop = eng, sem, 0, None

    def after(self):
        if self.loop is None:
            self.eng.wait_ge(self.sem, self.count)
        else:
            i, per = self.loop
            self.eng.wait_ge(self.sem, i * per + self.count)

    def step(self, ins):
        ins.then_inc(self.sem, 1)
        self.count += 1

    def link(self, ins):
        self.step(ins)
        self.after()

    def run(self, times, per, body):
        start = self.count
        with self.eng.Fori(0, times) as i:
            self.loop = (i, per)
            body(i)
        assert self.count == start + per, (self.count - start, per)
        self.loop, self.count = None, start + per * times


def build(nc, a, out):
    top = ExitStack()

    def sb(name, shape, dt=F32, ctx=top):
        return ctx.enter_context(nc.sbuf_tensor(name, shape, dt))

    def sem(name):
        return top.enter_context(nc.semaphore(name))

    def dram(name, shape):
        return nc.dram_tensor(name, shape, F32, kind="Internal").ap()

    x = sb("x", [P, NB, D])
    h = sb("h", [P, NB, D])
    s = sb("s", [P, NB, D])
    sums = sb("sums", [P, NB, 2 * D])
    acc, esum = sums[:, :, 0:D], sums[:, :, D:]
    degree = sb("degree", [P, NB])
    ring = sb("ring", [P, RING, D])
    index = sb("index", [P, 2, SLOTS + RING])
    local = sb("local", [P, SLOTS])
    tile_rows = sb("tile_rows", [1, SLOTS], I32)
    unsorted = sb("unsorted", [1, 1], I32)
    ones = sb("ones", [P, P])
    iota_s = sb("iota_s", [P, SLOTS])
    iota_t = sb("iota_t", [P, CH])
    blocks = sb("blocks", [1, SLOTS], I32)
    keep = sb("keep", [P, SLOTS])
    forget = sb("forget", [P, SLOTS])
    now = sb("now", [P, 4, 2 * D])
    cur = sb("cur", [P, RING], I32)
    onehot = sb("onehot", [P, RING, P])
    ident = sb("ident", [P, P])
    identb = sb("identb", [P, P], BF16)
    iota = sb("iota", [P, P])
    biases = sb("biases", [P, len(BIASES), D])
    small = sb("small", [P, 4, NB])
    ps = top.enter_context(nc.psum_tensor("ps", [P, 8, 512], F32))

    records = nc.dram_tensor("records", (EP, 4), I32, kind="Internal").ap()
    edge_sorted = dram("edge_sorted", (EP, DR + D))
    table0 = dram("table0", (NPAD * REL, D))
    table1 = dram("table1", (NPAD * REL, D))
    kv_table = dram("kv_table", (NPAD, 2 * DM))
    h_table = dram("h_table", (NPAD, D))
    h1_table = dram("h1_table", (NPAD, D))
    e_store = dram("e_store", (SLOTS // GRP * P, GRP * DM))

    chain = Chain(nc.vector, sem("vector_chain"))
    got = [sem(f"got{j}") for j in range(RING)]
    hot, summed, added, collected = sem("onehot_ready"), sem("slot_summed"), sem("sum_added"), sem("sum_collected")
    staged, gather_tick = sem("indices_staged"), sem("gather_tick")
    BANKS = 4
    slots_done = [0]

    def rows(table):
        return table.rearrange("(b p) f -> p b f", p=P)

    def inspect():
        with ExitStack() as ctx:
            first_next = sb("first_next", [P, 4], I32, ctx)
            block_of = sb("block_of", [P, COLS + 1], I32, ctx)
            block_f = sb("block_f", [P, COLS + 1], F32, ctx)
            breaks = sb("breaks", [P, COLS], F32, ctx)
            count = sb("count", [P, 1], F32, ctx)
            loaded, filled, iotas, x_cleared, x_loaded = (
                sem(f"in_{n}") for n in ("loaded", "filled", "iotas", "x_cleared", "x_loaded"))
            counted, total = sem("breaks_counted"), sem("breaks_total")
            with nc.Block() as block:

                @block.sync
                def _(sp):
                    sp.dma_start(rec_p[:, :, :].rearrange("p t c -> p (t c)"),
                                 a["records"][0:EP, :].rearrange("(p t) c -> p (t c)", p=P)).then_inc(loaded, 16)
                    sp.dma_start(first_next[:, :], a["records"][COLS:EP + 1:COLS, :]).then_inc(loaded, 16)
                    sp.wait_ge(x_cleared, 1)
                    sp.dma_start(x[:, 0:NB - 1, :], a["x"][0:(NB - 1) * P, :].rearrange("(b p) f -> p b f", p=P)).then_inc(x_loaded, 16)
                    sp.dma_start(x[0:LAST, NB - 1, :], a["x"][(NB - 1) * P:N, :]).then_inc(x_loaded, 16)
                    sp.dma_start(biases[:, :, :].rearrange("p k c -> p (k c)"), a["biases"].to_broadcast([P, len(BIASES) * D])).then_inc(x_loaded, 16)
                    load_weights(sp, w_rel, a["l0_w1"])
                    sp.wait_ge(x_loaded, 48)

                @block.gpsimd
                def _(pool):
                    pool.memset(x[:, NB - 1, :], 0.0).then_inc(x_cleared, 1)
                    pool.memset(ones[:, :], 1.0).then_inc(filled, 1)
                    pool.memset(ident[:, :], 1.0).then_inc(filled, 1)
                    pool.wait_ge(filled, 2)
                    pool.affine_select(out=ident[:, :], in_=ident[:, :], pattern=[[1, P]], compare_op=ALU.is_equal,
                                       fill=0.0, base=0, channel_multiplier=-1).then_inc(filled, 1)
                    pool.iota(iota[:, :], [[1, P]], 0, 0, allow_small_or_imprecise_dtypes=True).then_inc(iotas, 1)
                    pool.iota(iota_s[:, :], [[1, SLOTS]], 0, 0, allow_small_or_imprecise_dtypes=True).then_inc(iotas, 1)
                    pool.iota(iota_t[:, :], [[TQ, CH]], 0, 1, allow_small_or_imprecise_dtypes=True).then_inc(iotas, 1)

                @block.tensor
                def _(pe):
                    pe.wait_ge(filled, 3)
                    pe.wait_ge(counted, 1)
                    pe.matmul(ps[:, 0, 0:1], ones[:, :], count[:, :], start=True, stop=True).then_inc(total, 1)

                @block.vector
                def _(v):
                    c = chain
                    v.wait_ge(filled, 3)
                    c.step(v.tensor_copy(identb[:, :], ident[:, :]))
                    c.step(v.memset(index[:, :, SLOTS:], 0.0))
                    v.wait_ge(loaded, 32)
                    c.step(v.tensor_scalar(block_of[:, 0:COLS], rec_p[:, :, 0], LOG_P, None, ALU.logical_shift_right))
                    c.link(v.tensor_scalar(block_of[:, COLS:], first_next[:, 0:1], LOG_P, None, ALU.logical_shift_right))
                    c.link(v.tensor_copy(block_f[:, :], block_of[:, :]))
                    c.link(v.tensor_tensor(breaks[:, :], block_f[:, 0:COLS], block_f[:, 1:], ALU.is_gt))
                    v.tensor_reduce(count[:, :], breaks[:, :], AX.X, ALU.add).then_inc(counted, 1)
                    v.wait_ge(total, 1)
                    c.step(v.tensor_scalar(unsorted[:, :], ps[0:1, 0, 0:1], 1.0, None, ALU.min))

    def sort_edges():
        RB = next(k for k in (3, 2, 1) if COLS % k == 0)
        BUCKETS = NB + 1
        with ExitStack() as ctx:
            block_of = sb("block_of2", [P, COLS], I32, ctx)
            block_f = sb("block_f2", [P, COLS], F32, ctx)
            hit, run, tmp, place, every = (sb(n, [P, COLS], F32, ctx) for n in ("hit", "run", "tmp", "place", "every"))
            tri = sb("tri", [P, P], F32, ctx)
            tot = sb("tot", [P, BUCKETS], F32, ctx)
            ends = sb("ends", [P, BUCKETS], F32, ctx)
            base = sb("base", [P, BUCKETS], F32, ctx)
            attr = sb("attr", [P, RB, DR + D], F32, ctx)
            rec = sb("rec", [P, RB, 4], I32, ctx)
            copied, tri_ready, totals_ready, prefix_ready, places_ready, rec_staged, tick = (
                sem(f"sort_{n}") for n in ("copied", "tri", "totals", "prefix", "places", "staged", "tick"))
            attr_loaded = [sem(f"sort_attr{j}") for j in range(RB)]
            rec_out = [sem(f"sort_rec_out{j}") for j in range(RB)]
            attr_out = [sem(f"sort_attr_out{j}") for j in range(RB)]
            chain_sem = sem("sort_chain")

            def is_unsorted(eng):
                return eng.value_load(unsorted[0:1, 0:1], min_val=0, max_val=1)

            with nc.Block() as block:

                @block.sync
                def _(sp):
                    flag = is_unsorted(sp)
                    with sp.If(flag < 1):
                        sp.dma_start(records.rearrange("(p t) c -> p (t c)", p=P),
                                     a["records"][0:EP, :].rearrange("(p t) c -> p (t c)", p=P)).then_inc(copied, 16)
                        sp.wait_ge(copied, 16)
                    with sp.If(flag > 0):
                        columns = a["edge_attrs"].rearrange("(p t) f -> p t f", p=P)
                        for j in range(RB):
                            sp.dma_start(attr[:, j, :], columns[:, j, :]).then_inc(attr_loaded[j], 16)
                        with sp.Fori(1, COLS // RB) as i:
                            for j in range(RB):
                                sp.wait_ge(attr_out[j], i * 16)
                                sp.dma_start(attr[:, j:j + 1, :], columns[:, bass.ds(i * RB + j, 1), :]).then_inc(attr_loaded[j], 16)
                        for j in range(RB):
                            sp.wait_ge(attr_out[j], 16 * (COLS // RB))
                            sp.wait_ge(rec_out[j], 16 * (COLS // RB))

                @block.gpsimd
                def _(pool):
                    flag = is_unsorted(pool)
                    with pool.If(flag > 0):
                        pool.affine_select(out=tri[:, :], in_=ones[:, :], pattern=[[1, P]], compare_op=ALU.is_gt,
                                           fill=0.0, base=0, channel_multiplier=-1).then_inc(tri_ready, 1)
                        with pool.Fori(0, COLS // RB) as i:
                            for j in range(RB):
                                pool.wait_ge(rec_staged, (i * RB + j + 1) * 2)
                                pool.sem_inc(tick, 1)
                                pool.wait_ge(attr_loaded[j], i * 16 + 16)
                                pool.sem_inc(tick, 1)
                                where = bass.IndirectOffsetOnAxis(ap=cur[:, j:j + 1], axis=0)
                                pool.indirect_dma_start(records, where, rec[:, j, :], None).then_inc(rec_out[j], 16)
                                pool.indirect_dma_start(edge_sorted, where, attr[:, j, :], None).then_inc(attr_out[j], 16)

                @block.scalar
                def _(act):
                    flag = is_unsorted(act)
                    with act.If(flag > 0):
                        act.wait_ge(places_ready, 1)

                        def stage(at, j):
                            act.copy(cur[:, j:j + 1], place[:, at]).then_inc(rec_staged, 1)
                            act.copy(rec[:, j:j + 1, :], rec_p[:, at, :]).then_inc(rec_staged, 1)

                        for j in range(RB):
                            stage(slice(j, j + 1), j)
                        with act.Fori(1, COLS // RB) as i:
                            for j in range(RB):
                                act.wait_ge(rec_out[j], i * 16)
                                act.wait_ge(attr_out[j], i * 16)
                                stage(bass.ds(i * RB + j, 1), j)

                @block.tensor
                def _(pe):
                    flag = is_unsorted(pe)
                    with pe.If(flag > 0):
                        pe.wait_ge(tri_ready, 1)
                        pe.wait_ge(totals_ready, 1)
                        pe.matmul(ps[:, 0, 0:BUCKETS], tri[:, :], tot[:, :], start=True, stop=True).then_inc(prefix_ready, 1)
                        pe.matmul(ps[:, 1, 0:BUCKETS], ones[:, :], tot[:, :], start=True, stop=True).then_inc(prefix_ready, 1)

                @block.vector
                def _(v):
                    flag = is_unsorted(v)
                    with v.If(flag > 0):
                        c = Chain(v, chain_sem)
                        c.step(v.memset(place[:, :], 0.0))
                        c.step(v.memset(every[:, :], 1.0))
                        c.link(v.tensor_scalar(block_of[:, :], rec_p[:, :, 0], LOG_P, None, ALU.logical_shift_right))
                        c.link(v.tensor_copy(block_f[:, :], block_of[:, :]))

                        def ranks(i):
                            col = bass.ds(i, 1)
                            c.link(v.tensor_scalar(hit[:, :], block_f[:, :], iota[:, col], None, ALU.is_equal))
                            c.link(v.tensor_tensor_scan(run[:, :], every[:, :], hit[:, :], 0.0, ALU.mult, ALU.add))
                            c.step(v.tensor_copy(tot[:, col], run[:, COLS - 1:COLS]))
                            c.link(v.tensor_tensor(tmp[:, :], run[:, :], hit[:, :], ALU.mult))
                            c.link(v.tensor_tensor(place[:, :], place[:, :], tmp[:, :], ALU.add))

                        c.run(BUCKETS, 5, ranks)
                        v.tensor_copy(tmp[:, 0:1], tot[:, 0:1]).then_inc(totals_ready, 1)
                        v.wait_ge(prefix_ready, 2)
                        c.link(v.tensor_copy(base[:, :], ps[:, 1, 0:BUCKETS]))
                        c.link(v.tensor_tensor_scan(ends[:, :], every[:, 0:BUCKETS], base[:, :], -1.0, ALU.mult, ALU.add))
                        c.link(v.tensor_tensor(base[:, :], ends[:, :], base[:, :], ALU.subtract))
                        c.link(v.tensor_tensor(base[:, :], base[:, :], ps[:, 0, 0:BUCKETS], ALU.add))

                        def places(i):
                            col = bass.ds(i, 1)
                            c.link(v.tensor_scalar(hit[:, :], block_f[:, :], iota[:, col], base[:, col], ALU.is_equal, ALU.mult))
                            c.link(v.tensor_tensor(place[:, :], place[:, :], hit[:, :], ALU.add))

                        c.run(BUCKETS, 2, places)
                        v.tensor_copy(tmp[:, 0:1], place[:, 0:1]).then_inc(places_ready, 1)

    def make_slots():
        with ExitStack() as ctx:
            rt = sb("rt", [TQ, CH, P, 4], I32, ctx)
            first = sb("first", [TQ, CH], I32, ctx)
            start = sb("start", [TQ, CH], F32, ctx)
            fields = sb("fields", [TQ, 3, CH, P], F32, ctx)
            typ = sb("typ", [TQ, CH, P], F32, ctx)
            begun = sb("begun", [TQ, CH, SLOTS], F32, ctx)
            pick = sb("pick", [TQ, CH, SLOTS], F32, ctx)
            tile = sb("tile", [P, SLOTS], F32, ctx)
            block_f = sb("block_s", [P, SLOTS], F32, ctx)
            loaded, begun_ready, tiles_ready, pick_ready, picked = (
                sem(f"slots_{n}") for n in ("loaded", "begun", "tiles", "pick", "picked"))
            with nc.Block() as block:

                @block.sync
                def _(sp):
                    sp.dma_start(rt[:, :, :, :].rearrange("q c p f -> q c (p f)"),
                                 records.rearrange("(c q p) f -> q c (p f)", c=CH, q=TQ)).then_inc(loaded, 16)

                @block.tensor
                def _(pe):
                    pe.wait_ge(begun_ready, 1)
                    for c in range(CH):
                        ins = pe.matmul(ps[:, 0, 0:SLOTS], ones[0:TQ, :], begun[:, c, :], start=c == 0, stop=c == CH - 1)
                    ins.then_inc(tiles_ready, 1)
                    pe.wait_ge(pick_ready, 1)
                    for k in range(3):
                        for c in range(CH):
                            ins = pe.matmul(ps[:, 1 + k, 0:SLOTS], fields[:, k, c, :], pick[:, c, :], start=c == 0, stop=c == CH - 1)
                        ins.then_inc(picked, 1)

                @block.vector
                def _(v):
                    c = chain
                    v.wait_ge(loaded, 16)
                    c.link(v.tensor_scalar(first[:, :], rt[:, :, 0, 0], LOG_P, None, ALU.logical_shift_right))
                    c.link(v.tensor_copy(start[:, :], first[:, :]))
                    c.link(v.tensor_scalar(start[:, :], start[:, :], float(NB - 1), None, ALU.min))
                    c.link(v.tensor_tensor(start[:, :], start[:, :], iota_t[0:TQ, :], ALU.add))
                    c.link(v.memset(start[0:1, 0:1], 1e9))
                    for k in range(CH):
                        ins = v.tensor_scalar(begun[:, k, :], iota_s[0:TQ, :], start[:, k:k + 1], None, ALU.is_ge)
                        c.step(ins) if k < CH - 1 else ins.then_inc(begun_ready, 1)
                    c.step(v.tensor_copy(fields[:, 1, :, :], rt[:, :, :, 1]))
                    c.step(v.tensor_copy(fields[:, 2, :, :], rt[:, :, :, 0]))
                    c.link(v.tensor_copy(typ[:, :, :], rt[:, :, :, 2]))
                    c.step(v.scalar_tensor_tensor(fields[:, 0, :, :].rearrange("q c p -> q (c p)"),
                                                  fields[:, 1, :, :].rearrange("q c p -> q (c p)"), float(REL),
                                                  typ[:, :, :].rearrange("q c p -> q (c p)"), ALU.mult, ALU.add))
                    v.wait_ge(tiles_ready, 1)
                    c.link(v.tensor_copy(tile[:, :], ps[:, 0, 0:SLOTS]))
                    for k in range(CH):
                        ins = v.tensor_scalar(pick[:, k, :], tile[0:TQ, :], iota_t[0:TQ, k:k + 1], None, ALU.is_equal)
                        c.step(ins) if k < CH - 1 else ins.then_inc(pick_ready, 1)
                    c.link(v.tensor_tensor(block_f[:, :], iota_s[:, :], tile[:, :], ALU.subtract))
                    c.step(v.tensor_copy(blocks[:, :], block_f[0:1, :]))
                    c.step(v.tensor_scalar(tile_rows[:, :], tile[0:1, :], float(P), None, ALU.mult))
                    c.step(v.memset(keep[:, 0:1], 0.0))
                    c.link(v.tensor_tensor(keep[:, 1:], block_f[:, 1:], block_f[:, 0:SLOTS - 1], ALU.is_equal))
                    c.step(v.tensor_scalar(forget[:, :], keep[:, :], 1.0, -FORGET, ALU.subtract, ALU.mult))
                    v.wait_ge(picked, 3)
                    c.step(v.tensor_copy(index[:, 0, 0:SLOTS], ps[:, 1, 0:SLOTS]))
                    c.step(v.tensor_copy(index[:, 1, 0:SLOTS], ps[:, 2, 0:SLOTS]))
                    c.step(v.scalar_tensor_tensor(local[:, :], block_f[:, :], -float(P), ps[:, 3, 0:SLOTS], ALU.mult, ALU.add))

    var_ready, std_ready, scale_ready = sem("var_ready"), sem("std_ready"), sem("scale_ready")
    norms = [0]
    stats = sb("stats", [P, NB, 6])
    x_measured, measured_tiles = sem("x_measured"), [0]
    normed, norm_tiles = sem("normed"), [0]

    def normalised(act, dest, b):
        return act.activation(dest, x[:, b, :].rearrange("p o c -> p (o c)"), ACT.Relu, bias=small[:, 3, b], scale=small[:, 2, b])

    def layernorm(name, write=True, measured=False, meanwhile=None, outputs=None):
        with ExitStack() as ctx:
            mv = sb(f"{name}_mv", [P, NB, 2], F32, ctx)
            norms[0] += 1
            nth = norms[0]
            with nc.Block() as block:

                @block.vector
                def _(v):
                    c = chain

                    if measured:
                        v.wait_ge(x_measured, measured_tiles[0])
                    else:
                        for b in range(NB):
                            c.step(v.bn_stats(stats[:, b, :], x[:, b, :]))
                        c.after()
                    for b in range(NB):
                        c.step(v.bn_aggr(mv[:, b, :], stats[:, b, :]))
                    c.after()
                    v.tensor_scalar(small[:, 0, :], mv[:, :, 1], EPS, None, ALU.add).then_inc(var_ready, 1)
                    v.wait_ge(std_ready, nth)
                    c.link(v.reciprocal(small[:, 2, :], small[:, 1, :]))
                    v.scalar_tensor_tensor(small[:, 3, :], mv[:, :, 0], -1.0, small[:, 2, :], ALU.mult, ALU.mult).then_inc(scale_ready, 1)
                    if meanwhile is not None:
                        meanwhile(v)

                @block.scalar
                def _(act):
                    act.wait_ge(var_ready, nth)
                    act.activation(small[:, 1, :], small[:, 0, :], ACT.Sqrt).then_inc(std_ready, 1)
                    if write:
                        act.wait_ge(scale_ready, nth)
                        for b in range(NB):
                            act.activation(h[:, b, :], x[:, b, :], ACT.Relu, bias=small[:, 3, b:b + 1],
                                           scale=small[:, 2, b:b + 1]).then_inc(normed, 1)
                        norm_tiles[0] += NB

                if outputs is not None:
                    @block.sync
                    def _(sp):
                        outputs(sp)

    def gather_rows(pool, table, first_turn):
        with pool.Fori(0, SLOTS // RING) as i:
            for g in range(GROUPS):
                pool.wait_ge(staged, i * GROUPS + (first_turn // TURNS * (TURNS + 1) * GROUPS + g + 1))
                pool.sem_inc(gather_tick, 1)
                for j in range(g * GRP, (g + 1) * GRP):
                    pool.indirect_dma_start(ring[:, j, 0:table.shape[1]], None, table,
                                            bass.IndirectOffsetOnAxis(ap=cur[:, j:j + 1], axis=0)).then_inc(got[j], 16)

    def index_stager(act, column, used, base):
        for g in range(GROUPS):
            act.copy(cur[:, g * GRP:(g + 1) * GRP], index[:, column, g * GRP:(g + 1) * GRP]).then_inc(staged, 1)

        def stage(t):
            if t.k % GRP == GRP - 1:
                act.wait_ge(used, base + t.plus(1).n)
                g = t.of(RING) // GRP
                act.copy(cur[:, g * GRP:(g + 1) * GRP],
                         index[:, column, bass.ds(t.plus(RING - GRP + 1).n, GRP)]).then_inc(staged, 1)
        return stage

    def slot_block(eng, t):
        return bass.ds(eng.value_load(blocks[0:1, dyn(t)]), 1)

    def onehot_maker(v, base):
        def make_onehot(t):
            v.tensor_scalar(onehot[:, t.of(RING), :], iota[:, :], local[:, dyn(t)], None, ALU.is_equal).then_inc(hot, 1)
        return make_onehot

    def slot_summer(pe, base, turn, more=None):
        def sum_slot(t):
            pe.wait_ge(got[t.of(RING)], (t.turn + turn) * 16 + 16)
            pe.wait_ge(hot, base + t.plus(1).n)
            pe.wait_ge(added, base + t.plus(1).n)
            columns = [(0, ring[:, t.of(RING), 0:D])]
            if more is not None:
                columns.append((D, more(t)))
            for c, values in columns:
                ins = pe.matmul(ps[:, t.of(BANKS), c:c + values.shape[-1]], onehot[:, t.of(RING), :], values, start=True, stop=True)
            ins.then_inc(summed, 1)
        return sum_slot

    def slot_adder(v, base, width):
        def add_slot(t):
            v.wait_ge(summed, base + t.plus(1).n)
            v.wait_ge(added, base + t.plus(BANKS).n)
            v.wait_ge(collected, base + t.plus(1).n)
            v.scalar_tensor_tensor(now[:, t.of(4), 0:width], now[:, (t.k - 1) % 4, 0:width], keep[:, dyn(t)],
                                   ps[:, t.of(BANKS), 0:width], ALU.mult, ALU.add).then_inc(added, 1)
        return add_slot

    def slot_collector(act, base, into, width):
        def collect(t):
            block = slot_block(act, t)
            act.wait_ge(added, base + t.plus(BANKS + 1).n)
            act.wait_ge(collected, base + t.plus(4).n)
            act.copy(into[:, block, 0:width], now[:, t.of(4):t.of(4) + 1, 0:width]).then_inc(collected, 1)
        return collect

    def clear_sums(v, base, into, width, cleared, count=2):
        if base == 0:
            v.sem_inc(added, BANKS)
            v.sem_inc(collected, 4)
        v.memset(now[:, 3, 0:width], 0.0).then_inc(cleared, 1)
        v.memset(into[:, :, 0:width], 0.0).then_inc(cleared, 1)
        v.wait_ge(cleared, count)

    tin_ready, turned_in, tin_turned = sem("tin_ready"), sem("tin_turned"), sem("turned_copied")
    multiplied = [sem(f"multiplied{k}") for k in range(5)]
    taken = [sem(f"taken{k}") for k in range(5)]
    stage_free = [sem(f"stage_free{j}") for j in range(2)]
    weights_loaded = sem("weights_loaded")
    calls = {"weights": 0, "tile": 0, "store": 0, **{k: 0 for k in range(6)}}

    def load_weights(sp, dest, source):
        calls["weights"] += 16
        sp.dma_start(dest[:, :, :], source.rearrange("(k p) n -> p k n", p=P)).then_inc(weights_loaded, 16)

    def node_products(ctx, products):
        if not products:
            return (lambda sp: None), (), ()
        each, tiles, base = len(products), calls["tile"], calls[0]
        calls["tile"] += NB * each
        calls[0] += NB * each
        weights = [sb(f"beside{tiles}_w{q}", [P, 2, D], F32, ctx) for q in range(each)]
        tin = sb(f"beside{tiles}_tin", [P, D], F32, ctx)
        tt = sb(f"beside{tiles}_tt", [P, D], F32, ctx)
        turned_bank, product_bank = 4, 5
        work = {"pe": [], "dve": []}

        def load(sp):
            for q, (_, source, _, _) in enumerate(products):
                load_weights(sp, weights[q], source)

        def add_product(q, first, take, write):
            def before(i):
                return i * each + q

            def take_in(i):
                nc.vector.wait_ge(turned_in, before(i) + (tiles + 2))
                nc.vector.wait_ge(taken[0], before(i) + (base + 1))
                take(nc.vector, bass.ds(i, 1), tin).then_inc(tin_ready, 1)

            def turn_in(i):
                nc.tensor.wait_ge(tin_ready, before(i) + (tiles + 1))
                nc.tensor.wait_ge(tin_turned, before(i) + (tiles + 2))
                for k in range(2):
                    ins = nc.tensor.transpose(ps[:, turned_bank, k * P:(k + 1) * P], tin[:, k * P:(k + 1) * P], ident[:, :])
                ins.then_inc(turned_in, 1)

            def copy_turned(i):
                nc.vector.wait_ge(turned_in, before(i) + (tiles + 3))
                nc.vector.tensor_copy(tt[:, :], ps[:, turned_bank, 0:D]).then_inc(tin_turned, 1)

            def multiply(i):
                nc.tensor.wait_ge(weights_loaded, calls["weights"])
                nc.tensor.wait_ge(tin_turned, before(i) + (tiles + 3))
                nc.tensor.wait_ge(taken[0], before(i) + (base + 1))
                for k in range(2):
                    ins = nc.tensor.matmul(ps[:, product_bank, 0:D], tt[:, k * P:(k + 1) * P], weights[q][:, k, :],
                                           start=k == 0, stop=k == 1)
                ins.then_inc(multiplied[0], 1)

            def use_product(i):
                nc.vector.wait_ge(multiplied[0], before(i) + (base + 1))
                write(nc.vector, bass.ds(i, 1), ps[:, product_bank, 0:D]).then_inc(taken[0], 1)

            work["pe"] += [(first + 1, turn_in), (first + 4, multiply)]
            work["dve"] += [(first, take_in), (first + 3, copy_turned), (first + 7, use_product)]

        for q, (first, _, take, write) in enumerate(products):
            add_product(q, first, take, write)
        return load, work["pe"], work["dve"]

    gather_cleared, clearings = sem("gather_cleared"), [0]

    edge_in, tiles_loaded = [sem(f"edge_in{j}") for j in range(ERING)], [0]

    def load_tiles(sp, columns, buffer, used, base):
        flag = sp.value_load(unsorted[0:1, 0:1], min_val=0, max_val=1)

        def load_from(source):
            def load(t, wait):
                row = sp.value_load(tile_rows[0:1, dyn(t)])
                if wait and t.k % GRP == 0:
                    sp.wait_ge(used, base + t.plus(GRP - ERING).n)
                sp.dma_start(buffer[:, t.of(ERING), :], source[bass.ds(row, P), columns]).then_inc(edge_in[t.of(ERING)], 16)

            for j in range(ERING):
                load(At(None, ERING, j), False)
            with sp.Fori(1, SLOTS // ERING) as i:
                for j in range(ERING):
                    load(At(i, ERING, j), True)

        with sp.If(flag < 1):
            load_from(a["edge_attrs"])
        with sp.If(flag > 0):
            load_from(edge_sorted)

    def gather_sum(table, column, products=(), with_edges=False, loads=()):
        width = 2 * D if with_edges else D
        turn, base = slots_done[0] // RING, slots_done[0]
        slots_done[0] += SLOTS
        clearings[0] += 2
        with ExitStack() as ctx:
            load, pe_work, v_work = node_products(ctx, products)
            features = sb("features", [P, ERING, D], F32, ctx) if with_edges else None
            before = tiles_loaded[0] * 16
            tiles_loaded[0] += SLOTS // ERING if with_edges else 0

            def edge_features(t):
                nc.tensor.wait_ge(edge_in[t.of(ERING)], t.in_ring(ERING) * 16 + (before + 16))
                return features[:, t.of(ERING), :]

            with nc.Block() as block:

                @block.sync
                def _(sp):
                    load(sp)
                    for dest, source in loads:
                        load_weights(sp, dest, source)
                    if with_edges:
                        load_tiles(sp, slice(DR, DR + D), features, summed, base)

                @block.gpsimd
                def _(pool):
                    gather_rows(pool, table, turn)

                @block.scalar
                def _(act):
                    stager = index_stager(act, column, summed, base)
                    act.wait_ge(gather_cleared, clearings[0])
                    pipeline(act, SLOTS, RING, [(0, stager), (-1, slot_collector(act, base, sums, width))])

                @block.tensor
                def _(pe):
                    pipeline(pe, SLOTS, RING, [(0, slot_summer(pe, base, turn, edge_features if with_edges else None))], pe_work)

                @block.vector
                def _(v):
                    clear_sums(v, base, sums, width, gather_cleared, clearings[0])
                    pipeline(v, SLOTS, RING, [(2, onehot_maker(v, base)), (0, slot_adder(v, base, width))], v_work)

    def gather_sum_and_project_edges(table, column):
        turn, base = slots_done[0] // RING, slots_done[0]
        slots_done[0] += SLOTS
        tiles_loaded[0] += SLOTS // ERING
        cleared, loaded, turned, copied, projected, kept, w_product, w_ready = (
            sem(f"edge_{n}") for n in ("cleared", "w_loaded", "turned", "turned_copied", "projected", "kept", "w_product", "w_ready"))
        stored = [sem(f"edge_stored{g}") for g in range(2)]
        with ExitStack() as ctx:
            w_edge = sb("w_edge", [DR, DR], F32, ctx)
            we_t = sb("we_t", [DR, DM], F32, ctx)
            w_e = sb("w_e", [DR, DM], F32, ctx)
            radial = sb("radial", [P, ERING, P], F32, ctx)
            attr_t = sb("attr_t", [DR, 4, P], F32, ctx)
            e_out = sb("e_out", [P, 2, 2, GRP * DM], F32, ctx)

            PAIR = 2 * GRP

            def pair_rows(t):
                first = t.i * (RING // GRP * P) + t.k // PAIR * 2 * P if t.i is not None else t.k // PAIR * 2 * P
                return bass.ds(first, 2 * P)

            with nc.Block() as block:

                @block.sync
                def _(sp):
                    sp.dma_start(w_edge[:, :], a["w_edge"]).then_inc(loaded, 16)
                    sp.dma_start(we_t[:, :], a["we_t"]).then_inc(loaded, 16)
                    load_weights(sp, w_rel, a["l0_w2"])
                    load_tiles(sp, slice(0, P), radial, turned, 0)

                @block.gpsimd
                def _(pool):
                    gather_rows(pool, table, turn)

                @block.tensor
                def _(pe):
                    pe.wait_ge(loaded, 32)
                    pe.matmul(ps[0:DR, 7, 0:DM], w_edge[:, :], we_t[:, :], start=True, stop=True).then_inc(w_product, 1)
                    pe.wait_ge(w_ready, 1)

                    def turn_attr(t):
                        pe.wait_ge(edge_in[t.of(ERING)], t.in_ring(ERING) * 16 + 16)
                        pe.wait_ge(copied, t.plus(1).n)
                        pe.transpose(ps[:, 4 + t.of(2), 0:P], radial[:, t.of(ERING), :], ident[:, :]).then_inc(turned, 1)

                    def project_attr(t):
                        pe.wait_ge(copied, t.plus(3).n)
                        pe.wait_ge(kept, t.plus(1).n)
                        pe.matmul(ps[:, 6 + t.of(2), 0:DM], attr_t[:, t.of(4), :], w_e[:, :],
                                  start=True, stop=True).then_inc(projected, 1)

                    pipeline(pe, SLOTS, RING, [(2, turn_attr), (0, project_attr),
                                               (0, slot_summer(pe, base, turn, lambda t: ones[:, 0:1]))])

                @block.scalar
                def _(act):
                    act.wait_ge(w_product, 1)
                    act.copy(w_e[:, :], ps[0:DR, 7, 0:DM]).then_inc(w_ready, 1)
                    stager = index_stager(act, column, summed, base)
                    act.wait_ge(cleared, 2)
                    for g in range(2):
                        act.sem_inc(stored[g], 16)

                    def store(t):
                        if t.k % PAIR == PAIR - 1:
                            g = t.k // PAIR % 2
                            act.wait_ge(kept, t.plus(3).n)
                            act.dma_start(e_store[pair_rows(t), :].rearrange("(g p) n -> p g n", g=2), e_out[:, g, :, :]).then_inc(stored[g], 16)

                    pipeline(act, SLOTS, RING, [(0, stager), (0, store), (-1, slot_collector(act, base, sums, WC))])
                    for g in range(2):
                        act.wait_ge(stored[g], 16 * (SLOTS // PAIR // 2 + 1))

                @block.vector
                def _(v):
                    clear_sums(v, base, sums, WC, cleared)
                    v.sem_inc(copied, 2)
                    v.sem_inc(kept, 2)

                    def copy_turned(t):
                        v.wait_ge(turned, t.plus(1).n)
                        v.tensor_copy(attr_t[:, t.of(4), :], ps[0:DR, 4 + t.of(2), 0:P]).then_inc(copied, 1)

                    def keep_projected(t):
                        v.wait_ge(projected, t.plus(1).n)
                        if t.k % PAIR == 0:
                            v.wait_ge(stored[t.k // PAIR % 2], t.in_ring(2 * PAIR) * 16 + 16)
                        v.tensor_copy(e_out[:, t.k // PAIR % 2, t.k // GRP % 2, t.of(GRP) * DM:(t.of(GRP) + 1) * DM],
                                      ps[:, 6 + t.of(2), 0:DM]).then_inc(kept, 1)

                    pipeline(v, SLOTS, RING, [(2, onehot_maker(v, base)), (2, copy_turned), (0, keep_projected),
                                              (0, slot_adder(v, base, WC))])

    def attention():
        turn, base = slots_done[0] // RING, slots_done[0]
        slots_done[0] += SLOTS
        (cleared, turned, ot_ready, pen_ready, qx_ready, kve_ready, prod_ready, alpha_ready, scored, mx_ready,
         mnew_ready, md_ready, r_ready, me_ready, ad_ready, p_ready, msg_ready, scaled) = (
            sem(f"att_{n}") for n in ("cleared", "turned", "ot", "pen", "qx", "kve", "prod", "alpha", "scored", "mx",
                                      "mnew", "md", "r", "me", "ad", "p", "msg", "scaled"))
        e_got = [sem(f"att_e{g}") for g in range(GROUPS)]
        with ExitStack() as ctx:
            e_in = sb("e_in", [P, GROUPS, GRP, DM], F32, ctx)
            onehot_t = sb("onehot_t", [P, 8, P], F32, ctx)
            penalty = sb("penalty", [P, 8, P], BF16, ctx)
            kve = sb("kve", [P, 8, 2, DM], F32, ctx)
            prod = sb("prod", [P, 2, DM], F32, ctx)
            alpha = sb("alpha", [P, 8, HEADS], F32, ctx)
            mx = sb("mx", [P, 4, HEADS], F32, ctx)
            mnew = sb("mnew", [P, 4, HEADS], F32, ctx)
            md = sb("md", [P, 4, HEADS], F32, ctx)
            r = sb("r", [P, 8, HEADS], F32, ctx)
            ad = sb("ad", [P, 4, HEADS], F32, ctx)
            msg = sb("msg", [P, 4, HEADS, HU], F32, ctx)
            WM = HEADS * HU

            def sums_at(t):
                return ps[:, 6 + t.of(2), 0:WM]

            with nc.Block() as block:

                @block.sync
                def _(sp):
                    for g in range(GROUPS):
                        sp.dma_start(e_in[:, g, :, :].rearrange("p s c -> p (s c)"), e_store[g * P:(g + 1) * P, :]).then_inc(e_got[g], 16)
                    with sp.Fori(1, SLOTS // RING) as i:
                        for g in range(GROUPS):
                            sp.wait_ge(kve_ready, (i - 1) * RING + (g + 1) * GRP)
                            sp.dma_start(e_in[:, g, :, :].rearrange("p s c -> p (s c)"),
                                         e_store[bass.ds(i * (P * GROUPS) + g * P, P), :]).then_inc(e_got[g], 16)

                @block.gpsimd
                def _(pool):
                    groups = turn // TURNS * (TURNS + 1) * GROUPS

                    def gather(t):
                        if t.k % GRP == 0:
                            at = t.i * GROUPS if t.i is not None else 0
                            pool.wait_ge(staged, at + (groups + t.k // GRP + 1))
                            pool.sem_inc(gather_tick, 1)
                        j = t.of(RING)
                        pool.indirect_dma_start(ring[:, j, 0:2 * DM], None, kv_table,
                                                bass.IndirectOffsetOnAxis(ap=cur[:, j:j + 1], axis=0)).then_inc(got[j], 16)

                    def add_edge_part(t):
                        pool.wait_ge(got[t.of(RING)], (t.turn + turn) * 16 + 16)
                        pool.wait_ge(e_got[t.of(RING) // GRP], t.turn * 16 + 16)
                        pool.wait_ge(msg_ready, t.plus(1).n)
                        e = e_in[:, t.of(RING) // GRP, t.of(GRP):t.of(GRP) + 1, :].to_broadcast([P, 2, DM])
                        pool.tensor_tensor(kve[:, t.of(8), :, :], ring[:, t.of(RING), 0:2 * DM].rearrange("p (a c) -> p a c", a=2),
                                           e, ALU.add).then_inc(kve_ready, 1)

                    def rescale(t):
                        pool.wait_ge(r_ready, t.plus(1).n)
                        pool.wait_ge(added, base + t.plus(BANKS).n)
                        pool.wait_ge(collected, base + t.plus(1).n)
                        pool.tensor_tensor(now[:, t.of(4), 0:WM].rearrange("p (h c) -> p h c", h=HEADS),
                                        now[:, (t.k - 1) % 4, 0:WM].rearrange("p (h c) -> p h c", h=HEADS),
                                        r[:, t.of(8), :].unsqueeze(2).to_broadcast([P, HEADS, HU]), ALU.mult).then_inc(scaled, 1)

                    pipeline(pool, SLOTS, RING, [(3, add_edge_part), (11, gather), (-6, rescale)])

                @block.tensor
                def _(pe):
                    pe.wait_ge(cleared, 2)

                    def sum_messages(t):
                        pe.wait_ge(msg_ready, t.plus(1 + 8).n)
                        pe.wait_ge(added, base + t.plus(BANKS - 1).n)
                        pe.matmul(sums_at(t), onehot[:, t.of(RING), :], msg[:, t.of(4), :, :].rearrange("p h c -> p (h c)"),
                                  start=True, stop=True).then_inc(summed, 1)

                    def spread_maxima(t):
                        pe.wait_ge(mnew_ready, t.plus(2).n)
                        pe.wait_ge(ad_ready, t.plus(1).n)
                        pe.matmul(ps[:, 1, 0:HEADS], onehot_t[:, t.of(8), :], mnew[:, t.of(4), :], start=True, stop=True).then_inc(me_ready, 1)

                    def spread_scores(t):
                        pe.wait_ge(pen_ready, t.plus(2).n)
                        pe.wait_ge(mx_ready, t.plus(1).n)
                        bank = ps[:, 4 + t.of(2), :]
                        pe.matmul(bank, identb[:, :], penalty[:, t.of(8):t.of(8) + 1, :].to_broadcast([P, HEADS, P]),
                                  start=True, stop=False)
                        pe.wait_ge(alpha_ready, t.plus(1).n)
                        for head in range(HEADS):
                            ins = pe.matmul(bank[:, head * P:(head + 1) * P],
                                            alpha[:, t.of(8), head:head + 1].to_broadcast([P, P]), ident[:, :],
                                            start=False, stop=head == HEADS - 1)
                        ins.then_inc(scored, 1)

                    def spread_queries(t):
                        block_of = slot_block(pe, t)
                        pe.wait_ge(ot_ready, t.plus(1).n)
                        pe.wait_ge(prod_ready, t.plus(1).n)
                        pe.matmul(ps[:, 2 + t.of(2), 0:DM], onehot_t[:, t.of(8), :],
                                  s[:, block_of, 0:DM].rearrange("p o c -> p (o c)"), start=True, stop=True).then_inc(qx_ready, 1)

                    def turn_onehot(t):
                        pe.wait_ge(hot, base + t.plus(1).n)
                        pe.wait_ge(pen_ready, t.plus(1).n)
                        pe.transpose(ps[:, 0, 0:P], onehot[:, t.of(RING), :], ident[:, :]).then_inc(turned, 1)

                    pipeline(pe, SLOTS, RING, [(-6, sum_messages), (1, spread_scores),
                                               (3, spread_queries), (5, turn_onehot), (-2, spread_maxima)])

                @block.scalar
                def _(act):
                    act.sem_inc(pen_ready, 1)

                    def old_factor(t):
                        act.wait_ge(md_ready, t.plus(1).n)
                        act.activation(r[:, t.of(8), :], md[:, t.of(4), :], ACT.Exp, scale=SM_SCALE).then_inc(r_ready, 1)

                    def weights(t):
                        act.wait_ge(ad_ready, t.plus(2).n)
                        act.activation(msg[:, t.of(4), :, HC], ad[:, t.of(4), :], ACT.Exp, scale=SM_SCALE).then_inc(p_ready, 1)

                    def copy_turned(t):
                        act.wait_ge(turned, t.plus(1).n)
                        act.copy(onehot_t[:, t.of(8), :], ps[:, 0, 0:P]).then_inc(ot_ready, 1)
                        act.activation(penalty[:, t.of(8), :], ps[:, 0, 0:P], ACT.Copy, scale=-NEG, bias=NEG).then_inc(pen_ready, 1)

                    stager = index_stager(act, 1, kve_ready, 0)
                    act.wait_ge(cleared, 2)
                    pipeline(act, SLOTS, RING, [(4, copy_turned), (1, stager), (-8, slot_collector(act, base, acc, WM)),
                                                (-4, weights), (-1, old_factor)])

                @block.vector
                def _(v):
                    clear_sums(v, base, acc, WM, cleared)
                    v.memset(mnew[:, 3, :], NEG).then_inc(mnew_ready, 1)
                    v.sem_inc(prod_ready, 2)
                    v.sem_inc(mx_ready, 2)
                    v.sem_inc(ad_ready, 1)
                    v.sem_inc(msg_ready, 8)

                    def multiply(t):
                        v.wait_ge(qx_ready, t.plus(1).n)
                        v.wait_ge(kve_ready, t.plus(1).n)
                        v.tensor_tensor(prod[:, t.of(2), :], kve[:, t.of(8), 0, :], ps[:, 2 + t.of(2), 0:DM], ALU.mult).then_inc(prod_ready, 1)

                    def weigh(t):
                        v.wait_ge(p_ready, t.plus(1).n)
                        m = msg[:, t.of(4), :, :]
                        v.tensor_tensor(m[:, :, 0:HC], kve[:, t.of(8), 1, :].rearrange("p (h c) -> p h c", h=HEADS),
                                        m[:, :, HC:HU].to_broadcast([P, HEADS, HC]), ALU.mult).then_inc(msg_ready, 1)

                    def score(t):
                        v.wait_ge(prod_ready, t.plus(3).n)
                        v.tensor_reduce(alpha[:, t.of(8), :], prod[:, t.of(2), :].rearrange("p (h c) -> p h c", h=HEADS),
                                        AX.X, ALU.add).then_inc(alpha_ready, 1)

                    def add(t):
                        new = now[:, t.of(4), 0:WM]
                        v.wait_ge(summed, base + t.plus(1).n)
                        v.wait_ge(scaled, t.plus(1).n)
                        v.tensor_tensor(new, new, sums_at(t), ALU.add).then_inc(added, 1)

                    def slot_max(t):
                        v.wait_ge(scored, t.plus(1).n)
                        v.tensor_reduce(mx[:, t.of(4), :], ps[:, 4 + t.of(2), :].rearrange("p (h e) -> p h e", h=HEADS),
                                        AX.X, ALU.max).then_inc(mx_ready, 1)

                    def subtract(t):
                        v.wait_ge(me_ready, t.plus(1).n)
                        v.tensor_tensor(ad[:, t.of(4), :], alpha[:, t.of(8), :], ps[:, 1, 0:HEADS], ALU.subtract).then_inc(ad_ready, 1)

                    def new_max(t):
                        v.wait_ge(mx_ready, t.plus(3).n)
                        v.wait_ge(mnew_ready, t.plus(1).n)
                        v.scalar_tensor_tensor(mnew[:, t.of(4), :], mnew[:, (t.k - 1) % 4, :], forget[:, dyn(t)],
                                               mx[:, t.of(4), :], ALU.add, ALU.max).then_inc(mnew_ready, 1)

                    def max_step(t):
                        v.wait_ge(mnew_ready, t.plus(2).n)
                        v.scalar_tensor_tensor(md[:, t.of(4), :], mnew[:, (t.k - 1) % 4, :], forget[:, dyn(t)],
                                               mnew[:, t.of(4), :], ALU.add, ALU.subtract).then_inc(md_ready, 1)

                    pipeline(v, SLOTS, RING, [(-3, subtract), (2, multiply),
                                              (-5, weigh), (2, score), (0, slot_max), (6, onehot_maker(v, base)), (0, new_max), (-7, add), (0, max_step)])

    def project(name, inputs, source, width, outs, weights=None, store=None, meanwhile=None, measure=False):
        kt = sum(w for _, w in inputs) // P
        tiles, stores = calls["tile"], calls["store"]
        chunk_base = [calls[k] for k in range(len(outs))]
        calls["tile"] += NB
        for k in range(len(outs)):
            calls[k] += NB
        if store:
            calls["store"] += NB // 2
        assert outs[-1][1] == "dve"
        copies = 2 if len(outs) <= 3 else 1

        def bank(k, t):
            return 2 + t.of(copies) * len(outs) + k

        def chunk_done(k, t):
            return chunk_base[k] + t.plus(1).n

        with ExitStack() as ctx:
            w = weights if weights is not None else sb(f"{name}_w", [P, kt, width], F32, ctx)
            tin = sb(f"{name}_tin", [P, 2, kt * P], F32, ctx)
            tt = sb(f"{name}_tt", [P, 2, kt * P], F32, ctx)
            with nc.Block() as block:

                @block.sync
                def _(sp):
                    if source is not None:
                        load_weights(sp, w, source)
                    if store is not None:
                        if stores == 0:
                            for j in range(2):
                                sp.sem_inc(stage_free[j], 16)
                        with sp.Fori(0, NB // 2) as i:
                            for j in range(2):
                                t = At(i, 2, j)
                                for k, (_, _, _, staged_out) in enumerate(outs):
                                    if staged_out:
                                        sp.wait_ge(taken[k], chunk_base[k] + t.plus(2).n)
                                sp.dma_start(store[bass.ds(i * (2 * P) + j * P, P), :], stage[:, j, 0:store.shape[1]]).then_inc(stage_free[j], 16)
                        for j in range(2):
                            sp.wait_ge(stage_free[j], 16 * (stores + NB // 2 + 1))

                if meanwhile is not None:
                    @block.gpsimd
                    def _(pool):
                        meanwhile(pool)

                def evacuate(eng, mine):
                    def body(t):
                        for k, (cols, engine, write, staged_out) in enumerate(outs):
                            if engine == mine:
                                eng.wait_ge(multiplied[k], chunk_done(k, t))
                                if staged_out:
                                    eng.wait_ge(stage_free[t.of(2)], (t.turn + stores) * 16 + 16)
                                write(eng, t, ps[:, bank(k, t), 0:cols]).then_inc(taken[k], 1)
                    return body

                @block.scalar
                def _(act):
                    if tiles == 0:
                        act.sem_inc(turned_in, 2)

                    def take_in(t):
                        act.wait_ge(turned_in, tiles + t.plus(1).n)
                        c = 0
                        for take, wide in inputs:
                            ins = take(act, dyn(t), tin[:, t.of(2), c:c + wide])
                            c += wide
                        ins.then_inc(tin_ready, 1)

                    pipeline(act, NB, 2, [(1, take_in), (0, evacuate(act, "act"))])

                @block.tensor
                def _(pe):
                    if calls["weights"]:
                        pe.wait_ge(weights_loaded, calls["weights"])

                    def turn_in(t):
                        pe.wait_ge(tin_ready, tiles + t.plus(1).n)
                        pe.wait_ge(tin_turned, tiles + t.plus(1).n)
                        for k in range(kt):
                            ins = pe.transpose(ps[:, t.of(2), k * P:(k + 1) * P], tin[:, t.of(2), k * P:(k + 1) * P], ident[:, :])
                        ins.then_inc(turned_in, 1)

                    def multiply(t):
                        pe.wait_ge(tin_turned, tiles + t.plus(3).n)
                        c = 0
                        for n, (cols, _, _, _) in enumerate(outs):
                            pe.wait_ge(taken[n], chunk_base[n] + t.plus(2 - copies).n)
                            for k in range(kt):
                                ins = pe.matmul(ps[:, bank(n, t), 0:cols], tt[:, t.of(2), k * P:(k + 1) * P], w[:, k, c:c + cols],
                                                start=k == 0, stop=k == kt - 1)
                            ins.then_inc(multiplied[n], 1)
                            c += cols

                    pipeline(pe, NB, 2, [(1, turn_in), (0, multiply)])

                @block.vector
                def _(v):
                    if tiles == 0:
                        v.sem_inc(tin_turned, 2)
                    for k in range(len(outs)):
                        if chunk_base[k] == 0:
                            v.sem_inc(taken[k], 1)

                    def copy_turned(t):
                        v.wait_ge(turned_in, tiles + t.plus(3).n)
                        v.tensor_copy(tt[:, t.of(2), :], ps[:, t.of(2), 0:kt * P]).then_inc(tin_turned, 1)

                    def measure_tile(t):
                        v.wait_ge(taken[0], chunk_base[0] + t.plus(2).n)
                        v.bn_stats(flat(stats, dyn(t), 6), flat(x, dyn(t))).then_inc(x_measured, 1)

                    pipeline(v, NB, 2, [(1, copy_turned), (0, evacuate(v, "dve"))] + ([(-1, measure_tile)] if measure else []))
                    measured_tiles[0] += NB if measure else 0

    def flat(array, b, n=D):
        return array[:, b, 0:n].rearrange("p o c -> p (o c)")

    def plain(array):
        return lambda act, b, dest: act.copy(dest, flat(array, b, dest.shape[-1]))

    def rectified(array):
        return lambda act, b, dest: act.activation(dest, flat(array, b), ACT.Relu)

    def averaged(act, b, dest):
        return act.activation(dest, flat(acc, b), ACT.Copy, scale=small[:, 1, b])

    def copy_to_stage(c0):
        def write(eng, t, psum):
            dest = stage[:, t.of(2), c0:c0 + psum.shape[1]]
            return eng.copy(dest, psum) if eng is nc.scalar else eng.tensor_copy(dest, psum)
        return write

    def add_to(dest, other, c0=0):
        def write(eng, t, psum):
            n = psum.shape[1]
            d = dest[:, dyn(t), c0:c0 + n].rearrange("p o c -> p (o c)")
            return eng.tensor_tensor(d, psum, d if other is None else other[:, 0:n], ALU.add)
        return write

    def add_to_stage(other):
        def write(eng, t, psum):
            return eng.tensor_tensor(stage[:, t.of(2), 0:psum.shape[1]], psum, other[:, 0:psum.shape[1]], ALU.add)
        return write

    def on_all(fn):
        with nc.Block() as block:

            @block.vector
            def _(v):
                fn(chain, v)

    stage = ring[:, :, :].rearrange("p r c -> p (r c)").rearrange("p (j n) -> p j n", j=2)

    rows_written, row_stores = sem("rows_written"), [0]

    def store_rows(table, array):
        row_stores[0] += 1
        with nc.Block() as block:

            @block.sync
            def _(sp):
                sp.dma_start(rows(table), array[:, :, 0:D]).then_inc(rows_written, 16)
                sp.wait_ge(rows_written, 16 * row_stores[0])

    def relational(layer, take, table, self_out=(), meanwhile=None):
        outs = [(2 * D, "dve" if k % 2 else "act", copy_to_stage(2 * k * D), True) for k in range(REL // 2)]
        project(f"rel{layer}", [(take, D)], None, (REL + 1) * D, outs + list(self_out), weights=w_rel,
                store=table.rearrange("(n r) f -> n (r f)", r=REL), meanwhile=meanwhile)

    def into(dest, other):
        return lambda v, b, psum: v.tensor_tensor(flat(dest, b), psum, flat(dest, b) if other is None else other, ALU.add)

    pool_added, pool_adds = sem("pool_added"), [0]

    def add_bias_to_x(name):
        def work(pool):
            pool_adds[0] += 1
            pool.tensor_tensor(x[:, :, :], x[:, :, :], bias[name].unsqueeze(1).to_broadcast([P, NB, D]), ALU.add).then_inc(pool_added, 1)
            pool.wait_ge(pool_added, pool_adds[0])
        return work

    bias = {n: biases[:, k, :] for k, n in enumerate(BIASES)}

    relational_block = ExitStack()
    w_rel = sb("w_rel", [P, 2, (REL + 1) * D], F32, relational_block)
    with ExitStack() as edges_in:
        rec_p = sb("rec_p", [P, COLS, 4], I32, edges_in)
        inspect()
        sort_edges()
    make_slots()
    layernorm("norm0", write=False)
    relational(0, lambda act, b, dest: normalised(act, dest, b), table0,
               self_out=[(D, "dve", add_to(s, bias["l0_b1"]), False)])
    gather_sum_and_project_edges(table0, 0)

    def hidden0(c, v):
        c.link(v.tensor_copy(degree[:, :], sums[:, :, D]))
        c.link(v.tensor_tensor(h[:, :, :], acc[:, :, 0:D], s[:, :, :], ALU.add))
    on_all(hidden0)
    relational(1, rectified(h), table1, meanwhile=add_bias_to_x("l0_b2"))
    relational_block.close()
    att = ExitStack()
    w_n2m = sb("w_n2m", [P, 1, D], F32, att)
    w_cat = sb("w_cat", [P, 1, 4 * DM], F32, att)
    gather_sum(table1, 0, [(0, a["l0_w2"][:, REL * D:], lambda v, b, tin: v.tensor_scalar(tin[:, :], flat(h, b), 0.0, None, ALU.max),
                            into(x, None))],
               with_edges=True, loads=[(w_n2m, a["w_n2m"]), (w_cat, a["w_qskv_t"])])

    def residual0(c, v):
        c.link(v.tensor_tensor(x[:, :, :], x[:, :, :], acc[:, :, 0:D], ALU.add))
    on_all(residual0)

    layernorm("norm1", write=False)
    with att:
        w_att = sb("w_att", [P, 2, 4 * DM], F32, att)
        product = sem("att_w_product")
        with nc.Block() as block:

            @block.tensor
            def _(pe):
                pe.wait_ge(weights_loaded, calls["weights"])
                for k in range(2):
                    pe.matmul(ps[:, k, :], w_n2m[:, 0, k * P:(k + 1) * P], w_cat[:, 0, :], start=True, stop=True).then_inc(product, 1)

            @block.scalar
            def _(act):
                for k in range(2):
                    act.wait_ge(product, k + 1)
                    act.copy(w_att[:, k, :], ps[:, k, :])
        project("att_in", [(lambda act, b, dest: normalised(act, dest, b), D)], None, 4 * DM,
                [(D, "dve", add_to(s, bias["l1_qs"]), False), (D, "dve", add_to_stage(bias["l1_kv"]), True)],
                weights=w_att, store=kv_table)
    attention()

    with ExitStack() as fin:
        wbeta = sb("wbeta", [P, 3 * DM], F32, fin)
        col = sb("col", [P, 4, NB], F32, fin)
        inv = sb("inv", [P, NB, HEADS], F32, fin)
        loaded, logit, sig = sem("beta_loaded"), sem("beta_logit"), sem("beta_sigmoid")
        with nc.Block() as block:

            @block.sync
            def _(sp):
                sp.dma_start(wbeta[:, :], a["wbeta"].to_broadcast([P, 3 * DM])).then_inc(loaded, 16)

            @block.scalar
            def _(act):
                act.wait_ge(logit, 1)
                act.activation(col[:, 3, :], col[:, 2, :], ACT.Sigmoid).then_inc(sig, 1)

            @block.vector
            def _(v):
                c = chain
                o, diff, xr = h[:, :, 0:DM], h[:, :, DM:D], s[:, :, DM:D]

                def over_nodes(row):
                    return row.unsqueeze(1).to_broadcast([P, NB, DM])
                heads = acc[:, :, 0:HEADS * HU].rearrange("p b (h c) -> p b h c", h=HEADS)
                c.link(v.tensor_scalar(inv[:, :, :], heads[:, :, :, HC], 1e-16, None, ALU.add))
                c.link(v.reciprocal(inv[:, :, :], inv[:, :, :]))
                for head in range(HEADS):
                    c.step(v.tensor_tensor(h[:, :, head * HC:(head + 1) * HC], heads[:, :, head, 0:HC],
                                           inv[:, :, head:head + 1].to_broadcast([P, NB, HC]), ALU.mult))
                c.after()
                c.link(v.tensor_tensor(diff, o, xr, ALU.subtract))
                v.wait_ge(loaded, 16)
                c.step(v.tensor_tensor(acc[:, :, 0:DM], o, over_nodes(wbeta[:, 0:DM]), ALU.mult))
                c.link(v.tensor_tensor(acc[:, :, DM:D], xr, over_nodes(wbeta[:, DM:2 * DM]), ALU.mult))
                c.link(v.tensor_reduce(col[:, 0, :], acc[:, :, 0:D], AX.X, ALU.add))
                c.link(v.tensor_tensor(acc[:, :, 0:DM], diff, over_nodes(wbeta[:, 2 * DM:3 * DM]), ALU.mult))
                c.link(v.tensor_reduce(col[:, 1, :], acc[:, :, 0:DM], AX.X, ALU.add))
                v.tensor_tensor(col[:, 2, :], col[:, 0, :], col[:, 1, :], ALU.add).then_inc(logit, 1)
                v.wait_ge(sig, 1)
                c.link(v.tensor_tensor(diff, diff, col[:, 3, :].unsqueeze(2).to_broadcast([P, NB, DM]), ALU.mult))
                c.link(v.tensor_tensor(o, o, diff, ALU.subtract))
    project("att_out", [(plain(h), DM)], a["w_m2n_t"], D, [(D, "dve", add_to(x, None), False)], measure=True)

    layernorm("norm2", measured=True)
    store_rows(h_table, h)

    def from_nodes(array):
        return lambda v, b, tin: v.tensor_copy(tin[:, :], flat(array, b))

    def take_leaky(v, b, tin):
        return v.scalar_tensor_tensor(tin[:, :], flat(esum, b), SLOPE, flat(esum, b), ALU.mult, ALU.max)

    w_sage = sb("w_sage", [P, 2, D])
    gather_sum(h_table, 1, [(0, a["l2_w1"][D:2 * D, :], from_nodes(h), into(s, bias["l2_b1"])),
                            (7, a["l3_w1_t"], from_nodes(esum), into(esum, bias["l3_b1"]))],
               loads=[(w_sage, a["l2_w1"][0:D, :])])

    def inverse_counts(c, v):
        c.link(v.tensor_scalar(small[:, 0, :], degree[:, :], 1.0, None, ALU.max))
        c.link(v.reciprocal(small[:, 1, :], small[:, 0, :]))
    on_all(inverse_counts)
    project("sage0", [(averaged, D)], None, D, [(D, "dve", add_to(s, None), False)], weights=w_sage,
            meanwhile=add_bias_to_x("l2_b2"))

    def relu_s(c, v):
        c.link(v.tensor_scalar(s[:, :, :], s[:, :, :], 0.0, None, ALU.max))
    on_all(relu_s)
    store_rows(h1_table, s)
    gather_sum(h1_table, 1, [(0, a["l2_w2"][D:2 * D, :], from_nodes(s), into(x, None)),
                             (7, a["l3_w2_t"], take_leaky, into(esum, bias["l3_b2"]))],
               loads=[(w_sage, a["l2_w2"][0:D, :])])

    project("sage1", [(averaged, D)], None, D, [(D, "dve", add_to(x, None), False)], weights=w_sage, measure=True)

    finished, written = sem("finished"), sem("written")
    before = norm_tiles[0]

    def finish(v):
        chain.link(v.tensor_tensor(s[:, :, :], x[:, :, :], esum[:, :, :], ALU.add))
        for b in range(NB):
            v.wait_ge(normed, before + b + 1)
            v.tensor_tensor(x[:, b, :], s[:, b, :], h[:, b, :], ALU.add).then_inc(finished, 1)

    def write_out(sp):
        half = NB // 2
        for b0, b1 in ((0, half), (half, NB - 1)):
            sp.wait_ge(finished, b1)
            sp.dma_start(out[b0 * P:b1 * P, :].rearrange("(b p) f -> p b f", p=P), x[:, b0:b1, :]).then_inc(written, 16)
        sp.wait_ge(finished, NB)
        sp.dma_start(out[(NB - 1) * P:N, :], x[0:LAST, NB - 1, :]).then_inc(written, 16)
        sp.wait_ge(written, 48)

    layernorm("norm3", measured=True, meanwhile=finish, outputs=write_out)
    top.close()



def kernel(**inputs):
    import numpy as np
    from concourse import bacc
    from concourse.bass_utils import run_bass_kernel_spmd

    nc = bacc.Bacc("TRN2", target_bir_lowering=False, num_devices=1)
    arrays, args = {}, {}
    of = {k: np.asarray(v) for k, v in inputs.items()}

    def give(name, value):
        value = np.ascontiguousarray(value)
        arrays[f"in_{name}"] = value
        args[name] = nc.dram_tensor(f"in_{name}", value.shape, mybir.dt.from_np(value.dtype), kind="ExternalInput").ap()

    give("x", of["x"])
    records = np.stack([of["dst"], of["src"], of["edge_type_8"], np.zeros_like(of["dst"])], axis=1)
    padding = np.zeros((EP + 1 - E, 4), records.dtype)
    padding[:, 0] = NPAD
    give("records", np.concatenate([records, padding]))
    features = np.concatenate([of["edge_attr_64"], of["edge_attr_256"]], axis=1)
    give("edge_attrs", np.concatenate([features, np.zeros((EP - E, DR + D), features.dtype)]))
    for layer in "12":
        w = of[f"L0_gnn_W{layer}"].transpose(1, 0, 2).reshape(D, REL * D)
        give(f"l0_w{layer}", np.concatenate([w, of[f"L0_gnn_self_w{layer}"]], axis=1))
        give(f"l2_w{layer}", np.concatenate([of[f"L2_gnn_W_l{layer}"], of[f"L2_gnn_W_r{layer}"]], axis=0))
        give(f"l3_w{layer}_t", of[f"L3_gnn_W{layer}"].T)
    give("w_edge", of["L1_gnn_W_edge"])
    give("we_t", of["L1_gnn_We"].T)
    give("w_n2m", of["L1_gnn_W_n2m"])
    give("w_qskv_t", np.concatenate([of[f"L1_gnn_W{n}"].T for n in ("q", "skip", "k", "v")], axis=1))
    give("wbeta", of["L1_gnn_Wbeta"])
    give("w_m2n_t", of["L1_gnn_W_m2n"].T)
    rows = [of["L0_gnn_b1"], of["L0_gnn_b2"], np.concatenate([of["L1_gnn_bq"], of["L1_gnn_bskip"]]),
            np.concatenate([of["L1_gnn_bk"], of["L1_gnn_bv"]]), of["L2_gnn_b1"], of["L2_gnn_b2"], of["L3_gnn_b1"], of["L3_gnn_b2"]]
    give("biases", np.stack(rows).reshape(1, len(BIASES) * D))
    out = nc.dram_tensor("out", (N, D), F32, kind="ExternalOutput").ap()
    build(nc, args, out)
    r = run_bass_kernel_spmd(nc, [arrays], core_ids=[0])
    return r.results[0]["out"]
```
